# Optimizing a Trainium2 kernel written in Bass

```python
import numpy as np
import jax
import jax.numpy as jnp

def _softmax(x, axis=-1):
    return jax.nn.softmax(x, axis=axis)

def _gelu(x):
    return jax.nn.gelu(x, approximate=True)

def _silu(x):
    return jax.nn.silu(x)

def _sigmoid(x):
    return jax.nn.sigmoid(x)

def _layernorm(x, axis=-1, eps=1e-05):
    m = jnp.mean(x, axis=axis, keepdims=True)
    v = jnp.var(x, axis=axis, keepdims=True)
    return (x - m) / jnp.sqrt(v + eps)

def _scatter_add(tgt, idx, src, axis=0):
    return tgt.at[idx].add(src)

def _segment_sum(src, seg, n):
    return jax.ops.segment_sum(src, seg, n)
kernel_name = 'mk_adj_resnorm_d4_adj_r2_fe804f'

def setup_inputs(seed: int=0):
    np.random.seed(seed)
    _w = jnp.asarray

    def _rec_inputs():
        import jax
        import jax.numpy as jnp
        _gk = jax.random.key(seed)
        x = -0.0005207 + 1.001 * jax.random.normal(jax.random.fold_in(_gk, 1), (4096, 128), jnp.float32)
        _w = (1.0 + jnp.arange(4096, dtype=jnp.float32)) ** (-0.5)
        _w = _w / _w.mean()
        _pij = jnp.clip(0.00390625 * _w[:, None] * _w[None, :], 0.0, 1.0)
        _a = jax.random.uniform(jax.random.fold_in(_gk, 2), (4096, 4096)) < _pij
        _a = jnp.logical_or(_a, jnp.eye(4096, dtype=bool))
        _af = _a.astype(jnp.float32)
        _af = _af * jax.random.uniform(jax.random.fold_in(_gk, 3), (4096, 4096), jnp.float32, 0.05, 1)
        adj = _af
        return (x, adj)
    x, adj = _rec_inputs()

    def _L0_gnn_setup():
        import jax, jax.numpy as jnp
        import numpy as np
        N = 4096
        D_IN = 128
        D_OUT = 128
        key = jax.random.key(seed)
        k1, k2, k3, k4 = jax.random.split(key, 4)
        x = jax.random.normal(k1, (N, D_IN), dtype=jnp.float32)
        adj = jax.random.uniform(k2, (N, N), dtype=jnp.float32)
        W = jax.random.normal(k3, (D_OUT, D_IN), dtype=jnp.float32) * (1.0 / np.sqrt(D_IN))
        b = jax.random.normal(k4, (D_OUT,), dtype=jnp.float32) * 0.01
        return {'x': x, 'adj': adj, 'W': W, 'b': b}
    _L0_gnn_all = _L0_gnn_setup()
    _L0_gnn_in = {k: v for k, v in _L0_gnn_all.items() if k in ('W', 'b')}
    del _L0_gnn_all

    def _L1_gnn_setup():
        import jax, jax.numpy as jnp
        import numpy as np
        N, H, HEADS = (2048, 128, 3)
        ALPHA = 0.2
        NEG_INF = -9000000000000000.0

        def _sign_adj(key, n, density):
            k1, k2 = jax.random.split(key)
            mask = jax.random.uniform(k1, (n, n)) < density
            sign = jnp.where(jax.random.uniform(k2, (n, n)) < 0.5, -1.0, 1.0)
            adj = jnp.where(mask, sign, 0.0).astype(jnp.float32)
            idx = jnp.arange(n)
            return adj.at[idx, idx].set(1.0)

        def _gru_cell(x, hstate, Wih, Whh, bih, bhh):
            gi = x @ Wih.T + bih
            gh = hstate @ Whh.T + bhh
            ir, iz, inn = jnp.split(gi, 3, axis=1)
            hr, hz, hn = jnp.split(gh, 3, axis=1)
            r = jax.nn.sigmoid(ir + hr)
            z = jax.nn.sigmoid(iz + hz)
            n = jnp.tanh(inn + r * hn)
            return (1.0 - z) * n + z * hstate

        def _gat_head(h, node_adj, edge_adj, W, a):
            hW = h @ W
            hp = (node_adj > 0).astype(hW.dtype) @ hW
            hm = (node_adj < 0).astype(hW.dtype) @ hW
            e_plus = jax.nn.leaky_relu(jnp.concatenate([hp, hm], axis=1) @ a, ALPHA)[:, 0]
            e_minus = jax.nn.leaky_relu(jnp.concatenate([hm, hp], axis=1) @ a, ALPHA)[:, 0]
            att = jnp.where(edge_adj > 0, e_plus[None, :], NEG_INF)
            att = jnp.where(edge_adj < 0, e_minus[None, :], att)
            att = jax.nn.softmax(att, axis=1)
            return att * edge_adj @ hW
        key = jax.random.key(seed)
        ks = jax.random.split(key, 16)
        std = 0.01
        gain = 1.414
        return {'h': jax.random.normal(ks[0], (N, H), jnp.float32), 'node_adj': _sign_adj(ks[1], N, 0.005), 'edge_adj': _sign_adj(ks[2], N, 0.005), 'gat_W': jax.random.normal(ks[3], (HEADS, H, H), jnp.float32) * (gain / np.sqrt(H, dtype=np.float32)), 'gat_a': jax.random.normal(ks[4], (HEADS, 2 * H, 1), jnp.float32) * 0.1, 'edge_Wih': jax.random.normal(ks[5], (3 * H, H), jnp.float32) * std, 'edge_Whh': jax.random.normal(ks[6], (3 * H, H), jnp.float32) * std, 'edge_bih': jnp.zeros((3 * H,), jnp.float32), 'edge_bhh': jnp.zeros((3 * H,), jnp.float32), 'node_Wih': jax.random.normal(ks[7], (3 * H, H), jnp.float32) * std, 'node_Whh': jax.random.normal(ks[8], (3 * H, H), jnp.float32) * std, 'node_bih': jnp.zeros((3 * H,), jnp.float32), 'node_bhh': jnp.zeros((3 * H,), jnp.float32)}
    _L1_gnn_all = _L1_gnn_setup()
    _L1_gnn_in = {k: v for k, v in _L1_gnn_all.items() if k in ('gat_W', 'gat_a', 'edge_Wih', 'edge_Whh', 'edge_bih', 'edge_bhh', 'node_Wih', 'node_Whh', 'node_bih', 'node_bhh')}
    del _L1_gnn_all

    def _L2_gnn_setup():
        import jax, jax.numpy as jnp
        import numpy as np
        N = 4096
        D_IN = 128
        D_OUT = 128
        key = jax.random.key(seed)
        k_x, k_a, k_w, k_bias = jax.random.split(key, 4)
        x = jax.random.normal(k_x, (N, D_IN), dtype=jnp.float32)
        A_shape = jax.random.randint(k_a, (N, N), 0, 2).astype(jnp.float32)
        A_shape = A_shape.at[jnp.arange(N), jnp.arange(N)].set(1.0)
        lim = 1.0 / np.sqrt(D_IN)
        W = jax.random.uniform(k_w, (D_OUT, D_IN), jnp.float32, -lim, lim)
        bias = jax.random.uniform(k_bias, (D_OUT,), jnp.float32, -lim, lim)
        b = jnp.ones((1,), dtype=jnp.float32)
        return {'x': x, 'A_shape': A_shape, 'W': W, 'bias': bias, 'b': b}
    _L2_gnn_all = _L2_gnn_setup()
    _L2_gnn_in = {k: v for k, v in _L2_gnn_all.items() if k in ('W', 'bias', 'b')}
    del _L2_gnn_all

    def _L3_gnn_setup():
        import jax, jax.numpy as jnp
        import numpy as np
        N = 4096
        C = 128
        key = jax.random.key(seed)
        k1, k2, k3 = jax.random.split(key, 3)
        x = jax.random.normal(k1, (N, C), dtype=jnp.float32)
        evals = jax.random.uniform(k2, (N,), dtype=jnp.float32)
        evecs = jax.random.normal(k3, (N, N), dtype=jnp.float32)
        t = jnp.ones((1,), dtype=jnp.float32)
        return {'x': x, 'evals': evals, 'evecs': evecs, 't': t}
    _L3_gnn_all = _L3_gnn_setup()
    _L3_gnn_in = {k: v for k, v in _L3_gnn_all.items() if k in ('evals', 't')}
    del _L3_gnn_all
    return {'x': x, 'adj': adj, 'L0_gnn_W': _L0_gnn_in['W'], 'L0_gnn_b': _L0_gnn_in['b'], 'L1_gnn_gat_W': _L1_gnn_in['gat_W'], 'L1_gnn_gat_a': _L1_gnn_in['gat_a'], 'L1_gnn_edge_Wih': _L1_gnn_in['edge_Wih'], 'L1_gnn_edge_Whh': _L1_gnn_in['edge_Whh'], 'L1_gnn_edge_bih': _L1_gnn_in['edge_bih'], 'L1_gnn_edge_bhh': _L1_gnn_in['edge_bhh'], 'L1_gnn_node_Wih': _L1_gnn_in['node_Wih'], 'L1_gnn_node_Whh': _L1_gnn_in['node_Whh'], 'L1_gnn_node_bih': _L1_gnn_in['node_bih'], 'L1_gnn_node_bhh': _L1_gnn_in['node_bhh'], 'L2_gnn_W': _L2_gnn_in['W'], 'L2_gnn_bias': _L2_gnn_in['bias'], 'L2_gnn_b': _L2_gnn_in['b'], 'L3_gnn_evals': _L3_gnn_in['evals'], 'L3_gnn_t': _L3_gnn_in['t']}

def reference(x, adj, L0_gnn_W, L0_gnn_b, L1_gnn_gat_W, L1_gnn_gat_a, L1_gnn_edge_Wih, L1_gnn_edge_Whh, L1_gnn_edge_bih, L1_gnn_edge_bhh, L1_gnn_node_Wih, L1_gnn_node_Whh, L1_gnn_node_bih, L1_gnn_node_bhh, L2_gnn_W, L2_gnn_bias, L2_gnn_b, L3_gnn_evals, L3_gnn_t):
    import jax
    import jax.numpy as jnp

    def _L0_gnn_ref(x, adj, W, b):
        import jax, jax.numpy as jnp
        import numpy as np
        N = 4096
        D_IN = 128
        D_OUT = 128
        h = x @ W.T + b
        A = adj + jnp.eye(adj.shape[0], dtype=adj.dtype)
        rowsum = A.sum(axis=1)
        r_inv_sqrt = jnp.power(rowsum, -0.5)
        r_inv_sqrt = jnp.where(jnp.isinf(r_inv_sqrt), 0.0, r_inv_sqrt)
        A_norm = r_inv_sqrt[:, None] * A * r_inv_sqrt[None, :]
        return A_norm.astype(jnp.float32) @ h.astype(jnp.float32)

    def _L1_gnn_ref(h, node_adj, edge_adj, gat_W, gat_a, edge_Wih, edge_Whh, edge_bih, edge_bhh, node_Wih, node_Whh, node_bih, node_bhh):
        import jax, jax.numpy as jnp
        import numpy as np
        N, H, HEADS = (2048, 128, 3)
        ALPHA = 0.2
        NEG_INF = -9000000000000000.0

        def _sign_adj(key, n, density):
            k1, k2 = jax.random.split(key)
            mask = jax.random.uniform(k1, (n, n)) < density
            sign = jnp.where(jax.random.uniform(k2, (n, n)) < 0.5, -1.0, 1.0)
            adj = jnp.where(mask, sign, 0.0).astype(jnp.float32)
            idx = jnp.arange(n)
            return adj.at[idx, idx].set(1.0)

        def _gru_cell(x, hstate, Wih, Whh, bih, bhh):
            gi = x @ Wih.T + bih
            gh = hstate @ Whh.T + bhh
            ir, iz, inn = jnp.split(gi, 3, axis=1)
            hr, hz, hn = jnp.split(gh, 3, axis=1)
            r = jax.nn.sigmoid(ir + hr)
            z = jax.nn.sigmoid(iz + hz)
            n = jnp.tanh(inn + r * hn)
            return (1.0 - z) * n + z * hstate

        def _gat_head(h, node_adj, edge_adj, W, a):
            hW = h @ W
            hp = (node_adj > 0).astype(hW.dtype) @ hW
            hm = (node_adj < 0).astype(hW.dtype) @ hW
            e_plus = jax.nn.leaky_relu(jnp.concatenate([hp, hm], axis=1) @ a, ALPHA)[:, 0]
            e_minus = jax.nn.leaky_relu(jnp.concatenate([hm, hp], axis=1) @ a, ALPHA)[:, 0]
            att = jnp.where(edge_adj > 0, e_plus[None, :], NEG_INF)
            att = jnp.where(edge_adj < 0, e_minus[None, :], att)
            att = jax.nn.softmax(att, axis=1)
            return att * edge_adj @ hW
        dn = jnp.diag(node_adj)
        de = jnp.diag(edge_adj)
        idx = jnp.arange(node_adj.shape[0])
        node_adj_norm = node_adj.at[idx, idx].add(-dn)
        edge_adj_norm = edge_adj.at[idx, idx].add(-de)
        node_support = node_adj_norm @ h
        edge_output = _gru_cell(node_support, h, edge_Wih, edge_Whh, edge_bih, edge_bhh)
        edge_support = _gat_head(h, node_adj_norm, edge_adj_norm, gat_W[0], gat_a[0])
        for i in range(1, HEADS):
            edge_support = edge_support + _gat_head(h, node_adj_norm, edge_adj_norm, gat_W[i], gat_a[i])
        edge_support = edge_support / HEADS
        node_output = _gru_cell(edge_support, h, node_Wih, node_Whh, node_bih, node_bhh)
        return de[:, None] * edge_output + dn[:, None] * node_output

    def _L2_gnn_ref(x, A_shape, W, bias, b):
        import jax, jax.numpy as jnp
        import numpy as np
        N = 4096
        D_IN = 128
        D_OUT = 128
        y = jnp.linalg.norm(x, axis=-1, keepdims=True)
        A = x @ x.T / (y @ y.T)
        A = A * b
        A = jnp.tanh(A / 8.0) * 8.0
        A = jnp.exp(A) * A_shape
        A = A / jnp.sum(A, axis=-1, keepdims=True)
        x = A @ x
        return x @ W.T + bias

    def _L3_gnn_ref(x, evals, evecs, t):
        import jax, jax.numpy as jnp
        import numpy as np
        N = 4096
        C = 128
        t_eff = jnp.clip(t[0], 1e-08, None)
        x_spec = jnp.einsum('nk,nc->kc', evecs, x)
        coefs = jnp.exp(-evals * t_eff)[:, None]
        out = jnp.einsum('nk,kc->nc', evecs, coefs * x_spec)
        return out
    x = _layernorm(x + _L0_gnn_ref(x, adj, L0_gnn_W, L0_gnn_b), axis=-1)
    x = _layernorm(x + _L1_gnn_ref(x, adj, adj, L1_gnn_gat_W, L1_gnn_gat_a, L1_gnn_edge_Wih, L1_gnn_edge_Whh, L1_gnn_edge_bih, L1_gnn_edge_bhh, L1_gnn_node_Wih, L1_gnn_node_Whh, L1_gnn_node_bih, L1_gnn_node_bhh), axis=-1)
    x = _layernorm(x + _L2_gnn_ref(x, adj, L2_gnn_W, L2_gnn_bias, L2_gnn_b), axis=-1)
    x = _layernorm(x + _L3_gnn_ref(x, L3_gnn_evals, adj, L3_gnn_t), axis=-1)
    return x

_drawn_inputs = setup_inputs


def setup_inputs(seed=0):
    import zlib

    import numpy as np

    out = dict(_drawn_inputs(seed))
    spreads = {'L1_gnn_edge_bih': (0.0, 0.1),
     'L1_gnn_edge_bhh': (0.0, 0.1),
     'L1_gnn_node_bih': (0.0, 0.1),
     'L1_gnn_node_bhh': (0.0, 0.1)}
    factors = {'L1_gnn_gat_a': 10.391,
     'L1_gnn_edge_Whh': 4.595,
     'L1_gnn_node_Whh': 4.369,
     'L1_gnn_gat_W': 2.767}
    for name, (base, spread) in spreads.items():
        noise = np.random.default_rng([zlib.crc32(name.encode()), seed]).standard_normal(out[name].shape)
        drawn = base * np.exp(spread * noise) if base else spread * noise
        out[name] = jnp.asarray(drawn.astype(out[name].dtype))
    for name, factor in factors.items():
        out[name] = (out[name] * factor).astype(out[name].dtype)
    return out
```

```python
from contextlib import ExitStack, contextmanager

import concourse.bass as bass
from concourse import mybir

ALU = mybir.AluOpType
ACT = mybir.ActivationFunctionType
F32 = mybir.dt.float32
BF16 = mybir.dt.bfloat16
I32 = mybir.dt.int32
AX_X = mybir.AxisListType.X

P = 128
N = 4096
D = 128
NT = N // P
HEADS = 3
RING = 4
LN_EPS = 1e-5
ALPHA = 0.2
BIG = float(2.0**100)
CH = 1024
TPC = CH // P
NCH = N // CH
PARTS = 3
KROWS = 2 * PARTS


def tiles(eng, body, unroll):
    for u in range(unroll):
        body(u, u, 0)
    with eng.Fori(1, NT // unroll) as r:
        for u in range(unroll):
            body(r * unroll + u, u, r)


def wait_from(eng, sem, value):
    if not isinstance(value, int) or value > 0:
        eng.wait_ge(sem, value)


class Chain:

    def __init__(self, eng, sem):
        self.eng, self.sem, self.n = eng, sem, 0

    def __call__(self, instruction):
        instruction.then_inc(self.sem, 1)
        self.n += 1
        self.eng.wait_ge(self.sem, self.n)


def build(nc, t_in, out, stop=99, force_signed=True):
    with ExitStack() as ctx:
        def sb(name, shape, dt=F32, c=ctx):
            return c.enter_context(nc.sbuf_tensor(name, shape, dt))

        live = []

        def sem(name):
            live.append(nc.alloc_semaphore(name=name))
            return live[-1]

        def next_layer():
            nc.clear_and_free_semaphores(live)
            live.clear()
            nc.all_engine_barrier()

        ps = ctx.enter_context(nc.psum_tensor("banks", [P, 8, 512], F32))

        ident = sb("ident", [P, P])
        identb = sb("identb", [P, P], BF16)
        offdiag = sb("offdiag", [P, P])
        negdiag = sb("negdiag", [P, P])
        stats = sb("stats", [P, NT * 6])
        moments = sb("moments", [P, NT * 2])
        col = sb("col", [P, 8 * NT])
        rstd = sb("rstd", [P, NT])
        diag = sb("diag", [P, NT])
        evals = sb("evals", [P, NT])
        tval = sb("tval", [P, 1])
        bval = sb("bval", [P, 1])

        x_dram = nc.dram_tensor("x_spill", [P, N], F32).ap()
        edge_dram = nc.dram_tensor("edge_spill", [P, N], F32).ap()
        sup_dram = nc.dram_tensor("support_spill", [P, N], F32).ap()
        e_dram = nc.dram_tensor("e_spill", [2 * HEADS, N], F32).ap()
        x_node = t_in["x"].rearrange("(t p) c -> p t c", p=P)
        out_node = out.rearrange("(t p) c -> p t c", p=P)
        adj, adjT, adjC = t_in["adj"], t_in["adjT_blk"], t_in["adj_cols"]

        def vc(k):
            return col[:, k * NT:(k + 1) * NT]

        def inverse_sqrt(dve, link, v, sq_in, sq_out, to_act, from_act):
            nc.vector.reciprocal(sq_in, v).then_inc(to_act, 1)
            dve.wait_ge(from_act, 1)
            tmp = vc(6)
            link(nc.vector.tensor_tensor(tmp, sq_out, sq_out, ALU.mult))
            link(nc.vector.tensor_tensor(tmp, tmp, v, ALU.mult))
            link(nc.vector.tensor_scalar(tmp, tmp, -0.5, 1.5, ALU.mult, ALU.add))
            link(nc.vector.tensor_tensor(v, tmp, sq_out, ALU.mult))

        def norm_dve(dve, link, y, to_act, from_act):
            for t in range(NT):
                last = nc.vector.bn_aggr(moments[:, 2 * t:2 * t + 2], stats[:, 6 * t:6 * t + 6])
            link(last)
            mean = moments[:, :].rearrange("p (t k) -> p k t", k=2)
            link(nc.vector.tensor_scalar(rstd[:, :], mean[:, 1, :], LN_EPS, None, ALU.add))
            inverse_sqrt(dve, link, rstd[:, :], vc(4), vc(5), to_act, from_act)
            for t in range(NT):
                last = nc.vector.tensor_scalar(y[:, t * P:(t + 1) * P], y[:, t * P:(t + 1) * P],
                                               moments[:, 2 * t:2 * t + 1], rstd[:, t:t + 1],
                                               ALU.subtract, ALU.mult)
            link(last)

        def root_act(act, to_act, from_act):
            act.wait_ge(to_act, 1)
            nc.scalar.activation(vc(5), vc(4), ACT.Sqrt).then_inc(from_act, 1)

        def pe_transposes(pe, src, s_tr, s_ev):
            for q in range(NT // 4):
                if q >= 2:
                    pe.wait_ge(s_ev, q - 1)
                for k in range(4):
                    t = 4 * q + k
                    last = nc.tensor.transpose(ps[:, q % 2, k * P:(k + 1) * P], src[:, t * P:(t + 1) * P],
                                               ident[:, :])
                last.then_inc(s_tr, 1)

        def act_evacuates(act, dst, s_tr, s_ev):
            for q in range(NT // 4):
                act.wait_ge(s_tr, q + 1)
                nc.scalar.copy(dst[:, q * 512:(q + 1) * 512], ps[:, q % 2, :]).then_inc(s_ev, 1)

        def store_x(eng, x):
            done = sem("out_done")
            eng.dma_start(out_node, x[:, :].rearrange("p (t c) -> p t c", c=P)).then_inc(done, 16)
            eng.wait_ge(done, 16)

        with ExitStack() as c01:
            x = sb("x0", [P, N], c=c01)
            g = sb("g", [P, N], c=c01)
            ring = [sb(f"ring0_{i}", [P, N], c=c01) for i in range(RING)]
            rowsum = sb("rowsum", [P, NT], c=c01)
            rinv = sb("rinv", [P, NT], c=c01)
            with ExitStack() as c0:
                w = sb("w0", [P, D], c=c0)
                b = sb("b0", [P, D], c=c0)
                xT = sb("xT0", [P, N], c=c0)
                s_id0, s_id, s_w, s_x = sem("id_memset"), sem("id_ready"), sem("w0_in"), sem("x_in")
                s_row = [sem(f"row_in{i}") for i in range(RING)]
                s_rowused, s_tr, s_xT = sem("row_summed"), sem("xT_psum"), sem("xT_sbuf")
                s_h, s_hev = sem("h_psum"), sem("h_sbuf")
                s_c, s_ta, s_fa = sem("chain0"), sem("root0_in"), sem("root0_out")
                with nc.Block() as block:
                    @block.sync
                    def _(sp):
                        sp.dma_start(w[:, :], t_in["W0T"]).then_inc(s_w, 16)
                        sp.dma_start(b[:, :], t_in["b0"].broadcast_to([P, D])).then_inc(s_w, 16)
                        sp.dma_start(diag[:, :], t_in["diag"]).then_inc(s_w, 16)
                        sp.dma_start(evals[:, :], t_in["evals"]).then_inc(s_w, 16)
                        sp.dma_start(tval[:, :], t_in["t"].broadcast_to([P, 1])).then_inc(s_w, 16)
                        sp.dma_start(bval[:, :], t_in["b2"].broadcast_to([P, 1])).then_inc(s_w, 16)
                        sp.dma_start(x[:, :].rearrange("p (t c) -> p t c", c=P), x_node).then_inc(s_x, 16)

                        def load(t, u, r):
                            wait_from(sp, s_rowused, t - RING + 1)
                            sp.dma_start(ring[u][:, :], adj[bass.ts(t, P), :]).then_inc(s_row[u], 16)
                        tiles(sp, load, RING)

                    @block.gpsimd
                    def _(pool):
                        nc.gpsimd.memset(ident[:, :], 0.0).then_inc(s_id0, 1)
                        nc.gpsimd.memset(identb[:, :], 0.0).then_inc(s_id0, 1)
                        nc.gpsimd.memset(offdiag[:, :], 1.0).then_inc(s_id0, 1)
                        nc.gpsimd.memset(negdiag[:, :], 0.0).then_inc(s_id0, 1)
                        pool.wait_ge(s_id0, 4)
                        for m, fill in ((ident, 1.0), (identb, 1.0), (offdiag, 0.0), (negdiag, -BIG)):
                            nc.gpsimd.affine_select(out=m[:, :], in_=m[:, :], compare_op=ALU.not_equal, fill=fill,
                                                    base=0, pattern=[[-1, P]], channel_multiplier=1).then_inc(s_id, 1)

                    @block.tensor
                    def _(pe):
                        pe.wait_ge(s_id, 4)
                        pe.wait_ge(s_x, 16)
                        pe.wait_ge(s_w, 96)
                        for q in range(NT // 4):
                            if q >= 2:
                                pe.wait_ge(s_xT, q - 1)
                            for k in range(4):
                                t = 4 * q + k
                                last = nc.tensor.transpose(ps[:, q % 2, k * P:(k + 1) * P], x[:, t * P:(t + 1) * P],
                                                           ident[:, :])
                            last.then_inc(s_tr, 1)
                        for q in range(NT // 4):
                            pe.wait_ge(s_xT, q + 1)
                            if q >= 2:
                                pe.wait_ge(s_hev, q - 1)
                            for k in range(4):
                                t = 4 * q + k
                                last = nc.tensor.matmul(ps[:, 2 + q % 2, k * P:(k + 1) * P],
                                                        xT[:, t * P:(t + 1) * P], w[:, :], start=True, stop=True)
                            last.then_inc(s_h, 1)

                    @block.scalar
                    def _(act):
                        for q in range(NT // 4):
                            act.wait_ge(s_tr, q + 1)
                            nc.scalar.copy(xT[:, q * 512:(q + 1) * 512], ps[:, q % 2, :]).then_inc(s_xT, 1)
                        root_act(act, s_ta, s_fa)

                    @block.vector
                    def _(dve):
                        dve.wait_ge(s_w, 96)
                        for q in range(NT // 4):
                            dve.wait_ge(s_h, q + 1)
                            nc.vector.tensor_tensor(
                                g[:, q * 512:(q + 1) * 512].rearrange("p (k c) -> p k c", c=D),
                                ps[:, 2 + q % 2, :].rearrange("p (k c) -> p k c", c=D),
                                b[:, :].rearrange("p (a c) -> p a c", a=1).broadcast_to([P, 4, D]),
                                ALU.add).then_inc(s_hev, 1)

                        def row_sum(t, u, r):
                            dve.wait_ge(s_row[u], r * 16 + 16)
                            nc.vector.tensor_reduce(rowsum[:, bass.ds(t, 1)], ring[u][:, :], AX_X,
                                                    ALU.add).then_inc(s_rowused, 1)
                        tiles(dve, row_sum, RING)
                        dve.wait_ge(s_rowused, NT)
                        dve.wait_ge(s_hev, NT // 4)
                        link = Chain(dve, s_c)
                        link(nc.vector.tensor_scalar(rinv[:, :], rowsum[:, :], 1.0, None, ALU.add))
                        link(nc.vector.tensor_scalar(vc(0), rinv[:, :], 0.0, None, ALU.is_equal))
                        link(nc.vector.tensor_tensor(rinv[:, :], rinv[:, :], vc(0), ALU.add))
                        inverse_sqrt(dve, link, rinv[:, :], vc(4), vc(5), s_ta, s_fa)
                        link(nc.vector.tensor_scalar(vc(0), vc(0), -1.0, 1.0, ALU.mult, ALU.add))
                        link(nc.vector.tensor_tensor(rinv[:, :], rinv[:, :], vc(0), ALU.mult))
                        for t in range(NT):
                            last = nc.vector.tensor_scalar(g[:, t * P:(t + 1) * P], g[:, t * P:(t + 1) * P],
                                                           rinv[:, t:t + 1], None, ALU.mult)
                        link(last)

            s_blk = [sem(f"blk0_in{i}") for i in range(RING)]
            s_agg, s_ev, s_c = sem("agg0_psum"), sem("agg0_read"), sem("chain0b")
            s_c2, s_ta, s_fa, s_sp = sem("chain0c"), sem("root0b_in"), sem("root0b_out"), sem("x1_out")
            with nc.Block() as block:
                @block.sync
                def _(sp):
                    def load(t, u, r):
                        wait_from(sp, s_agg, t - RING + 1)
                        sp.dma_start(ring[u][:, :], adjT[t]).then_inc(s_blk[u], 16)
                    tiles(sp, load, RING)
                    sp.wait_ge(s_sp, 1)
                    x_done = sem("x1_done")
                    sp.dma_start(x_dram, x[:, :]).then_inc(x_done, 16)
                    sp.wait_ge(x_done, 16)

                @block.tensor
                def _(pe):
                    def aggregate(t, u, r):
                        pe.wait_ge(s_blk[u], r * 16 + 16)
                        wait_from(pe, s_ev, t - 1)
                        for j in range(NT):
                            last = nc.tensor.matmul(ps[:, u % 2, 0:D], ring[u][:, j * P:(j + 1) * P],
                                                    g[:, j * P:(j + 1) * P], start=(j == 0), stop=(j == NT - 1))
                        last.then_inc(s_agg, 1)
                    tiles(pe, aggregate, RING)

                @block.scalar
                def _(act):
                    root_act(act, s_ta, s_fa)

                @block.vector
                def _(dve):
                    tmp = col[:, 0:P]

                    def residual(t, u, r):
                        dve.wait_ge(s_agg, t + 1)
                        nc.vector.tensor_tensor(tmp, ps[:, u % 2, 0:D], g[:, bass.ts(t, P)],
                                                ALU.add).then_inc(s_ev, 1)
                        dve.wait_ge(s_ev, t + 1)
                        nc.vector.scalar_tensor_tensor(out=x[:, bass.ts(t, P)], in0=tmp, scalar=rinv[:, bass.ds(t, 1)],
                                                       in1=x[:, bass.ts(t, P)], op0=ALU.mult,
                                                       op1=ALU.add).then_inc(s_c, 1)
                        dve.wait_ge(s_c, t + 1)
                        nc.vector.bn_stats(stats[:, bass.ts(t, 6)], x[:, bass.ts(t, P)]).then_inc(s_c2, 1)
                    tiles(dve, residual, RING)
                    dve.wait_ge(s_c2, NT)
                    link = Chain(dve, sem("chain0d"))
                    norm_dve(dve, link, x, s_ta, s_fa)
                    nc.vector.tensor_copy(col[:, 0:1], x[:, 0:1]).then_inc(s_sp, 1)

            if stop == 0:
                with nc.Block() as block:
                    @block.sync
                    def _(sp):
                        store_x(sp, x)
                return

        next_layer()
        def gru(src, x, base, dst, wih, whh, bias, scale, own, steps, first_act=None, after_dve=None, sync=None):
            srcT, xT, pre, rz, cand, diff = own
            s_tr, s_tev, s_gate, s_pre, s_rz, s_nin, s_n, s_out, s_c = [sem(f"gru_{steps}_{k}") for k in (
                "transposed", "transposed_sbuf", "gates", "pre", "rz", "cand_in", "cand", "out", "chain")]
            PER = 7

            def groups(eng, body):
                body(0)
                with eng.Fori(1, NT // 4) as q:
                    body(q)

            def on_pe(pe):
                def body(q):
                    wait_from(pe, s_tev, q)
                    for k in range(4):
                        nc.tensor.transpose(ps[:, 0, k * P:(k + 1) * P], src[:, (4 * q + k) * P:(4 * q + k + 1) * P], ident[:, :])
                        last = nc.tensor.transpose(ps[:, 1, k * P:(k + 1) * P], x[:, (4 * q + k) * P:(4 * q + k + 1) * P],
                                                   ident[:, :])
                    last.then_inc(s_tr, 1)
                    pe.wait_ge(s_tev, q + 1)
                    wait_from(pe, s_pre, q)
                    for k in range(4):
                        c = slice(k * P, (k + 1) * P)
                        nc.tensor.matmul(ps[:, 2 + k, 0:256], srcT[:, c], wih[:, 0:256], start=True, stop=False)
                        nc.tensor.matmul(ps[:, 2 + k, 0:256], xT[:, c], whh[:, 0:256], start=False, stop=True)
                        nc.tensor.matmul(ps[:, 2 + k, 256:384], srcT[:, c], wih[:, 256:384], start=False, stop=True,
                                         skip_group_check=True)
                        last = nc.tensor.matmul(ps[:, 2 + k, 384:512], xT[:, c], whh[:, 256:384], start=False,
                                                stop=True, skip_group_check=True)
                    last.then_inc(s_gate, 1)
                for q in range(NT // 4):
                    body(q)

            def on_act(act):
                def body(q):
                    act.wait_ge(s_tr, q + 1)
                    wait_from(act, s_gate, q)
                    nc.scalar.copy(srcT[:, :], ps[:, 0, :])
                    nc.scalar.copy(xT[:, :], ps[:, 1, :]).then_inc(s_tev, 1)
                    act.wait_ge(s_pre, q + 1)
                    nc.scalar.activation(rz3, pre3[:, :, 0:256], ACT.Tanh, scale=0.5).then_inc(s_rz, 1)
                    act.wait_ge(s_nin, q + 1)
                    nc.scalar.activation(cand[:, :], cand[:, :], ACT.Tanh).then_inc(s_n, 1)
                groups(act, body)

            pre3 = pre[:, :].rearrange("p (k c) -> p k c", c=512)
            rz3 = rz[:, :].rearrange("p (k c) -> p k c", c=256)
            cand3 = cand[:, :].rearrange("p (k c) -> p k c", c=P)
            diff3 = diff[:, :].rearrange("p (k c) -> p k c", c=P)

            def on_dve(dve):
                def body(q):
                    dve.wait_ge(s_gate, q + 1)
                    nc.vector.tensor_tensor(pre3, ps[:, 2:6, :],
                                            bias[:, :].rearrange("p (a c) -> p a c", a=1).broadcast_to([P, 4, 512]),
                                            ALU.add).then_inc(s_pre, 1)
                    dve.wait_ge(s_pre, q + 1)
                    dve.wait_ge(s_rz, q + 1)
                    step = [0]

                    def link(ins):
                        step[0] += 1
                        ins.then_inc(s_c, 1)
                        dve.wait_ge(s_c, q * PER + step[0])
                    link(nc.vector.tensor_scalar(rz[:, :], rz[:, :], 0.5, 0.5, ALU.mult, ALU.add))
                    link(nc.vector.tensor_tensor(cand3, rz3[:, :, 0:P], pre3[:, :, 384:512], ALU.mult))
                    nc.vector.tensor_tensor(cand3, cand3, pre3[:, :, 256:384], ALU.add).then_inc(s_nin, 1)
                    dve.wait_ge(s_n, q + 1)
                    x4 = x[:, bass.ts(q, 512)].rearrange("p (k c) -> p k c", c=P)
                    link(nc.vector.tensor_tensor(diff3, x4, cand3, ALU.subtract))
                    link(nc.vector.tensor_tensor(diff3, diff3, rz3[:, :, P:256], ALU.mult))
                    link(nc.vector.tensor_tensor(diff3, diff3, cand3, ALU.add))
                    for k in range(4):
                        t = q * 4 + k
                        last = nc.vector.scalar_tensor_tensor(
                            out=dst[:, bass.ts(t, P)], in0=diff[:, k * P:(k + 1) * P], scalar=scale[:, bass.ds(t, 1)],
                            in1=base[:, bass.ts(t, P)], op0=ALU.mult, op1=ALU.add)
                    link(last)
                    if after_dve is not None:
                        for k in range(4):
                            last = nc.vector.bn_stats(stats[:, bass.ts(q * 4 + k, 6)], dst[:, bass.ts(q * 4 + k, P)])
                        last.then_inc(s_c, 1)
                    else:
                        nc.vector.tensor_copy(col[:, 0:1], diff[:, 0:1]).then_inc(s_c, 1)
                groups(dve, body)
                dve.wait_ge(s_c, PER * NT // 4)
                if after_dve is not None:
                    after_dve(dve)

            return on_pe, on_act, on_dve

        def gru_buffers(c, which):
            return [sb(f"{which}_{k}", [P, n], c=c) for k, n in (
                ("srcT", 512), ("xT", 512), ("pre", 2048), ("rz", 1024), ("cand", 512), ("diff", 512))]

        def gru_bias(dve, link, braw, bias):
            link(nc.vector.tensor_tensor(bias[:, 0:256], braw[:, 0:256], braw[:, 384:640], ALU.add))
            link(nc.vector.tensor_copy(bias[:, 256:384], braw[:, 256:384]))
            link(nc.vector.tensor_copy(bias[:, 384:512], braw[:, 640:768]))

        UC = 2 * HEADS * PARTS + 1
        UW = UC + 1
        with ExitStack() as c1:
            hW = sb("hW", [P, NT * HEADS * D], c=c1)
            prow = sb("prow", [P, N], BF16, c=c1)
            esc = sb("esc", [P, 2 * HEADS * NT], c=c1)
            flag = sb("flag", [P, 1], I32, c=c1)
            with ExitStack() as ca:
                x = sb("x1", [P, N], c=ca)
                ns = sb("ns", [P, N], c=ca)
                usplit = sb("usplit", [P, NT * UW], BF16, c=ca)
                usp3 = usplit[:, :].rearrange("p (t k) -> p t k", k=UW)
                with ExitStack() as cp:
                    xT = sb("x1T", [P, N], c=cp)
                    gW = sb("gW", [P, HEADS * D], c=cp)
                    gWT = sb("gWT", [P, HEADS * D], c=cp)
                    ga = sb("ga", [P, 2 * HEADS], c=cp)
                    va = sb("va", [P, 2 * HEADS], c=cp)
                    u = sb("u", [P, NT * 2 * HEADS], c=cp)
                    s_in, s_tr, s_ev, s_va, s_vac, s_u, s_hw, s_hwe, s_c = [sem(f"proj_{k}") for k in (
                        "in", "tr", "ev", "va", "vac", "u", "hw", "hwe", "chain")]
                    with nc.Block() as block:
                        @block.sync
                        def _(sp):
                            sp.dma_start(x[:, :], x_dram).then_inc(s_in, 16)
                            sp.dma_start(gW[:, :], t_in["gat_W"]).then_inc(s_in, 16)
                            sp.dma_start(gWT[:, :], t_in["gat_WT"]).then_inc(s_in, 16)
                            sp.dma_start(ga[:, :], t_in["gat_a"]).then_inc(s_in, 16)

                        @block.tensor
                        def _(pe):
                            pe.wait_ge(s_in, 64)
                            for h in range(HEADS):
                                last = nc.tensor.matmul(ps[:, 7, 2 * h:2 * h + 2], gWT[:, h * D:(h + 1) * D],
                                                        ga[:, 2 * h:2 * h + 2], start=True, stop=True)
                            last.then_inc(s_va, 1)
                            pe_transposes(pe, x, s_tr, s_ev)
                            pe.wait_ge(s_ev, NT // 4)
                            pe.wait_ge(s_vac, 1)
                            for t in range(NT):
                                last = nc.tensor.matmul(ps[:, 6, t * 6:t * 6 + 6], xT[:, t * P:(t + 1) * P], va[:, :],
                                                        start=True, stop=True)
                            last.then_inc(s_u, 1)
                            for t in range(NT):
                                if t >= 4:
                                    pe.wait_ge(s_hwe, t - 3)
                                nc.tensor.matmul(ps[:, 2 + t % 4, 0:HEADS * D], xT[:, t * P:(t + 1) * P], gW[:, :],
                                                 start=True, stop=True).then_inc(s_hw, 1)

                        @block.scalar
                        def _(act):
                            act_evacuates(act, xT, s_tr, s_ev)
                            for t in range(NT):
                                act.wait_ge(s_hw, t + 1)
                                nc.scalar.copy(hW[:, t * 384:(t + 1) * 384], ps[:, 2 + t % 4, 0:384]).then_inc(s_hwe, 1)

                        @block.vector
                        def _(dve):
                            link = Chain(dve, s_c)
                            dve.wait_ge(s_va, 1)
                            nc.vector.tensor_copy(va[:, :], ps[:, 7, 0:6]).then_inc(s_vac, 1)
                            nc.vector.memset(usplit[:, :], 1.0).then_inc(s_c, 1)
                            link.n += 1
                            dve.wait_ge(s_c, link.n)
                            dve.wait_ge(s_u, 1)
                            link(nc.vector.tensor_copy(u[:, :], ps[:, 6, 0:NT * 6]))
                            u3 = u[:, :].rearrange("p (t k) -> p t k", k=6)
                            for k in range(PARTS):
                                part = usp3[:, :, 6 * k:6 * k + 6]
                                link(nc.vector.tensor_copy(part, u3))
                                if k < PARTS - 1:
                                    link(nc.vector.tensor_tensor(u3, u3, part, ALU.subtract))
                if stop == 1:
                    return

                with ExitStack() as cl:
                    R1 = 2
                    ring = [sb(f"ring1_{i}", [P, N], c=cl) for i in range(R1)]
                    pos = [sb(f"pos{i}", [P, N], BF16, c=cl) for i in range(2)]
                    neg = [sb(f"neg{i}", [P, N], BF16, c=cl) for i in range(2)]
                    raw = sb("raw", [P, NT * 2 * UC], c=cl)
                    s_blk = [sem(f"blk1_in{i}") for i in range(R1)]
                    s_dz, s_pos, s_neg, s_ns, s_pn, s_rd = [sem(f"sums_{k}") for k in (
                        "diag_cleared", "positive", "negative", "ns_psum", "pn_psum", "read")]
                    with nc.Block() as block:
                        @block.sync
                        def _(sp):
                            def load(t, u, r):
                                wait_from(sp, s_ns, t - R1 + 1)
                                wait_from(sp, s_neg, t - R1 + 1)
                                sp.dma_start(ring[u][:, :], adjT[t]).then_inc(s_blk[u], 16)
                            tiles(sp, load, R1)

                        @block.vector
                        def _(dve):
                            def masks(t, u, r):
                                dve.wait_ge(s_blk[u], r * 16 + 16)
                                d = ring[u][:, bass.ts(t, P)]
                                nc.vector.tensor_tensor(d, d, offdiag[:, :], ALU.mult).then_inc(s_dz, 1)
                                dve.wait_ge(s_dz, t + 1)
                                wait_from(dve, s_pn, t - 1)
                                nc.vector.tensor_scalar(pos[u][:, :], ring[u][:, :], 0.0, None,
                                                        ALU.is_gt).then_inc(s_pos, 1)
                                nc.vector.tensor_scalar(neg[u][:, :], ring[u][:, :], 0.0, None,
                                                        ALU.is_lt).then_inc(s_neg, 1)
                            tiles(dve, masks, R1)

                        @block.tensor
                        def _(pe):
                            def sums(t, u, r):
                                pe.wait_ge(s_blk[u], r * 16 + 16)
                                pe.wait_ge(s_dz, t + 1)
                                wait_from(pe, s_rd, t - 1)
                                for j in range(NT):
                                    last = nc.tensor.matmul(ps[:, u, 0:D], ring[u][:, j * P:(j + 1) * P],
                                                            x[:, j * P:(j + 1) * P], start=(j == 0), stop=(j == NT - 1))
                                last.then_inc(s_ns, 1)
                                for m, (mask, ready) in enumerate(((pos[u], s_pos), (neg[u], s_neg))):
                                    pe.wait_ge(ready, t + 1)
                                    for j in range(NT):
                                        last = nc.tensor.matmul(ps[:, 2 + u, m * UC:(m + 1) * UC],
                                                                mask[:, j * P:(j + 1) * P],
                                                                usplit[:, j * UW:j * UW + UC],
                                                                start=(j == 0), stop=(j == NT - 1))
                                last.then_inc(s_pn, 1)
                            tiles(pe, sums, R1)

                        @block.scalar
                        def _(act):
                            def keep(t, u, r):
                                act.wait_ge(s_ns, t + 1)
                                nc.scalar.copy(ns[:, bass.ts(t, P)], ps[:, u, 0:D])
                                act.wait_ge(s_pn, t + 1)
                                nc.scalar.copy(raw[:, bass.ts(t, 2 * UC)], ps[:, 2 + u, 0:2 * UC]).then_inc(s_rd, 1)
                            tiles(act, keep, R1)

                    s_c, s_any, s_anyc, s_e, s_ec, s_row, s_wr, s_pm, s_pt, s_pe_, s_z = [sem(f"score_{k}") for k in (
                        "chain", "any", "any_sbuf", "e", "e_rows", "rowT", "written", "pcol", "ptr", "prow", "z")]
                    sm = sb("score_parts", [P, NT * 12], c=cl)
                    eT = sb("eT", [P, P], c=cl)
                    cnt = sb("cnt", [P, 1], c=cl)
                    onec = sb("onec", [P, 1], c=cl)
                    pcol = sb("pcol", [P, N], BF16, c=cl)
                    rem = sb("rem", [P, HEADS * NT], c=cl)
                    with nc.Block() as block:
                        @block.vector
                        def _(dve):
                            link = Chain(dve, s_c)
                            r4 = raw[:, :].rearrange("p (t m k) -> p t m k", m=2, k=UC)
                            s4 = sm[:, :].rearrange("p (t m k) -> p t m k", m=2, k=6)
                            link(nc.vector.tensor_reduce(cnt[:, :], r4[:, :, 1, UC - 1], AX_X, ALU.max))
                            nc.vector.memset(onec[:, :], 1.0).then_inc(s_any, 1)
                            for m in range(2):
                                link(nc.vector.tensor_tensor(s4[:, :, m, :], r4[:, :, m, 12:18], r4[:, :, m, 6:12], ALU.add))
                                link(nc.vector.tensor_tensor(s4[:, :, m, :], s4[:, :, m, :], r4[:, :, m, 0:6], ALU.add))
                            e4 = esc[:, :].rearrange("p (s h t) -> p s h t", s=2, h=HEADS)
                            for h in range(HEADS):
                                for s in range(2):
                                    link(nc.vector.tensor_tensor(e4[:, s, h, :], s4[:, :, s, 2 * h],
                                                                 s4[:, :, 1 - s, 2 * h + 1], ALU.add))
                            link(nc.vector.tensor_scalar(sm[:, 0:192], esc[:, :], ALPHA, None, ALU.mult))
                            link(nc.vector.tensor_tensor(esc[:, :], esc[:, :], sm[:, 0:192], ALU.max))
                            link(nc.vector.memset(pcol[:, :], 0.0))
                            p3 = pcol[:, :].rearrange("p (t k) -> p t k", k=P)
                            link(nc.vector.tensor_copy(rem[:, :], esc[:, 0:HEADS * NT]))
                            for k in range(PARTS):
                                for h in range(HEADS):
                                    link(nc.vector.tensor_copy(p3[:, :, KROWS * h + k], rem[:, h * NT:(h + 1) * NT]))
                                    link(nc.vector.memset(p3[:, :, KROWS * h + PARTS + k], 1.0))
                                    if k < PARTS - 1:
                                        link(nc.vector.tensor_tensor(rem[:, h * NT:(h + 1) * NT],
                                                                     rem[:, h * NT:(h + 1) * NT],
                                                                     p3[:, :, KROWS * h + k], ALU.subtract))
                            nc.vector.tensor_copy(cnt[:, :], cnt[:, :]).then_inc(s_e, 1)
                            dve.wait_ge(s_anyc, 1)
                            nc.vector.tensor_scalar(flag[0:1, :], ps[0:1, 7, 0:1], 1.0, None, ALU.min).then_inc(s_z, 1)

                        @block.tensor
                        def _(pe):
                            pe.wait_ge(s_any, 1)
                            pe.wait_ge(s_e, 1)
                            nc.tensor.matmul(ps[0:1, 7, 0:1], cnt[:, :], onec[:, :], start=True, stop=True)\
                                .then_inc(s_anyc, 1)
                            nc.tensor.transpose(ps[0:HEADS * NT, 6, 0:P], esc[:, 0:HEADS * NT], ident[:, :])
                            nc.tensor.transpose(ps[0:HEADS * NT, 6, P:2 * P], esc[:, HEADS * NT:], ident[:, :])\
                                .then_inc(s_row, 1)
                            for q in range(NT // 4):
                                if q >= 2:
                                    pe.wait_ge(s_pe_, q - 1)
                                for k in range(4):
                                    t = 4 * q + k
                                    last = nc.tensor.transpose(
                                        ps[:, q % 2, :].bitcast(BF16)[:, k * P:(k + 1) * P], pcol[:, t * P:(t + 1) * P],
                                        identb[:, :])
                                last.then_inc(s_pt, 1)

                        @block.scalar
                        def _(act):
                            act.wait_ge(s_row, 1)
                            eT2 = sb("eT2", [P, 2 * P], c=cl)
                            nc.scalar.copy(eT2[0:HEADS * NT, :], ps[0:HEADS * NT, 6, 0:2 * P]).then_inc(s_ec, 1)
                            act.wait_ge(s_ec, 1)
                            for s in range(2):
                                act.dma_start(e_dram[s * HEADS:(s + 1) * HEADS, :].rearrange("h (t p) -> (h t) p", p=P),
                                              eT2[0:HEADS * NT, s * P:(s + 1) * P]).then_inc(s_wr, 16)
                            for q in range(NT // 4):
                                act.wait_ge(s_pt, q + 1)
                                nc.scalar.copy(prow[:, q * 512:(q + 1) * 512],
                                               ps[:, q % 2, :].bitcast(BF16)[:, 0:512]).then_inc(s_pe_, 1)
                            act.wait_ge(s_wr, 32)

                with ExitStack() as cg:
                    own = gru_buffers(cg, "edge")
                    wih, whh = sb("edge_wih", [P, 384], c=cg), sb("edge_whh", [P, 384], c=cg)
                    braw, bias = sb("edge_braw", [P, 768], c=cg), sb("edge_bias", [P, 512], c=cg)
                    s_in, s_b, s_fin, s_dn = sem("edge_in"), sem("edge_bias_ready"), sem("edge_done"), sem("edge_out")
                    pe_f, act_f, dve_f = gru(ns, x, x, ns, wih, whh, bias, diag, own, "edge")
                    with nc.Block() as block:
                        @block.sync
                        def _(sp):
                            sp.dma_start(wih[:, :], t_in["edge_WihT"]).then_inc(s_in, 16)
                            sp.dma_start(whh[:, :], t_in["edge_WhhT"]).then_inc(s_in, 16)
                            sp.dma_start(braw[:, :], t_in["edge_b"].broadcast_to([P, 768])).then_inc(s_in, 16)
                            sp.wait_ge(s_fin, 1)
                            sp.dma_start(edge_dram, ns[:, :]).then_inc(s_dn, 16)
                            sp.wait_ge(s_dn, 16)

                        @block.tensor
                        def _(pe):
                            pe.wait_ge(s_in, 48)
                            pe_f(pe)

                        @block.scalar
                        def _(act):
                            act_f(act)

                        @block.vector
                        def _(dve):
                            dve.wait_ge(s_in, 48)
                            gru_bias(dve, Chain(dve, s_b), braw, bias)
                            dve_f(dve)
                            nc.vector.tensor_copy(col[:, 0:1], diag[:, 0:1]).then_inc(s_fin, 1)

            if stop == 2:
                with ExitStack() as cd:
                    x = sb("dbg", [P, N], c=cd)
                    with nc.Block() as block:
                        @block.sync
                        def _(sp):
                            d = sem("dbg_in")
                            sp.dma_start(x[:, :], edge_dram).then_inc(d, 16)
                            sp.wait_ge(d, 16)
                            store_x(sp, x)
                return
            @contextmanager
            def only_if_signed(eng, signed):
                found = eng.alloc_register(f"negative_weights_{int(signed)}")
                eng.load(found, flag[0:1, 0:1])
                with eng.If_eq(found, int(signed)):
                    yield

            SLOTS, EXPD, WGT = 6, 3, 2
            with ExitStack() as cl:
                ebc = sb("ebc", [P, HEADS * N], c=cl)
                blk = [sb(f"at{i}", [P, N], c=cl) for i in range(2)]
                row = sb("row", [P, N], c=cl)
                score = sb("score", [P, SLOTS * CH], c=cl)
                maskT = [sb(f"maskT{i}", [P, N], BF16, c=cl) for i in range(2)]
                expd = [sb(f"expd{i}", [P, CH], c=cl) for i in range(EXPD)]
                wgt = [sb(f"wgt{i}", [P, CH], c=cl) for i in range(WGT)]
                mcol = sb("mcol", [P, HEADS * P], BF16, c=cl)
                mrow = [sb(f"mrow{i}", [P, HEADS * P], BF16, c=cl) for i in range(2)]
                nmax = [sb(f"nmax{i}", [P, HEADS], c=cl) for i in range(2)]
                nrem = sb("nrem", [P, HEADS], c=cl)
                mx = sb("mx", [P, HEADS * NCH], c=cl)
                den = sb("den", [P, HEADS * NT * NCH], c=cl)
                iden = sb("iden", [P, HEADS], c=cl)
                es = [sb(f"es{i}", [P, D], c=cl) for i in range(2)]
                s_ebc, s_row, s_mask, s_top, s_top1, s_nm, s_den = [sem(f"gat_{k}") for k in (
                    "ebc_in", "row_in", "mask_steps", "max", "head_max", "negmax", "den")]
                s_blk = [sem(f"gat_blk_in{i}") for i in range(2)]
                s_part, s_mcol, s_mtr, s_mrow, s_lt, s_x, s_r, s_b, s_num = [sem(f"gat_{k}") for k in (
                    "part_steps", "mcol", "mcol_T", "mrow", "maskT", "exponent", "expd", "weighted", "summed")]
                s_e, s_es = sem("gat_es_steps"), sem("gat_es")
                s_eout = [sem(f"gat_es_out{i}") for i in range(2)]
                s_id2, s_init = sem("gat_init"), sem("gat_mcol_init")
                Q = HEADS * NCH

                def blocks(eng, body, start=0):
                    for t in range(start, 2):
                        body(t, t, 2)
                    with eng.Fori(1, NT // 2 - 1) as r:
                        body(r * 2, 0, 2)
                        body(r * 2 + 1, 1, 2)
                    body(NT - 2, 0, 1)
                    body(NT - 1, 1, 0)

                with nc.Block() as block:
                    @block.sync
                    def _(sp):
                        with only_if_signed(sp, False):
                            for h in range(HEADS):
                                sp.dma_start(ebc[:, h * N:(h + 1) * N],
                                             e_dram[h:h + 1, :].broadcast_to([P, N])).then_inc(s_ebc, 16)

                            def rows(t):
                                for c in range(NCH):
                                    wait_from(sp, s_top, t * Q - NCH + c + 1)
                                    sp.dma_start(row[:, c * CH:(c + 1) * CH],
                                                 adj[bass.ts(t, P), c * CH:(c + 1) * CH]).then_inc(s_row, 16)

                            def store(t, u):
                                sp.wait_ge(s_es, t + 1)
                                sp.dma_start(sup_dram[:, bass.ts(t, P)], es[u][:, :]).then_inc(s_eout[u], 16)

                            rows(0)
                            for u in range(2):
                                sp.dma_start(blk[u][:, :], adjT[u]).then_inc(s_blk[u], 16)
                            rows(1)
                            rows(2)

                            def load(t, u, left):
                                if left:
                                    rows(t + 1)
                                sp.wait_ge(s_b, (t - 1) * Q)
                                sp.dma_start(blk[u][:, :], adjT[t]).then_inc(s_blk[u], 16)
                                store(t - 2, u)
                            blocks(sp, load, start=2)
                            for u in range(2):
                                store(NT - 2 + u, u)
                            for u in range(2):
                                sp.wait_ge(s_eout[u], 16 * NT // 2)

                    @block.vector
                    def _(dve):
                        with only_if_signed(dve, False):
                            def row_mask(t):
                                dve.wait_ge(s_row, (t + 1) * 16 * NCH)
                                nc.vector.tensor_scalar(row[:, :], row[:, :], 0.0, -BIG, ALU.is_equal,
                                                        ALU.mult).then_inc(s_mask, 1)
                                dve.wait_ge(s_mask, t * 2 + 1)
                                d = row[:, bass.ts(t, P)]
                                nc.vector.tensor_tensor(d, d, negdiag[:, :], ALU.add).then_inc(s_mask, 1)

                            def row_piece(t, u, k):
                                h, c = k // NCH, k % NCH
                                slot = k % SLOTS
                                nc.vector.tensor_tensor_reduce(score[:, slot * CH:(slot + 1) * CH],
                                                               row[:, c * CH:(c + 1) * CH],
                                                               ebc[:, h * N + c * CH:h * N + (c + 1) * CH], 1.0, -3.0e38,
                                                               ALU.add, ALU.max, mx[:, k:k + 1]).then_inc(s_top, 1)
                                if c < NCH - 1:
                                    return
                                dve.wait_ge(s_top, t * Q + k + 1)
                                nc.vector.tensor_reduce(nrem[:, h:h + 1], mx[:, h * NCH:(h + 1) * NCH], AX_X,
                                                        ALU.max).then_inc(s_top1, 1)
                                dve.wait_ge(s_top1, t * HEADS + h + 1)
                                nc.vector.tensor_scalar(nmax[u][:, h:h + 1], nrem[:, h:h + 1], -BIG / 2, -1.0, ALU.max,
                                                        ALU.mult).then_inc(s_nm, 1)

                            def slot_free(t, k):
                                wait_from(dve, s_den, t * Q + k + 1 - SLOTS)

                            def max_parts(t, u):
                                dve.wait_ge(s_nm, (t + 1) * HEADS)
                                wait_from(dve, s_mtr, t)
                                src = nmax[u]
                                n = 0
                                for k in range(PARTS):
                                    s0 = PARTS + k
                                    part = mcol[:, s0:s0 + 2 * (P + KROWS) + 1:P + KROWS]
                                    ins = nc.vector.tensor_copy(part, src[:, :])
                                    if k == PARTS - 1:
                                        ins.then_inc(s_mcol, 1)
                                        break
                                    n += 1
                                    ins.then_inc(s_part, 1)
                                    dve.wait_ge(s_part, t * 4 + n)
                                    n += 1
                                    nc.vector.tensor_tensor(nrem[:, :], src[:, :], part, ALU.subtract).then_inc(s_part, 1)
                                    dve.wait_ge(s_part, t * 4 + n)
                                    src = nrem

                            def block_mask(t, u, r16):
                                dve.wait_ge(s_blk[u], r16)
                                wait_from(dve, s_x, (t - 1) * Q)
                                nc.vector.tensor_scalar(maskT[u][:, :], blk[u][:, :], 0.0, -BIG, ALU.is_equal,
                                                        ALU.mult).then_inc(s_lt, 1)
                                dve.wait_ge(s_lt, t * 2 + 1)
                                d = maskT[u][:, bass.ts(t, P)]
                                nc.vector.tensor_tensor(d, d, negdiag[:, :], ALU.add).then_inc(s_lt, 1)

                            def weigh(t, u, q):
                                c = q % NCH
                                dve.wait_ge(s_r, t * Q + q + 1)
                                wait_from(dve, s_num, t * Q + q + 1 - WGT)
                                nc.vector.tensor_tensor(wgt[q % WGT][:, :], expd[q % EXPD][:, :], blk[u][:, c * CH:(c + 1) * CH],
                                                        ALU.mult).then_inc(s_b, 1)

                            def combine(t, u):
                                dve.wait_ge(s_den, (t + 1) * Q)
                                wait_from(dve, s_es, t)
                                nc.vector.tensor_reduce(iden[:, :], den[:, bass.ds(t * Q, Q)]
                                                        .rearrange("p (h c) -> p h c", c=NCH), AX_X,
                                                        ALU.add).then_inc(s_e, 1)
                                dve.wait_ge(s_e, t * 5 + 1)
                                nc.vector.tensor_scalar(iden[:, :], iden[:, :], 1e-30, float(HEADS),
                                                        ALU.max, ALU.mult).then_inc(s_e, 1)
                                dve.wait_ge(s_e, t * 5 + 2)
                                nc.vector.reciprocal(iden[:, :], iden[:, :]).then_inc(s_e, 1)
                                dve.wait_ge(s_e, t * 5 + 3)
                                dve.wait_ge(s_num, (t + 1) * Q)
                                if not (isinstance(t, int) and t < 2):
                                    dve.wait_ge(s_eout[u], (t - u) * 8)
                                for h in range(HEADS):
                                    a = ps[:, 4 + u, h * D:(h + 1) * D]
                                    if h == 0:
                                        ins = nc.vector.tensor_scalar(es[u][:, :], a, iden[:, 0:1], None, ALU.mult)
                                    else:
                                        ins = nc.vector.scalar_tensor_tensor(out=es[u][:, :], in0=a,
                                                                             scalar=iden[:, h:h + 1], in1=es[u][:, :],
                                                                             op0=ALU.mult, op1=ALU.add)
                                    if h < HEADS - 1:
                                        ins.then_inc(s_e, 1)
                                        dve.wait_ge(s_e, t * 5 + 4 + h)
                                    else:
                                        ins.then_inc(s_es, 1)

                            nc.vector.memset(mcol[:, :], 0.0).then_inc(s_id2, 1)
                            dve.wait_ge(s_id2, 1)
                            for h in range(HEADS):
                                for k in range(PARTS):
                                    at = h * P + h * KROWS + k
                                    last = nc.vector.memset(mcol[:, at:at + 1], 1.0)
                            last.then_inc(s_init, 1)
                            dve.wait_ge(s_init, 1)
                            dve.wait_ge(s_ebc, 16 * HEADS)
                            for t in range(2):
                                row_mask(t)
                                dve.wait_ge(s_mask, t * 2 + 2)
                                for k in range(Q):
                                    slot_free(t, k)
                                    row_piece(t, t, k)
                                max_parts(t, t)
                            block_mask(0, 0, 16)

                            def body(t, u, left):
                                for q in range(Q):
                                    pieces = {0: [], 1: [0], 2: [1, 2]}.get(q, [q]) if left == 2 else []
                                    for k in pieces:
                                        slot_free(t + 2, k)
                                    if q == 1 and left == 2:
                                        dve.wait_ge(s_mask, (t + 2) * 2 + 2)
                                    weigh(t, u, q)
                                    if q == 0 and not (isinstance(t, int) and t == 0):
                                        combine(t - 1, 1 - u)
                                    if q == 0 and left == 2:
                                        row_mask(t + 2)
                                    for k in pieces:
                                        row_piece(t + 2, u, k)
                                    if q == 6 and left:
                                        block_mask(t + 1, 1 - u, (t + 1 - (1 - u)) * 8 + 16)
                                    if q == Q - 1 and left == 2:
                                        max_parts(t + 2, u)
                                if not left:
                                    combine(t, u)
                            blocks(dve, body)

                    @block.tensor
                    def _(pe):
                        with only_if_signed(pe, False):
                            def exponents(t, u, q):
                                h, c = q // NCH, q % NCH
                                wait_from(pe, s_r, t * Q + q - 1)
                                if q == 0:
                                    pe.wait_ge(s_lt, (t + 1) * 2)
                                    pe.wait_ge(s_mrow, t + 1)
                                for b in range(CH // 512):
                                    bank = 2 * (q % 2) + b
                                    nc.tensor.matmul(ps[:, bank, :], identb[:, :],
                                                     maskT[u][:, c * CH + b * 512:c * CH + (b + 1) * 512],
                                                     start=True, stop=False, skip_group_check=True)
                                    for k in range(4):
                                        j = c * TPC + b * 4 + k
                                        last = nc.tensor.matmul(ps[:, bank, k * P:(k + 1) * P], prow[:, j * P:(j + 1) * P],
                                                                mrow[u][:, h * P:(h + 1) * P], start=False, stop=True,
                                                                skip_group_check=True)
                                last.then_inc(s_x, 1)

                            def weighted_sum(t, u, q):
                                h, c = q // NCH, q % NCH
                                pe.wait_ge(s_b, t * Q + q + 1)
                                if q == 0:
                                    wait_from(pe, s_es, t - 1)
                                for k in range(TPC):
                                    j = c * TPC + k
                                    last = nc.tensor.matmul(ps[:, 4 + u, h * D:(h + 1) * D],
                                                            wgt[q % WGT][:, k * P:(k + 1) * P],
                                                            hW[:, (j * HEADS + h) * D:(j * HEADS + h + 1) * D],
                                                            start=(j == 0), stop=(j == NT - 1))
                                last.then_inc(s_num, 1)

                            def turn_max(t):
                                pe.wait_ge(s_mcol, t + 1)
                                wait_from(pe, s_mrow, t)
                                for h in range(HEADS):
                                    last = nc.tensor.transpose(ps[:, 6, :].bitcast(BF16)[:, h * P:(h + 1) * P],
                                                               mcol[:, h * P:(h + 1) * P], identb[:, :])
                                last.then_inc(s_mtr, 1)

                            pe.wait_ge(s_init, 1)
                            turn_max(0)
                            exponents(0, 0, 0)
                            exponents(0, 0, 1)

                            def body(t, u, left):
                                for q in range(Q):
                                    if q + 2 < Q:
                                        exponents(t, u, q + 2)
                                    elif left:
                                        exponents(t + 1, 1 - u, q + 2 - Q)
                                    weighted_sum(t, u, q)
                                    if q == 3 and left:
                                        turn_max(t + 1)
                            blocks(pe, body)

                    @block.scalar
                    def _(act):
                        with only_if_signed(act, False):
                            def row_sum(t, u, k):
                                slot = k % SLOTS
                                act.wait_ge(s_nm, t * HEADS + k // NCH + 1)
                                piece = score[:, slot * CH:(slot + 1) * CH]
                                nc.scalar.activation(piece, piece, ACT.Exp, bias=nmax[u][:, k // NCH:k // NCH + 1],
                                                     accum_out=den[:, bass.ds(t * Q + k, 1)]).then_inc(s_den, 1)

                            def max_row(t, u):
                                act.wait_ge(s_mtr, t + 1)
                                nc.scalar.copy(mrow[u][:, :], ps[:, 6, :].bitcast(BF16)[:, 0:HEADS * P]).then_inc(s_mrow, 1)

                            def body(t, u, left):
                                for q in range(Q):
                                    act.wait_ge(s_x, t * Q + q + 1)
                                    wait_from(act, s_b, t * Q + q + 1 - EXPD)
                                    nc.scalar.activation(expd[q % EXPD][:, :], ps[:, 2 * (q % 2):2 * (q % 2) + 2, :]
                                                         .rearrange("p a c -> p (a c)"), ACT.Exp).then_inc(s_r, 1)
                                    if q < NCH:
                                        if left and not (isinstance(t, int) and t == 0):
                                            row_sum(t + 1, 1 - u, q + Q - NCH)
                                    elif left == 2:
                                        row_sum(t + 2, u, q - NCH)
                                    if q == 4 and left:
                                        max_row(t + 1, 1 - u)
                            for t in range(2):
                                for k in range(Q):
                                    row_sum(t, t, k)
                                if t == 0:
                                    max_row(0, 0)
                            blocks(act, body)


            with ExitStack() as cl:
                blk, row, pb, qb, score, wgt = [sb(f"signed_{k}", [P, N], c=cl) for k in (
                    "blk", "row", "p_row", "q_row", "score", "wgt")]
                dcol = sb("signed_dcol", [P, HEADS * NT], c=cl)
                ones = sb("signed_ones", [P, P], c=cl)
                mdiag = sb("signed_mdiag", [P, P], c=cl)
                nmax, den, iden = [sb(f"signed_{k}", [P, 1], c=cl) for k in ("nmax", "den", "iden")]
                es = sb("signed_es", [P, D], c=cl)
                s_adj, s_sc, s_v0, s_v, s_nm, s_dg, s_mb, s_den, s_w, s_ex, s_wt, s_num, s_es, s_out = [
                    sem(f"signed_{k}") for k in (
                        "adj_in", "scores_in", "constants", "steps", "negmax", "max_diag", "max_row",
                        "den", "exponent", "expd", "weighted", "summed", "es", "es_out")]
                PER = 2 + 13 * HEADS - 1

                def each_tile(eng, body, after=None):
                    with only_if_signed(eng, True):
                        body(0)
                        with eng.Fori(1, NT) as t:
                            body(t)
                        if after is not None:
                            after()

                with nc.Block() as block:
                    @block.sync
                    def _(sp):
                        def load(t):
                            wait_from(sp, s_wt, t * HEADS)
                            sp.dma_start(row[:, :], adj[bass.ts(t, P), :]).then_inc(s_adj, 16)
                            sp.dma_start(blk[:, :], adjT[t]).then_inc(s_adj, 16)
                            for h in range(HEADS):
                                wait_from(sp, s_w, t * HEADS + h)
                                sp.dma_start(pb[:, :], e_dram[h:h + 1, :].broadcast_to([P, N])).then_inc(s_sc, 16)
                                sp.dma_start(qb[:, :], e_dram[HEADS + h:HEADS + h + 1, :]
                                             .broadcast_to([P, N])).then_inc(s_sc, 16)
                        each_tile(sp, load)

                    @block.tensor
                    def _(pe):
                        def body(t):
                            for h in range(HEADS):
                                pe.wait_ge(s_dg, t * HEADS + h + 1)
                                nc.tensor.matmul(ps[:, 0, 0:P], ones[:, :], mdiag[:, :], start=True,
                                                 stop=True).then_inc(s_mb, 1)
                                pe.wait_ge(s_wt, t * HEADS + h + 1)
                                for j in range(NT):
                                    last = nc.tensor.matmul(ps[:, 1, 0:D], wgt[:, j * P:(j + 1) * P],
                                                            hW[:, (j * HEADS + h) * D:(j * HEADS + h + 1) * D],
                                                            start=(j == 0), stop=(j == NT - 1))
                                last.then_inc(s_num, 1)
                        each_tile(pe, body)

                    @block.scalar
                    def _(act):
                        def body(t):
                            for h in range(HEADS):
                                act.wait_ge(s_nm, t * HEADS + h + 1)
                                nc.scalar.activation(wgt[:, :], score[:, :], ACT.Exp, bias=nmax[:, 0:1],
                                                     accum_out=den[:, :]).then_inc(s_den, 1)
                                act.wait_ge(s_w, t * HEADS + h + 1)
                                nc.scalar.activation(score[:, :], score[:, :], ACT.Exp).then_inc(s_ex, 1)
                            act.wait_ge(s_es, t + 1)
                            act.dma_start(sup_dram[:, bass.ts(t, P)], es[:, :]).then_inc(s_out, 16)
                        each_tile(act, body, lambda: act.wait_ge(s_out, NT * 16))

                    @block.vector
                    def _(dve):
                        def body(t):
                            step = [0]

                            def link(ins):
                                step[0] += 1
                                ins.then_inc(s_v, 1)
                                dve.wait_ge(s_v, t * PER + step[0])

                            dve.wait_ge(s_adj, t * 32 + 32)
                            for m in (row, blk):
                                d = m[:, bass.ts(t, P)]
                                link(nc.vector.tensor_tensor(d, d, offdiag[:, :], ALU.mult))
                            s3, b3 = [m[:, :].rearrange("p (j i) -> p j i", i=P) for m in (score, blk)]
                            for h in range(HEADS):
                                dve.wait_ge(s_sc, (t * HEADS + h) * 32 + 32)
                                link(nc.vector.tensor_tensor(pb[:, :], pb[:, :], qb[:, :], ALU.subtract))
                                link(nc.vector.scalar_tensor_tensor(out=score[:, :], in0=row[:, :], scalar=0.0,
                                                                    in1=pb[:, :], op0=ALU.is_gt, op1=ALU.mult))
                                link(nc.vector.tensor_tensor(score[:, :], score[:, :], qb[:, :], ALU.add))
                                link(nc.vector.tensor_scalar(qb[:, :], row[:, :], 0.0, -BIG, ALU.is_equal, ALU.mult))
                                link(nc.vector.tensor_tensor(score[:, :], score[:, :], qb[:, :], ALU.add))
                                link(nc.vector.tensor_reduce(nmax[:, :], score[:, :], AX_X, ALU.max))
                                nc.vector.tensor_scalar(nmax[:, :], nmax[:, :], -BIG / 2, -1.0, ALU.max,
                                                        ALU.mult).then_inc(s_nm, 1)
                                dve.wait_ge(s_nm, t * HEADS + h + 1)
                                nc.vector.tensor_scalar(mdiag[:, :], ident[:, :], nmax[:, 0:1], None,
                                                        ALU.mult).then_inc(s_dg, 1)
                                dve.wait_ge(s_den, t * HEADS + h + 1)
                                dj = dcol[:, h * NT:(h + 1) * NT].rearrange("p (j a) -> p j a", a=1)
                                qj = esc[:, (HEADS + h) * NT:(HEADS + h + 1) * NT].rearrange("p (j a) -> p j a", a=1)
                                link(nc.vector.scalar_tensor_tensor(out=s3, in0=b3, scalar=0.0,
                                                                    in1=dj.broadcast_to([P, NT, P]), op0=ALU.is_gt,
                                                                    op1=ALU.mult))
                                link(nc.vector.tensor_tensor(s3, s3, qj.broadcast_to([P, NT, P]), ALU.add))
                                dve.wait_ge(s_mb, t * HEADS + h + 1)
                                link(nc.vector.tensor_tensor(s3, s3, ps[:, 0, 0:P].rearrange("p (a i) -> p a i", a=1)
                                                             .broadcast_to([P, NT, P]), ALU.add))
                                link(nc.vector.tensor_scalar(qb[:, :], blk[:, :], 0.0, -BIG, ALU.is_equal, ALU.mult))
                                nc.vector.tensor_tensor(score[:, :], score[:, :], qb[:, :], ALU.add).then_inc(s_w, 1)
                                dve.wait_ge(s_ex, t * HEADS + h + 1)
                                nc.vector.tensor_tensor(wgt[:, :], score[:, :], blk[:, :], ALU.mult).then_inc(s_wt, 1)
                                link(nc.vector.tensor_scalar(iden[:, :], den[:, :], 1e-30, float(HEADS), ALU.max,
                                                             ALU.mult))
                                link(nc.vector.reciprocal(iden[:, :], iden[:, :]))
                                dve.wait_ge(s_num, t * HEADS + h + 1)
                                if h == 0:
                                    wait_from(dve, s_out, t * 16)
                                    link(nc.vector.tensor_scalar(es[:, :], ps[:, 1, 0:D], iden[:, 0:1], None, ALU.mult))
                                    continue
                                ins = nc.vector.scalar_tensor_tensor(out=es[:, :], in0=ps[:, 1, 0:D],
                                                                     scalar=iden[:, 0:1], in1=es[:, :],
                                                                     op0=ALU.mult, op1=ALU.add)
                                if h < HEADS - 1:
                                    link(ins)
                                else:
                                    ins.then_inc(s_es, 1)
                            assert step[0] == PER, step[0]

                        nc.vector.memset(ones[:, :], 1.0).then_inc(s_v0, 1)
                        nc.vector.tensor_tensor(dcol[:, :], esc[:, 0:HEADS * NT], esc[:, HEADS * NT:], ALU.subtract)\
                            .then_inc(s_v0, 1)
                        dve.wait_ge(s_v0, 2)
                        each_tile(dve, body)

        with ExitStack() as c2:
            x = sb("x2", [P, N], c=c2)
            with ExitStack() as cg:
                x1, es, edge = [sb(f"node_{k}", [P, N], c=cg) for k in ("x1", "support", "edge")]
                own = gru_buffers(cg, "node")
                wih, whh = sb("node_wih", [P, 384], c=cg), sb("node_whh", [P, 384], c=cg)
                braw, bias = sb("node_braw", [P, 768], c=cg), sb("node_bias", [P, 512], c=cg)
                s_in, s_b, s_n, s_ta, s_fa = [sem(f"node_{k}") for k in ("in", "bias_ready", "norm", "root_in", "root_out")]
                pe_f, act_f, dve_f = gru(es, x1, edge, x, wih, whh, bias, diag, own, "node",
                                         after_dve=lambda dve: norm_dve(dve, Chain(dve, s_n), x, s_ta, s_fa))
                with nc.Block() as block:
                    @block.sync
                    def _(sp):
                        sp.dma_start(wih[:, :], t_in["node_WihT"]).then_inc(s_in, 16)
                        sp.dma_start(whh[:, :], t_in["node_WhhT"]).then_inc(s_in, 16)
                        sp.dma_start(braw[:, :], t_in["node_b"].broadcast_to([P, 768])).then_inc(s_in, 16)
                        sp.dma_start(x1[:, :], x_dram).then_inc(s_in, 16)
                        sp.dma_start(es[:, :], sup_dram).then_inc(s_in, 16)
                        sp.dma_start(edge[:, :], edge_dram).then_inc(s_in, 16)

                    @block.tensor
                    def _(pe):
                        pe.wait_ge(s_in, 96)
                        pe_f(pe)

                    @block.scalar
                    def _(act):
                        act_f(act)
                        root_act(act, s_ta, s_fa)

                    @block.vector
                    def _(dve):
                        dve.wait_ge(s_in, 96)
                        gru_bias(dve, Chain(dve, s_b), braw, bias)
                        dve_f(dve)

            if stop == 3:
                with nc.Block() as block:
                    @block.sync
                    def _(sp):
                        store_x(sp, x)
                return

            next_layer()
            with ExitStack() as cl:
                xhT = sb("xhT", [P, N], c=cl)
                XW = D + 1
                x1s = sb("x_ones", [P, NT * XW], c=cl)
                agg = sb("agg2", [P, N], c=cl)
                bs = sb("bscale", [P, 1], c=cl)
                w2, b2b = sb("w2", [P, D], c=cl), sb("bias2", [P, D], c=cl)
                blk = [sb(f"blk2_{i}", [P, N], c=cl) for i in range(RING)]
                tnh = [sb(f"tnh{i}", [P, CH], c=cl) for i in range(2)]
                expd = [sb(f"expd2_{i}", [P, CH], c=cl) for i in range(2)]
                wgt = [sb(f"wgt2_{i}", [P, CH], c=cl) for i in range(2)]
                rec = sb("rec", [P, 1], c=cl)
                s_w, s_c, s_ta, s_fa, s_xh, s_tr, s_ev = [sem(f"cos_{k}") for k in (
                    "w_in", "chain", "root_in", "root_out", "xhat", "tr", "ev")]
                with nc.Block() as block:
                    @block.sync
                    def _(sp):
                        sp.dma_start(w2[:, :], t_in["W2T"]).then_inc(s_w, 16)
                        sp.dma_start(b2b[:, :], t_in["bias2"].broadcast_to([P, D])).then_inc(s_w, 16)
                        sp.wait_ge(s_w, 32)

                    @block.vector
                    def _(dve):
                        link = Chain(dve, s_c)
                        for t in range(NT):
                            last = nc.vector.tensor_tensor_reduce(agg[:, t * P:(t + 1) * P], x[:, t * P:(t + 1) * P],
                                                                  x[:, t * P:(t + 1) * P], 1.0, 0.0, ALU.mult, ALU.add,
                                                                  rstd[:, t:t + 1])
                        link(last)
                        inverse_sqrt(dve, link, rstd[:, :], vc(4), vc(5), s_ta, s_fa)
                        for t in range(NT):
                            last = nc.vector.tensor_scalar(agg[:, t * P:(t + 1) * P], x[:, t * P:(t + 1) * P],
                                                           rstd[:, t:t + 1], None, ALU.mult)
                        last.then_inc(s_xh, 1)
                        link(nc.vector.memset(x1s[:, :], 1.0))
                        link(nc.vector.tensor_copy(x1s[:, :].rearrange("p (t c) -> p t c", c=XW)[:, :, 0:D],
                                                   x[:, :].rearrange("p (t c) -> p t c", c=D)))
                        link(nc.vector.tensor_scalar(bs[:, :], bval[:, :], 0.125, None, ALU.mult))

                    @block.tensor
                    def _(pe):
                        pe.wait_ge(s_xh, 1)
                        pe_transposes(pe, agg, s_tr, s_ev)

                    @block.scalar
                    def _(act):
                        root_act(act, s_ta, s_fa)
                        act_evacuates(act, xhT, s_tr, s_ev)

                s_blk = [sem(f"cos_blk_in{i}") for i in range(RING)]
                s_x, s_t, s_r, s_b, s_num, s_d, s_ag = [sem(f"cos_{k}") for k in (
                    "cosine", "tanh", "expd", "weighted", "summed", "recip", "agg")]
                Q = NCH

                def cos_tiles(eng, body):
                    for t in range(RING):
                        body(t, t, False)
                    with eng.Fori(1, NT // RING - 1) as r:
                        for u in range(RING):
                            body(r * RING + u, u, False)
                    for u in range(RING):
                        body(NT - RING + u, u, u == RING - 1)

                with nc.Block() as block:
                    @block.sync
                    def _(sp):
                        def load(t, u, last):
                            wait_from(sp, s_b, (t - RING + 1) * Q)
                            sp.dma_start(blk[u][:, :], adjT[t]).then_inc(s_blk[u], 16)
                        cos_tiles(sp, load)

                    @block.tensor
                    def _(pe):
                        def cosines(t, u, q):
                            wait_from(pe, s_t, t * Q + q - 1)
                            for k in range(TPC):
                                j = q * TPC + k
                                last = nc.tensor.matmul(ps[:, 2 * (q % 2) + k // 4, (k % 4) * P:(k % 4 + 1) * P],
                                                        xhT[:, j * P:(j + 1) * P], xhT[:, bass.ts(t, P)],
                                                        start=True, stop=True)
                            last.then_inc(s_x, 1)

                        def weighted_sum(t, u, q):
                            pe.wait_ge(s_b, t * Q + q + 1)
                            if q == 0:
                                wait_from(pe, s_ag, t - 1)
                            for k in range(TPC):
                                j = q * TPC + k
                                last = nc.tensor.matmul(ps[:, 4 + u % 2, 0:XW], wgt[q % 2][:, k * P:(k + 1) * P],
                                                        x1s[:, j * XW:(j + 1) * XW], start=(j == 0), stop=(j == NT - 1))
                            last.then_inc(s_num, 1)
                        cosines(0, 0, 0)
                        cosines(0, 0, 1)

                        def body(t, u, last):
                            for q in range(Q):
                                if q + 2 < Q:
                                    cosines(t, u, q + 2)
                                elif not last:
                                    cosines(t + 1, (u + 1) % RING, q + 2 - Q)
                                weighted_sum(t, u, q)
                        cos_tiles(pe, body)

                    @block.scalar
                    def _(act):
                        def tanh(t, q):
                            act.wait_ge(s_x, t * Q + q + 1)
                            wait_from(act, s_r, t * Q + q - 1)
                            nc.scalar.activation(tnh[q % 2][:, :], ps[:, 2 * (q % 2):2 * (q % 2) + 2, :]
                                                 .rearrange("p a c -> p (a c)"), ACT.Tanh,
                                                 scale=bs[:, 0:1]).then_inc(s_t, 1)
                        tanh(0, 0)

                        def body(t, u, last):
                            for q in range(Q):
                                if q + 1 < Q:
                                    tanh(t, q + 1)
                                elif not last:
                                    tanh(t + 1, 0)
                                act.wait_ge(s_t, t * Q + q + 1)
                                wait_from(act, s_b, t * Q + q - 1)
                                nc.scalar.activation(expd[q % 2][:, :], tnh[q % 2][:, :], ACT.Exp,
                                                     scale=8.0).then_inc(s_r, 1)
                        cos_tiles(act, body)

                    @block.vector
                    def _(dve):
                        def finish(t, u):
                            dve.wait_ge(s_num, (t + 1) * Q)
                            nc.vector.reciprocal(rec[:, :], ps[:, 4 + u % 2, D:D + 1]).then_inc(s_d, 1)
                            dve.wait_ge(s_d, t + 1)
                            nc.vector.tensor_scalar(agg[:, bass.ts(t, P)], ps[:, 4 + u % 2, 0:D], rec[:, 0:1], None,
                                                    ALU.mult).then_inc(s_ag, 1)

                        def body(t, u, last):
                            for q in range(Q):
                                if q == 0:
                                    dve.wait_ge(s_blk[u], (t - u) * (16 // RING) + 16)
                                dve.wait_ge(s_r, t * Q + q + 1)
                                wait_from(dve, s_num, t * Q + q - 1)
                                nc.vector.tensor_tensor(wgt[q % 2][:, :], expd[q % 2][:, :],
                                                        blk[u][:, q * CH:(q + 1) * CH], ALU.mult).then_inc(s_b, 1)
                                if q == 0 and not (isinstance(t, int) and t == 0):
                                    finish(t - 1, (u - 1) % RING)
                            if last:
                                finish(t, u)
                        cos_tiles(dve, body)

                s_tr, s_ev, s_l, s_y, s_c, s_n, s_ta, s_fa = [sem(f"lin_{k}") for k in (
                    "tr", "ev", "psum", "y", "stats", "norm", "root_in", "root_out")]
                with nc.Block() as block:
                    @block.tensor
                    def _(pe):
                        pe_transposes(pe, agg, s_tr, s_ev)
                        for q in range(NT // 4):
                            pe.wait_ge(s_ev, q + 1)
                            if q >= 2:
                                pe.wait_ge(s_y, 2 * (q - 1))
                            for k in range(4):
                                t = 4 * q + k
                                last = nc.tensor.matmul(ps[:, 2 + q % 2, k * P:(k + 1) * P], xhT[:, t * P:(t + 1) * P],
                                                        w2[:, :], start=True, stop=True)
                            last.then_inc(s_l, 1)

                    @block.scalar
                    def _(act):
                        act_evacuates(act, xhT, s_tr, s_ev)
                        root_act(act, s_ta, s_fa)

                    @block.vector
                    def _(dve):
                        for q in range(NT // 4):
                            dve.wait_ge(s_l, q + 1)
                            y4 = x[:, q * 512:(q + 1) * 512]
                            nc.vector.tensor_tensor(y4, y4, ps[:, 2 + q % 2, :], ALU.add).then_inc(s_y, 1)
                            dve.wait_ge(s_y, 2 * q + 1)
                            nc.vector.tensor_tensor(y4.rearrange("p (k c) -> p k c", c=D),
                                                    y4.rearrange("p (k c) -> p k c", c=D),
                                                    b2b[:, :].rearrange("p (a c) -> p a c", a=1).broadcast_to([P, 4, D]),
                                                    ALU.add).then_inc(s_y, 1)
                            dve.wait_ge(s_y, 2 * q + 2)
                            for k in range(4):
                                t = 4 * q + k
                                last = nc.vector.bn_stats(stats[:, 6 * t:6 * t + 6], x[:, t * P:(t + 1) * P])
                        last.then_inc(s_c, 1)
                        dve.wait_ge(s_c, 1)
                        norm_dve(dve, Chain(dve, s_n), x, s_ta, s_fa)

            if stop == 4:
                with nc.Block() as block:
                    @block.sync
                    def _(sp):
                        store_x(sp, x)
                return

            next_layer()
            with ExitStack() as cl:
                spec = sb("spec", [P, N], c=cl)
                coef = sb("coef", [P, NT], c=cl)
                teff = sb("teff", [P, 1], c=cl)
                ring = [sb(f"ring3_{i}", [P, N], c=cl) for i in range(RING)]
                s_c, s_co, s_coef = sem("heat_chain"), sem("heat_exponent"), sem("heat_coef")
                for half in range(2):
                    src, operand = (adjC, x) if half == 0 else (adjT, spec)
                    s_blk = [sem(f"heat{half}_blk_in{i}") for i in range(RING)]
                    s_sum, s_ev, s_st = [sem(f"heat{half}_{k}") for k in ("summed", "read", "stats")]
                    s_n, s_ta, s_fa, s_done = [sem(f"heat{half}_{k}") for k in ("norm", "root_in", "root_out", "done")]
                    with nc.Block() as block:
                        @block.sync
                        def _(sp):
                            def load(t, u, r):
                                wait_from(sp, s_sum, t - RING + 1)
                                sp.dma_start(ring[u][:, :], src[t]).then_inc(s_blk[u], 16)
                            tiles(sp, load, RING)
                            if half == 1:
                                sp.wait_ge(s_done, 1)
                                store_x(sp, x)

                        @block.tensor
                        def _(pe):
                            def product(t, u, r):
                                pe.wait_ge(s_blk[u], r * 16 + 16)
                                wait_from(pe, s_ev, t - 1)
                                for j in range(NT):
                                    last = nc.tensor.matmul(ps[:, u % 2, 0:D], ring[u][:, j * P:(j + 1) * P],
                                                            operand[:, j * P:(j + 1) * P], start=(j == 0),
                                                            stop=(j == NT - 1))
                                last.then_inc(s_sum, 1)
                            tiles(pe, product, RING)

                        @block.scalar
                        def _(act):
                            if half == 0:
                                act.wait_ge(s_co, 1)
                                nc.scalar.activation(coef[:, :], coef[:, :], ACT.Exp, scale=-1.0).then_inc(s_coef, 1)
                            else:
                                root_act(act, s_ta, s_fa)

                        @block.vector
                        def _(dve):
                            if half == 0:
                                link = Chain(dve, s_c)
                                link(nc.vector.tensor_scalar(teff[:, :], tval[:, :], 1e-8, None, ALU.max))
                                nc.vector.tensor_scalar(coef[:, :], evals[:, :], teff[:, 0:1], None,
                                                        ALU.mult).then_inc(s_co, 1)
                                dve.wait_ge(s_coef, 1)

                                def scale(t, u, r):
                                    dve.wait_ge(s_sum, t + 1)
                                    nc.vector.tensor_scalar(spec[:, bass.ts(t, P)], ps[:, u % 2, 0:D],
                                                            coef[:, bass.ds(t, 1)], None, ALU.mult).then_inc(s_ev, 1)
                                tiles(dve, scale, RING)
                            else:
                                def residual(t, u, r):
                                    dve.wait_ge(s_sum, t + 1)
                                    xt = x[:, bass.ts(t, P)]
                                    nc.vector.tensor_tensor(xt, xt, ps[:, u % 2, 0:D], ALU.add).then_inc(s_ev, 1)
                                    dve.wait_ge(s_ev, t + 1)
                                    nc.vector.bn_stats(stats[:, bass.ts(t, 6)], xt).then_inc(s_st, 1)
                                tiles(dve, residual, RING)
                                dve.wait_ge(s_st, NT)
                                norm_dve(dve, Chain(dve, s_n), x, s_ta, s_fa)
                                nc.vector.tensor_copy(col[:, 0:1], x[:, 0:1]).then_inc(s_done, 1)


def layouts(inp):
    import numpy as np
    adj = np.ascontiguousarray(inp["adj"])
    blk = adj.reshape(NT, P, NT, P)
    f = np.ascontiguousarray
    return {
        "x": f(inp["x"]),
        "adj": adj,
        "adjT_blk": f(blk.transpose(0, 3, 2, 1)).reshape(NT, P, N),
        "adj_cols": f(blk.transpose(2, 1, 0, 3)).reshape(NT, P, N),
        "diag": f(np.diagonal(adj).reshape(NT, P).T),
        "evals": f(inp["L3_gnn_evals"].reshape(NT, P).T),
        "t": f(inp["L3_gnn_t"].reshape(1, 1)),
        "b2": f(inp["L2_gnn_b"].reshape(1, 1)),
        "W0T": f(inp["L0_gnn_W"].T),
        "b0": f(inp["L0_gnn_b"].reshape(1, D)),
        "gat_W": f(inp["L1_gnn_gat_W"].transpose(1, 0, 2)).reshape(D, HEADS * D),
        "gat_WT": f(inp["L1_gnn_gat_W"].transpose(2, 0, 1)).reshape(D, HEADS * D),
        "gat_a": f(inp["L1_gnn_gat_a"].reshape(HEADS, 2, D).transpose(2, 0, 1)).reshape(D, 2 * HEADS),
        "edge_WihT": f(inp["L1_gnn_edge_Wih"].T),
        "edge_WhhT": f(inp["L1_gnn_edge_Whh"].T),
        "edge_b": f(np.concatenate([inp["L1_gnn_edge_bih"], inp["L1_gnn_edge_bhh"]]).reshape(1, 6 * D)),
        "node_WihT": f(inp["L1_gnn_node_Wih"].T),
        "node_WhhT": f(inp["L1_gnn_node_Whh"].T),
        "node_b": f(np.concatenate([inp["L1_gnn_node_bih"], inp["L1_gnn_node_bhh"]]).reshape(1, 6 * D)),
        "W2T": f(inp["L2_gnn_W"].T),
        "bias2": f(inp["L2_gnn_bias"].reshape(1, D)),
    }


def kernel(**inputs):
    import numpy as _np
    import concourse.bacc as _bacc
    from concourse import mybir as _mybir
    from concourse.bass_utils import run_bass_kernel_spmd as _run

    nc = _bacc.Bacc("TRN2", target_bir_lowering=False, num_devices=1,
                     dynamic_dma_scratch_size=1024)
    arrays, args = {}, {}
    for name, a in layouts({k: _np.asarray(v) for k, v in inputs.items()}).items():
        arrays[f"in_{name}_dram"] = a
        args[name] = nc.dram_tensor(f"in_{name}_dram", a.shape, _mybir.dt.from_np(a.dtype), kind="ExternalInput").ap()
    out = nc.dram_tensor("out_0_dram", (N, D), F32, kind="ExternalOutput").ap()
    build(nc, args, out, stop=STOP)
    r = _run(nc, [arrays], core_ids=[0])
    return r.results[0]["out_0_dram"]


STOP = 99
```

```python
from contextlib import ExitStack, contextmanager

import concourse.bass as bass
from concourse import mybir

ALU = mybir.AluOpType
ACT = mybir.ActivationFunctionType
F32 = mybir.dt.float32
BF16 = mybir.dt.bfloat16
I32 = mybir.dt.int32
AX_X = mybir.AxisListType.X

P = 128
N = 4096
D = 128
NT = N // P
HEADS = 3
RING = 4
LN_EPS = 1e-5
ALPHA = 0.2
BIG = float(2.0**100)
CH = 1024
TPC = CH // P
NCH = N // CH
PARTS = 3
KROWS = 2 * PARTS


def tiles(eng, body, unroll):
    for u in range(unroll):
        body(u, u, 0)
    with eng.Fori(1, NT // unroll) as r:
        for u in range(unroll):
            body(r * unroll + u, u, r)


def wait_from(eng, sem, value):
    if not isinstance(value, int) or value > 0:
        eng.wait_ge(sem, value)


class Chain:

    def __init__(self, eng, sem):
        self.eng, self.sem, self.n = eng, sem, 0

    def __call__(self, instruction):
        instruction.then_inc(self.sem, 1)
        self.n += 1
        self.eng.wait_ge(self.sem, self.n)


def build(nc, t_in, out):
    with ExitStack() as ctx:
        def sb(name, shape, dt=F32, c=ctx):
            return c.enter_context(nc.sbuf_tensor(name, shape, dt))

        live = []

        def sem(name):
            live.append(nc.alloc_semaphore(name=name))
            return live[-1]

        def next_layer():
            nc.clear_and_free_semaphores(live)
            live.clear()
            nc.all_engine_barrier()

        ps = ctx.enter_context(nc.psum_tensor("banks", [P, 8, 512], F32))

        ident = sb("ident", [P, P])
        identb = sb("identb", [P, P], BF16)
        offdiag = sb("offdiag", [P, P])
        stats = sb("stats", [P, NT * 6])
        moments = sb("moments", [P, NT * 2])
        col = sb("col", [P, 8 * NT])
        rstd = sb("rstd", [P, NT])
        diag = sb("diag", [P, NT])
        evals = sb("evals", [P, NT])
        tval = sb("tval", [P, 1])
        bval = sb("bval", [P, 1])

        x_dram = nc.dram_tensor("x_spill", [P, N], F32).ap()
        edge_dram = nc.dram_tensor("edge_spill", [P, N], F32).ap()
        sup_dram = nc.dram_tensor("support_spill", [P, N], F32).ap()
        e_dram = nc.dram_tensor("e_spill", [2 * HEADS, N], F32).ap()
        x_node = t_in["x"].rearrange("(t p) c -> p t c", p=P)
        out_node = out.rearrange("(t p) c -> p t c", p=P)
        adj, adjT, adjC = t_in["adj"], t_in["adjT_blk"], t_in["adj_cols"]

        def vc(k):
            return col[:, k * NT:(k + 1) * NT]

        def inverse_sqrt(dve, link, v, sq_in, sq_out, to_act, from_act):
            nc.vector.reciprocal(sq_in, v).then_inc(to_act, 1)
            dve.wait_ge(from_act, 1)
            tmp = vc(6)
            link(nc.vector.tensor_tensor(tmp, sq_out, sq_out, ALU.mult))
            link(nc.vector.tensor_tensor(tmp, tmp, v, ALU.mult))
            link(nc.vector.tensor_scalar(tmp, tmp, -0.5, 1.5, ALU.mult, ALU.add))
            link(nc.vector.tensor_tensor(v, tmp, sq_out, ALU.mult))

        def norm_dve(dve, link, y, to_act, from_act, scaled=None):
            for t in range(NT):
                last = nc.vector.bn_aggr(moments[:, 2 * t:2 * t + 2], stats[:, 6 * t:6 * t + 6])
            link(last)
            mean = moments[:, :].rearrange("p (t k) -> p k t", k=2)
            link(nc.vector.tensor_scalar(rstd[:, :], mean[:, 1, :], LN_EPS, None, ALU.add))
            inverse_sqrt(dve, link, rstd[:, :], vc(4), vc(5), to_act, from_act)
            link(nc.vector.tensor_tensor(vc(6), mean[:, 0, :], rstd[:, :], ALU.mult))
            nc.vector.tensor_scalar(vc(7), vc(6), -1.0, None, ALU.mult).then_inc(to_act, 1)
            for t in range(0, NT, 2):
                last = nc.vector.tensor_scalar(y[:, t * P:(t + 1) * P], y[:, t * P:(t + 1) * P],
                                               moments[:, 2 * t:2 * t + 1], rstd[:, t:t + 1],
                                               ALU.subtract, ALU.mult)
                if scaled is not None and t % (NT // 4) == NT // 4 - 2:
                    last.then_inc(scaled, 1)
            if scaled is None:
                link(last)

        def root_act(act, to_act, from_act):
            act.wait_ge(to_act, 1)
            nc.scalar.activation(vc(5), vc(4), ACT.Sqrt).then_inc(from_act, 1)

        def norm_act(act, y, to_act, from_act, scaled=None):
            root_act(act, to_act, from_act)
            act.wait_ge(to_act, 2)
            for t in range(1, NT, 2):
                last = nc.scalar.activation(y[:, t * P:(t + 1) * P], y[:, t * P:(t + 1) * P], ACT.Identity,
                                            scale=rstd[:, t:t + 1], bias=vc(7)[:, t:t + 1])
                if scaled is not None and t % (NT // 4) == NT // 4 - 1:
                    last.then_inc(scaled, 1)

        def pe_transposes(pe, src, s_tr, s_ev):
            for q in range(NT // 4):
                if q >= 2:
                    pe.wait_ge(s_ev, q - 1)
                for k in range(4):
                    t = 4 * q + k
                    last = nc.tensor.transpose(ps[:, q % 2, k * P:(k + 1) * P], src[:, t * P:(t + 1) * P],
                                               ident[:, :])
                last.then_inc(s_tr, 1)

        def act_evacuates(act, dst, s_tr, s_ev):
            for q in range(NT // 4):
                act.wait_ge(s_tr, q + 1)
                nc.scalar.copy(dst[:, q * 512:(q + 1) * 512], ps[:, q % 2, :]).then_inc(s_ev, 1)

        UC = 2 * HEADS * PARTS + 1
        UW = UC + 1
        c1, ca = ExitStack(), ExitStack()
        hW = sb("hW", [P, NT * HEADS * D], c=c1)
        ebc = sb("ebc", [P, HEADS * N], c=c1)
        prow = sb("prow", [P, N], BF16, c=c1)
        esc = sb("esc", [P, 2 * HEADS * NT], c=c1)
        flag = sb("flag", [P, 1], I32, c=c1)
        x = sb("x1", [P, N], c=ca)
        ns = sb("ns", [P, N], c=ca)
        with ExitStack() as c01:
            g = ns
            ring = [hW[:, i * N:(i + 1) * N] for i in range(HEADS)] + [ebc[:, 0:N]]
            xT = ebc[:, N:2 * N]
            rowsum = sb("rowsum", [P, NT], c=c01)
            rinv = sb("rinv", [P, NT], c=c01)
            with ExitStack() as c0:
                w = sb("w0", [P, D], c=c0)
                b = sb("b0", [P, D], c=c0)
                s_id0, s_id, s_w, s_x = sem("id_memset"), sem("id_ready"), sem("w0_in"), sem("x_in")
                s_row = [sem(f"row_in{i}") for i in range(RING)]
                s_rowused, s_tr, s_xT = sem("row_summed"), sem("xT_psum"), sem("xT_sbuf")
                s_h, s_hev = sem("h_psum"), sem("h_sbuf")
                s_c, s_ta, s_fa = sem("chain0"), sem("root0_in"), sem("root0_out")
                with nc.Block() as block:
                    @block.sync
                    def _(sp):
                        sp.dma_start(w[:, :], t_in["W0T"]).then_inc(s_w, 16)
                        sp.dma_start(b[:, :], t_in["b0"].broadcast_to([P, D])).then_inc(s_w, 16)
                        sp.dma_start(diag[:, :], t_in["diag"]).then_inc(s_w, 16)
                        sp.dma_start(evals[:, :], t_in["evals"]).then_inc(s_w, 16)
                        sp.dma_start(tval[:, :], t_in["t"].broadcast_to([P, 1])).then_inc(s_w, 16)
                        sp.dma_start(bval[:, :], t_in["b2"].broadcast_to([P, 1])).then_inc(s_w, 16)
                        sp.dma_start(x[:, :].rearrange("p (t c) -> p t c", c=P), x_node).then_inc(s_x, 16)

                        def load(t, u, r):
                            wait_from(sp, s_rowused, t - RING + 1)
                            sp.dma_start(ring[u][:, :], adj[bass.ts(t, P), :]).then_inc(s_row[u], 16)
                        tiles(sp, load, RING)

                    @block.gpsimd
                    def _(pool):
                        nc.gpsimd.memset(ident[:, :], 0.0).then_inc(s_id0, 1)
                        nc.gpsimd.memset(identb[:, :], 0.0).then_inc(s_id0, 1)
                        nc.gpsimd.memset(offdiag[:, :], 1.0).then_inc(s_id0, 1)
                        pool.wait_ge(s_id0, 3)
                        for m, fill in ((ident, 1.0), (identb, 1.0), (offdiag, 0.0)):
                            nc.gpsimd.affine_select(out=m[:, :], in_=m[:, :], compare_op=ALU.not_equal, fill=fill,
                                                    base=0, pattern=[[-1, P]], channel_multiplier=1).then_inc(s_id, 1)

                    @block.tensor
                    def _(pe):
                        pe.wait_ge(s_id, 3)
                        pe.wait_ge(s_x, 16)
                        pe.wait_ge(s_w, 96)
                        for q in range(NT // 4):
                            if q >= 2:
                                pe.wait_ge(s_xT, q - 1)
                            for k in range(4):
                                t = 4 * q + k
                                last = nc.tensor.transpose(ps[:, q % 2, k * P:(k + 1) * P], x[:, t * P:(t + 1) * P],
                                                           ident[:, :])
                            last.then_inc(s_tr, 1)
                        for q in range(NT // 4):
                            pe.wait_ge(s_xT, q + 1)
                            if q >= 2:
                                pe.wait_ge(s_hev, q - 1)
                            for k in range(4):
                                t = 4 * q + k
                                last = nc.tensor.matmul(ps[:, 2 + q % 2, k * P:(k + 1) * P],
                                                        xT[:, t * P:(t + 1) * P], w[:, :], start=True, stop=True)
                            last.then_inc(s_h, 1)

                    @block.scalar
                    def _(act):
                        for q in range(NT // 4):
                            act.wait_ge(s_tr, q + 1)
                            nc.scalar.copy(xT[:, q * 512:(q + 1) * 512], ps[:, q % 2, :]).then_inc(s_xT, 1)
                        root_act(act, s_ta, s_fa)

                    @block.vector
                    def _(dve):
                        dve.wait_ge(s_w, 96)
                        for q in range(NT // 4):
                            dve.wait_ge(s_h, q + 1)
                            nc.vector.tensor_tensor(
                                g[:, q * 512:(q + 1) * 512].rearrange("p (k c) -> p k c", c=D),
                                ps[:, 2 + q % 2, :].rearrange("p (k c) -> p k c", c=D),
                                b[:, :].rearrange("p (a c) -> p a c", a=1).broadcast_to([P, 4, D]),
                                ALU.add).then_inc(s_hev, 1)

                        def row_sum(t, u, r):
                            dve.wait_ge(s_row[u], r * 16 + 16)
                            nc.vector.tensor_reduce(rowsum[:, bass.ds(t, 1)], ring[u][:, :], AX_X,
                                                    ALU.add).then_inc(s_rowused, 1)
                        tiles(dve, row_sum, RING)
                        dve.wait_ge(s_rowused, NT)
                        dve.wait_ge(s_hev, NT // 4)
                        link = Chain(dve, s_c)
                        link(nc.vector.tensor_scalar(rinv[:, :], rowsum[:, :], 1.0, None, ALU.add))
                        link(nc.vector.tensor_scalar(vc(0), rinv[:, :], 0.0, None, ALU.is_equal))
                        link(nc.vector.tensor_tensor(rinv[:, :], rinv[:, :], vc(0), ALU.add))
                        inverse_sqrt(dve, link, rinv[:, :], vc(4), vc(5), s_ta, s_fa)
                        link(nc.vector.tensor_scalar(vc(0), vc(0), -1.0, 1.0, ALU.mult, ALU.add))
                        link(nc.vector.tensor_tensor(rinv[:, :], rinv[:, :], vc(0), ALU.mult))
                        for t in range(NT):
                            last = nc.vector.tensor_scalar(g[:, t * P:(t + 1) * P], g[:, t * P:(t + 1) * P],
                                                           rinv[:, t:t + 1], None, ALU.mult)
                        link(last)

            s_blk = [sem(f"blk0_in{i}") for i in range(RING)]
            s_agg, s_ev, s_c = sem("agg0_psum"), sem("agg0_read"), sem("chain0b")
            s_c2, s_ta, s_fa = sem("chain0c"), sem("root0b_in"), sem("root0b_out")
            with nc.Block() as block:
                @block.sync
                def _(sp):
                    def load(t, u, r):
                        wait_from(sp, s_agg, t - RING + 1)
                        sp.dma_start(ring[u][:, :], adjT[t]).then_inc(s_blk[u], 16)
                    tiles(sp, load, RING)

                @block.tensor
                def _(pe):
                    def aggregate(t, u, r):
                        pe.wait_ge(s_blk[u], r * 16 + 16)
                        wait_from(pe, s_ev, t - 1)
                        for j in range(NT):
                            last = nc.tensor.matmul(ps[:, u % 2, 0:D], ring[u][:, j * P:(j + 1) * P],
                                                    g[:, j * P:(j + 1) * P], start=(j == 0), stop=(j == NT - 1))
                        last.then_inc(s_agg, 1)
                    tiles(pe, aggregate, RING)

                @block.scalar
                def _(act):
                    norm_act(act, x, s_ta, s_fa)

                @block.vector
                def _(dve):
                    tmp = col[:, 0:P]

                    def residual(t, u, r):
                        dve.wait_ge(s_agg, t + 1)
                        nc.vector.tensor_tensor(tmp, ps[:, u % 2, 0:D], g[:, bass.ts(t, P)],
                                                ALU.add).then_inc(s_ev, 1)
                        dve.wait_ge(s_ev, t + 1)
                        nc.vector.scalar_tensor_tensor(out=x[:, bass.ts(t, P)], in0=tmp, scalar=rinv[:, bass.ds(t, 1)],
                                                       in1=x[:, bass.ts(t, P)], op0=ALU.mult,
                                                       op1=ALU.add).then_inc(s_c, 1)
                        dve.wait_ge(s_c, t + 1)
                        nc.vector.bn_stats(stats[:, bass.ts(t, 6)], x[:, bass.ts(t, P)]).then_inc(s_c2, 1)
                    tiles(dve, residual, RING)
                    dve.wait_ge(s_c2, NT)
                    link = Chain(dve, sem("chain0d"))
                    norm_dve(dve, link, x, s_ta, s_fa)

        next_layer()
        def gru(src, x, base, dst, wih, whh, bias, scale, own, steps, after_dve=None, arrived=None):
            srcT, xT, pre, rz, cand, diff = own
            s_tr, s_tev, s_gate, s_pre, s_rz, s_nin, s_n, s_c = [sem(f"gru_{steps}_{k}") for k in (
                "transposed", "transposed_sbuf", "gates", "pre", "rz", "cand_in", "cand", "chain")]
            GROUPS, STEPS = NT // 4, 7

            def groups(eng, body):
                body(0, 0, True)
                body(1, 1, True)
                with eng.Fori(1, GROUPS // 2 - 1) as r:
                    body(r * 2, 0, True)
                    body(r * 2 + 1, 1, True)
                body(GROUPS - 2, 0, True)
                body(GROUPS - 1, 1, False)

            def on_pe(pe):
                def transposes(q):
                    if arrived is not None:
                        pe.wait_ge(arrived[q], 48)
                    wait_from(pe, s_tev, q)
                    for k in range(4):
                        c = slice((4 * q + k) * P, (4 * q + k + 1) * P)
                        nc.tensor.transpose(ps[:, 0, k * P:(k + 1) * P], src[:, c], ident[:, :])
                        last = nc.tensor.transpose(ps[:, 1, k * P:(k + 1) * P], x[:, c], ident[:, :])
                    last.then_inc(s_tr, 1)

                def gates(q):
                    pe.wait_ge(s_tev, q + 1)
                    for k in range(4):
                        if k % 2 == 0:
                            wait_from(pe, s_pre, 2 * q - 1 + k // 2)
                        c = slice(k * P, (k + 1) * P)
                        nc.tensor.matmul(ps[:, 2 + k, 0:256], srcT[q % 2][:, c], wih[:, 0:256], start=True, stop=False)
                        nc.tensor.matmul(ps[:, 2 + k, 0:256], xT[q % 2][:, c], whh[:, 0:256], start=False, stop=True)
                        nc.tensor.matmul(ps[:, 2 + k, 256:384], srcT[q % 2][:, c], wih[:, 256:384], start=False,
                                         stop=True, skip_group_check=True)
                        last = nc.tensor.matmul(ps[:, 2 + k, 384:512], xT[q % 2][:, c], whh[:, 256:384], start=False,
                                                stop=True, skip_group_check=True)
                        if k % 2:
                            last.then_inc(s_gate, 1)

                transposes(0)
                for q in range(GROUPS):
                    if q + 1 < GROUPS:
                        transposes(q + 1)
                    gates(q)

            def on_act(act):
                def evacuate(q, u):
                    act.wait_ge(s_tr, q + 1)
                    wait_from(act, s_gate, 2 * q - 2)
                    nc.scalar.copy(srcT[u][:, :], ps[:, 0, :])
                    nc.scalar.copy(xT[u][:, :], ps[:, 1, :]).then_inc(s_tev, 1)

                def body(q, u, more):
                    if more:
                        evacuate(q + 1, 1 - u)
                    act.wait_ge(s_pre, 2 * q + 2)
                    nc.scalar.activation(by_tile(rz[u], 256), by_tile(pre[u], 512)[:, :, 0:256], ACT.Tanh,
                                         scale=0.5).then_inc(s_rz, 1)
                    act.wait_ge(s_nin, q + 1)
                    nc.scalar.activation(cand[:, :], cand[:, :], ACT.Tanh).then_inc(s_n, 1)
                evacuate(0, 0)
                groups(act, body)

            def by_tile(a, width):
                return a[:, :].rearrange("p (k c) -> p k c", c=width)

            def on_dve(dve):
                def add_bias(q, u):
                    for half in range(2):
                        dve.wait_ge(s_gate, 2 * q + half + 1)
                        nc.vector.tensor_tensor(by_tile(pre[u], 512)[:, 2 * half:2 * half + 2, :],
                                                ps[:, 2 + 2 * half:4 + 2 * half, :],
                                                bias[:, :].rearrange("p (a c) -> p a c", a=1).broadcast_to([P, 2, 512]),
                                                ALU.add).then_inc(s_pre, 1)

                def body(q, u, more):
                    pre3, rz3, cand3, diff3 = by_tile(pre[u], 512), by_tile(rz[u], 256), by_tile(cand, P), by_tile(diff, P)
                    dve.wait_ge(s_pre, 2 * q + 2)
                    dve.wait_ge(s_rz, q + 1)
                    step = [0]

                    def link(ins):
                        step[0] += 1
                        ins.then_inc(s_c, 1)
                        dve.wait_ge(s_c, q * STEPS + step[0])
                    link(nc.vector.tensor_scalar(rz[u][:, :], rz[u][:, :], 0.5, 0.5, ALU.mult, ALU.add))
                    link(nc.vector.tensor_tensor(cand3, rz3[:, :, 0:P], pre3[:, :, 384:512], ALU.mult))
                    nc.vector.tensor_tensor(cand3, cand3, pre3[:, :, 256:384], ALU.add).then_inc(s_nin, 1)
                    if more:
                        add_bias(q + 1, 1 - u)
                    dve.wait_ge(s_n, q + 1)
                    x4 = x[:, bass.ts(q, 512)].rearrange("p (k c) -> p k c", c=P)
                    link(nc.vector.tensor_tensor(diff3, x4, cand3, ALU.subtract))
                    link(nc.vector.tensor_tensor(diff3, diff3, rz3[:, :, P:256], ALU.mult))
                    link(nc.vector.tensor_tensor(diff3, diff3, cand3, ALU.add))
                    for k in range(4):
                        t = q * 4 + k
                        last = nc.vector.scalar_tensor_tensor(
                            out=dst[:, bass.ts(t, P)], in0=diff[:, k * P:(k + 1) * P], scalar=scale[:, bass.ds(t, 1)],
                            in1=base[:, bass.ts(t, P)], op0=ALU.mult, op1=ALU.add)
                    link(last)
                    if after_dve is not None:
                        for k in range(4):
                            last = nc.vector.bn_stats(stats[:, bass.ts(q * 4 + k, 6)], dst[:, bass.ts(q * 4 + k, P)])
                        last.then_inc(s_c, 1)
                    else:
                        nc.vector.tensor_copy(col[:, 0:1], diff[:, 0:1]).then_inc(s_c, 1)
                add_bias(0, 0)
                groups(dve, body)
                dve.wait_ge(s_c, STEPS * GROUPS)
                if after_dve is not None:
                    after_dve(dve)

            return s_c, on_pe, on_act, on_dve

        def gru_buffers(c, which):
            pairs = [[sb(f"{which}_{k}{i}", [P, n], c=c) for i in range(2)] for k, n in (
                ("srcT", 512), ("xT", 512), ("pre", 2048), ("rz", 1024))]
            return pairs + [sb(f"{which}_{k}", [P, 512], c=c) for k in ("cand", "diff")]

        def gru_bias(dve, link, braw, bias):
            link(nc.vector.tensor_tensor(bias[:, 0:256], braw[:, 0:256], braw[:, 384:640], ALU.add))
            link(nc.vector.tensor_copy(bias[:, 256:384], braw[:, 256:384]))
            link(nc.vector.tensor_copy(bias[:, 384:512], braw[:, 640:768]))

        with c1:
            with ca:
                usplit = sb("usplit", [P, NT * UW], BF16, c=ca)
                usp3 = usplit[:, :].rearrange("p (t k) -> p t k", k=UW)
                R1 = 2
                cl = ExitStack()
                ring = [sb(f"ring1_{i}", [P, N], c=cl) for i in range(R1)]
                s_blk = [sem(f"blk1_in{i}") for i in range(R1)]
                with ExitStack() as cp:
                    xT = sb("x1T", [P, N], c=cp)
                    gW = sb("gW", [P, HEADS * D], c=cp)
                    gWT = sb("gWT", [P, HEADS * D], c=cp)
                    ga = sb("ga", [P, 2 * HEADS], c=cp)
                    va = sb("va", [P, 2 * HEADS], c=cp)
                    u = sb("u", [P, NT * 2 * HEADS], c=cp)
                    s_in, s_tr, s_ev, s_va, s_vac, s_u, s_hw, s_hwe, s_c = [sem(f"proj_{k}") for k in (
                        "in", "tr", "ev", "va", "vac", "u", "hw", "hwe", "chain")]
                    with nc.Block() as block:
                        @block.sync
                        def _(sp):
                            sp.dma_start(gW[:, :], t_in["gat_W"]).then_inc(s_in, 16)
                            sp.dma_start(gWT[:, :], t_in["gat_WT"]).then_inc(s_in, 16)
                            sp.dma_start(ga[:, :], t_in["gat_a"]).then_inc(s_in, 16)
                            for i in range(R1):
                                sp.dma_start(ring[i][:, :], adjT[i]).then_inc(s_blk[i], 16)
                            x_kept = sem("x1_kept")
                            sp.dma_start(x_dram, x[:, :]).then_inc(x_kept, 16)
                            sp.wait_ge(x_kept, 16)

                        @block.tensor
                        def _(pe):
                            pe.wait_ge(s_in, 48)
                            for h in range(HEADS):
                                last = nc.tensor.matmul(ps[:, 7, 2 * h:2 * h + 2], gWT[:, h * D:(h + 1) * D],
                                                        ga[:, 2 * h:2 * h + 2], start=True, stop=True)
                            last.then_inc(s_va, 1)
                            pe_transposes(pe, x, s_tr, s_ev)
                            pe.wait_ge(s_ev, NT // 4)
                            pe.wait_ge(s_vac, 1)
                            for t in range(NT):
                                last = nc.tensor.matmul(ps[:, 6, t * 6:t * 6 + 6], xT[:, t * P:(t + 1) * P], va[:, :],
                                                        start=True, stop=True)
                            last.then_inc(s_u, 1)
                            for t in range(NT):
                                if t >= 4:
                                    pe.wait_ge(s_hwe, t - 3)
                                nc.tensor.matmul(ps[:, 2 + t % 4, 0:HEADS * D], xT[:, t * P:(t + 1) * P], gW[:, :],
                                                 start=True, stop=True).then_inc(s_hw, 1)

                        @block.scalar
                        def _(act):
                            act_evacuates(act, xT, s_tr, s_ev)
                            for t in range(NT):
                                act.wait_ge(s_hw, t + 1)
                                nc.scalar.copy(hW[:, t * 384:(t + 1) * 384], ps[:, 2 + t % 4, 0:384]).then_inc(s_hwe, 1)

                        @block.vector
                        def _(dve):
                            link = Chain(dve, s_c)
                            dve.wait_ge(s_va, 1)
                            nc.vector.tensor_copy(va[:, :], ps[:, 7, 0:6]).then_inc(s_vac, 1)
                            nc.vector.memset(usplit[:, :], 1.0).then_inc(s_c, 1)
                            link.n += 1
                            dve.wait_ge(s_c, link.n)
                            dve.wait_ge(s_u, 1)
                            link(nc.vector.tensor_copy(u[:, :], ps[:, 6, 0:NT * 6]))
                            u3 = u[:, :].rearrange("p (t k) -> p t k", k=6)
                            for k in range(PARTS):
                                part = usp3[:, :, 6 * k:6 * k + 6]
                                link(nc.vector.tensor_copy(part, u3))
                                if k < PARTS - 1:
                                    link(nc.vector.tensor_tensor(u3, u3, part, ALU.subtract))

                with cl:
                    pos = [sb(f"pos{i}", [P, N], BF16, c=cl) for i in range(2)]
                    neg = [sb(f"neg{i}", [P, N], BF16, c=cl) for i in range(2)]
                    raw = sb("raw", [P, NT * 2 * UC], c=cl)
                    s_dz, s_pos, s_neg, s_ns, s_pn, s_rd = [sem(f"sums_{k}") for k in (
                        "diag_cleared", "positive", "negative", "ns_psum", "pn_psum", "read")]
                    with nc.Block() as block:
                        @block.sync
                        def _(sp):
                            def load(t, u, r):
                                if isinstance(t, int):
                                    return
                                sp.wait_ge(s_ns, t - R1 + 1)
                                sp.wait_ge(s_neg, t - R1 + 1)
                                sp.dma_start(ring[u][:, :], adjT[t]).then_inc(s_blk[u], 16)
                            tiles(sp, load, R1)

                        @block.vector
                        def _(dve):
                            def masks(t, u, r):
                                dve.wait_ge(s_blk[u], r * 16 + 16)
                                d = ring[u][:, bass.ts(t, P)]
                                nc.vector.tensor_tensor(d, d, offdiag[:, :], ALU.mult).then_inc(s_dz, 1)
                                dve.wait_ge(s_dz, t + 1)
                                wait_from(dve, s_pn, t - 1)
                                nc.vector.tensor_scalar(pos[u][:, :], ring[u][:, :], 0.0, None,
                                                        ALU.is_gt).then_inc(s_pos, 1)
                                nc.vector.tensor_scalar(neg[u][:, :], ring[u][:, :], 0.0, None,
                                                        ALU.is_lt).then_inc(s_neg, 1)
                            tiles(dve, masks, R1)

                        @block.tensor
                        def _(pe):
                            def sums(t, u, r):
                                pe.wait_ge(s_blk[u], r * 16 + 16)
                                pe.wait_ge(s_dz, t + 1)
                                wait_from(pe, s_rd, t - 1)
                                for j in range(NT):
                                    last = nc.tensor.matmul(ps[:, u, 0:D], ring[u][:, j * P:(j + 1) * P],
                                                            x[:, j * P:(j + 1) * P], start=(j == 0), stop=(j == NT - 1))
                                last.then_inc(s_ns, 1)
                                for m, (mask, ready) in enumerate(((pos[u], s_pos), (neg[u], s_neg))):
                                    pe.wait_ge(ready, t + 1)
                                    for j in range(NT):
                                        last = nc.tensor.matmul(ps[:, 2 + u, m * UC:(m + 1) * UC],
                                                                mask[:, j * P:(j + 1) * P],
                                                                usplit[:, j * UW:j * UW + UC],
                                                                start=(j == 0), stop=(j == NT - 1))
                                last.then_inc(s_pn, 1)
                            tiles(pe, sums, R1)

                        @block.scalar
                        def _(act):
                            def keep(t, u, r):
                                act.wait_ge(s_ns, t + 1)
                                nc.scalar.copy(ns[:, bass.ts(t, P)], ps[:, u, 0:D])
                                act.wait_ge(s_pn, t + 1)
                                nc.scalar.copy(raw[:, bass.ts(t, 2 * UC)], ps[:, 2 + u, 0:2 * UC]).then_inc(s_rd, 1)
                            tiles(act, keep, R1)

                    s_c, s_any, s_anyc, s_e, s_ec, s_row, s_wr, s_pm, s_pt, s_pe_, s_z = [sem(f"score_{k}") for k in (
                        "chain", "any", "any_sbuf", "e", "e_rows", "rowT", "written", "pcol", "ptr", "prow", "z")]
                    sm = sb("score_parts", [P, NT * 12], c=cl)
                    cnt = sb("cnt", [P, 1], c=cl)
                    onec = sb("onec", [P, 1], c=cl)
                    pcol = sb("pcol", [P, N], BF16, c=cl)
                    rem = sb("rem", [P, HEADS * NT], c=cl)
                    with nc.Block() as block:
                        @block.vector
                        def _(dve):
                            link = Chain(dve, s_c)
                            r4 = raw[:, :].rearrange("p (t m k) -> p t m k", m=2, k=UC)
                            s4 = sm[:, :].rearrange("p (t m k) -> p t m k", m=2, k=6)
                            link(nc.vector.tensor_reduce(cnt[:, :], r4[:, :, 1, UC - 1], AX_X, ALU.max))
                            nc.vector.memset(onec[:, :], 1.0).then_inc(s_any, 1)
                            for m in range(2):
                                link(nc.vector.tensor_tensor(s4[:, :, m, :], r4[:, :, m, 12:18], r4[:, :, m, 6:12], ALU.add))
                                link(nc.vector.tensor_tensor(s4[:, :, m, :], s4[:, :, m, :], r4[:, :, m, 0:6], ALU.add))
                            e4 = esc[:, :].rearrange("p (s h t) -> p s h t", s=2, h=HEADS)
                            for h in range(HEADS):
                                for s in range(2):
                                    link(nc.vector.tensor_tensor(e4[:, s, h, :], s4[:, :, s, 2 * h],
                                                                 s4[:, :, 1 - s, 2 * h + 1], ALU.add))
                            link(nc.vector.tensor_scalar(sm[:, 0:192], esc[:, :], ALPHA, None, ALU.mult))
                            link(nc.vector.tensor_tensor(esc[:, :], esc[:, :], sm[:, 0:192], ALU.max))
                            link(nc.vector.memset(pcol[:, :], 0.0))
                            p3 = pcol[:, :].rearrange("p (t k) -> p t k", k=P)
                            link(nc.vector.tensor_copy(rem[:, :], esc[:, 0:HEADS * NT]))
                            for k in range(PARTS):
                                for h in range(HEADS):
                                    link(nc.vector.tensor_copy(p3[:, :, KROWS * h + k], rem[:, h * NT:(h + 1) * NT]))
                                    link(nc.vector.memset(p3[:, :, KROWS * h + PARTS + k], 1.0))
                                    if k < PARTS - 1:
                                        link(nc.vector.tensor_tensor(rem[:, h * NT:(h + 1) * NT],
                                                                     rem[:, h * NT:(h + 1) * NT],
                                                                     p3[:, :, KROWS * h + k], ALU.subtract))
                            nc.vector.tensor_copy(cnt[:, :], cnt[:, :]).then_inc(s_e, 1)
                            dve.wait_ge(s_anyc, 1)
                            nc.vector.tensor_scalar(flag[0:1, :], ps[0:1, 7, 0:1], 1.0, None, ALU.min).then_inc(s_z, 1)

                        @block.tensor
                        def _(pe):
                            pe.wait_ge(s_any, 1)
                            pe.wait_ge(s_e, 1)
                            nc.tensor.matmul(ps[0:1, 7, 0:1], cnt[:, :], onec[:, :], start=True, stop=True)\
                                .then_inc(s_anyc, 1)
                            nc.tensor.transpose(ps[0:HEADS * NT, 6, 0:P], esc[:, 0:HEADS * NT], ident[:, :])
                            nc.tensor.transpose(ps[0:HEADS * NT, 6, P:2 * P], esc[:, HEADS * NT:], ident[:, :])\
                                .then_inc(s_row, 1)
                            for q in range(NT // 4):
                                if q >= 2:
                                    pe.wait_ge(s_pe_, q - 1)
                                for k in range(4):
                                    t = 4 * q + k
                                    last = nc.tensor.transpose(
                                        ps[:, q % 2, :].bitcast(BF16)[:, k * P:(k + 1) * P], pcol[:, t * P:(t + 1) * P],
                                        identb[:, :])
                                last.then_inc(s_pt, 1)

                        @block.scalar
                        def _(act):
                            act.wait_ge(s_row, 1)
                            eT2 = sb("eT2", [P, 2 * P], c=cl)
                            nc.scalar.copy(eT2[0:HEADS * NT, :], ps[0:HEADS * NT, 6, 0:2 * P]).then_inc(s_ec, 1)
                            act.wait_ge(s_ec, 1)
                            for s in range(2):
                                act.dma_start(e_dram[s * HEADS:(s + 1) * HEADS, :].rearrange("h (t p) -> (h t) p", p=P),
                                              eT2[0:HEADS * NT, s * P:(s + 1) * P]).then_inc(s_wr, 16)
                            for q in range(NT // 4):
                                act.wait_ge(s_pt, q + 1)
                                nc.scalar.copy(prow[:, q * 512:(q + 1) * 512],
                                               ps[:, q % 2, :].bitcast(BF16)[:, 0:512]).then_inc(s_pe_, 1)
                            act.wait_ge(s_wr, 32)

                with ExitStack() as cg:
                    own = gru_buffers(cg, "edge")
                    wih, whh = sb("edge_wih", [P, 384], c=cg), sb("edge_whh", [P, 384], c=cg)
                    braw, bias = sb("edge_braw", [P, 768], c=cg), sb("edge_bias", [P, 512], c=cg)
                    s_in, s_b, s_dn = sem("edge_in"), sem("edge_bias_ready"), sem("edge_out")
                    s_fin, pe_f, act_f, dve_f = gru(ns, x, x, ns, wih, whh, bias, diag, own, "edge")
                    with nc.Block() as block:
                        @block.sync
                        def _(sp):
                            sp.dma_start(wih[:, :], t_in["edge_WihT"]).then_inc(s_in, 16)
                            sp.dma_start(whh[:, :], t_in["edge_WhhT"]).then_inc(s_in, 16)
                            sp.dma_start(braw[:, :], t_in["edge_b"].broadcast_to([P, 768])).then_inc(s_in, 16)
                            s_ebc = sem("e_rows_in")
                            for h in range(HEADS):
                                sp.dma_start(ebc[:, h * N:(h + 1) * N],
                                             e_dram[h:h + 1, :].broadcast_to([P, N])).then_inc(s_ebc, 16)
                            for q in range(NT // 4):
                                sp.wait_ge(s_fin, 7 * (q + 1))
                                sp.dma_start(edge_dram[:, q * 512:(q + 1) * 512],
                                             ns[:, q * 512:(q + 1) * 512]).then_inc(s_dn, 16)
                            sp.wait_ge(s_ebc, 16 * HEADS)
                            sp.wait_ge(s_dn, 16 * NT // 4)

                        @block.tensor
                        def _(pe):
                            pe.wait_ge(s_in, 48)
                            pe_f(pe)

                        @block.scalar
                        def _(act):
                            act_f(act)

                        @block.vector
                        def _(dve):
                            dve.wait_ge(s_in, 48)
                            gru_bias(dve, Chain(dve, s_b), braw, bias)
                            dve_f(dve)

            @contextmanager
            def only_if_signed(eng, signed):
                found = eng.alloc_register(f"negative_weights_{int(signed)}")
                eng.load(found, flag[0:1, 0:1])
                with eng.If_eq(found, int(signed)):
                    yield

            SLOTS, EXPD, WGT, LAG = 6, 3, 3, 5
            with ExitStack() as cl:
                blk = [sb(f"at{i}", [P, N], c=cl) for i in range(2)]
                row = sb("row", [P, N], c=cl)
                score = sb("score", [P, SLOTS * CH], c=cl)
                maskT = [sb(f"maskT{i}", [P, N], BF16, c=cl) for i in range(2)]
                expd = [sb(f"expd{i}", [P, CH], c=cl) for i in range(EXPD)]
                wgt = [sb(f"wgt{i}", [P, CH], c=cl) for i in range(WGT)]
                mcol = sb("mcol", [P, HEADS * P], BF16, c=cl)
                mrow = [sb(f"mrow{i}", [P, HEADS * P], BF16, c=cl) for i in range(2)]
                Q = HEADS * NCH
                es = [col[:, i * D:(i + 1) * D] for i in range(2)]
                den = [stats[:, i * Q:(i + 1) * Q] for i in range(2)]
                mx = stats[:, 2 * Q:3 * Q]
                nmax = [stats[:, 3 * Q + i * HEADS:3 * Q + (i + 1) * HEADS] for i in range(2)]
                iden = [stats[:, 3 * Q + (2 + i) * HEADS:3 * Q + (3 + i) * HEADS] for i in range(2)]
                nbig = moments[:, :].bitcast(BF16)
                nrem = stats[:, 3 * Q + 4 * HEADS:3 * Q + 5 * HEADS]
                s_row, s_mask, s_top, s_top1, s_nm, s_den = [sem(f"gat_{k}") for k in (
                    "row_in", "mask_steps", "max", "head_max", "negmax", "den")]
                s_blk = [sem(f"gat_blk_in{i}") for i in range(2)]
                s_part, s_mcol, s_mtr, s_mrow, s_lt, s_x, s_r, s_b, s_num = [sem(f"gat_{k}") for k in (
                    "part_steps", "mcol", "mcol_T", "mrow", "mask", "exponent", "expd", "weighted", "summed")]
                s_e, s_es = sem("gat_es_steps"), sem("gat_es")
                s_eout = [sem(f"gat_es_out{i}") for i in range(2)]
                s_dz, s_rz, s_inv = sem("gat_diag_cleared"), sem("gat_row_diag_cleared"), sem("gat_inverse_steps")
                s_id2, s_init = sem("gat_init"), sem("gat_mcol_init")

                def blocks(eng, body, start=0):
                    for t in range(start, 2):
                        body(t, t, 2)
                    with eng.Fori(1, NT // 2 - 1) as r:
                        body(r * 2, 0, 2)
                        body(r * 2 + 1, 1, 2)
                    body(NT - 2, 0, 1)
                    body(NT - 1, 1, 0)

                with nc.Block() as block:
                    @block.sync
                    def _(sp):
                        with only_if_signed(sp, False):
                            def rows(t):
                                for c in range(NCH):
                                    wait_from(sp, s_top, t * Q - NCH + c + 1)
                                    sp.dma_start(row[:, c * CH:(c + 1) * CH],
                                                 adj[bass.ts(t, P), c * CH:(c + 1) * CH]).then_inc(s_row, 16)

                            def store(t, u):
                                sp.wait_ge(s_es, t + 1)
                                sp.dma_start(sup_dram[:, bass.ts(t, P)], es[u][:, :]).then_inc(s_eout[u], 16)

                            rows(0)
                            for u in range(2):
                                sp.dma_start(blk[u][:, :], adjT[u]).then_inc(s_blk[u], 16)
                            rows(1)
                            rows(2)

                            def load(t, u, left):
                                if left:
                                    rows(t + 1)
                                sp.wait_ge(s_b, (t - 1) * Q)
                                sp.dma_start(blk[u][:, :], adjT[t]).then_inc(s_blk[u], 16)
                                store(t - 2, u)
                            blocks(sp, load, start=2)
                            for u in range(2):
                                store(NT - 2 + u, u)
                            for u in range(2):
                                sp.wait_ge(s_eout[u], 16 * NT // 2)

                    @block.vector
                    def _(dve):
                        with only_if_signed(dve, False):
                            def row_diagonal(t):
                                dve.wait_ge(s_row, (t + 1) * 16 * NCH)
                                d = row[:, bass.ts(t, P)]
                                nc.vector.tensor_tensor(d, d, offdiag[:, :], ALU.mult).then_inc(s_rz, 1)

                            def row_mask(t, c):
                                if c == 0:
                                    dve.wait_ge(s_rz, t + 1)
                                piece = row[:, c * CH:(c + 1) * CH]
                                nc.vector.tensor_scalar(piece, piece, 0.0, -BIG, ALU.is_equal,
                                                        ALU.mult).then_inc(s_mask, 1)

                            def row_piece(t, u, k):
                                h, c = k // NCH, k % NCH
                                slot = k % SLOTS
                                nc.vector.tensor_tensor_reduce(score[:, slot * CH:(slot + 1) * CH],
                                                               row[:, c * CH:(c + 1) * CH],
                                                               ebc[:, h * N + c * CH:h * N + (c + 1) * CH], 1.0, -3.0e38,
                                                               ALU.add, ALU.max, mx[:, k:k + 1]).then_inc(s_top, 1)
                                if c < NCH - 1:
                                    return
                                dve.wait_ge(s_top, t * Q + k + 1)
                                nc.vector.tensor_reduce(nrem[:, h:h + 1], mx[:, h * NCH:(h + 1) * NCH], AX_X,
                                                        ALU.max).then_inc(s_top1, 1)
                                dve.wait_ge(s_top1, t * HEADS + h + 1)
                                nc.vector.tensor_scalar(nmax[u][:, h:h + 1], nrem[:, h:h + 1], -BIG / 2, -1.0, ALU.max,
                                                        ALU.mult).then_inc(s_nm, 1)

                            def slot_free(t, k):
                                wait_from(dve, s_den, t * Q + k + 1 - SLOTS)

                            def max_parts(t, u):
                                dve.wait_ge(s_nm, (t + 1) * HEADS)
                                wait_from(dve, s_mtr, t)
                                src = nmax[u]
                                n = 0
                                for k in range(PARTS):
                                    s0 = PARTS + k
                                    part = mcol[:, s0:s0 + 2 * (P + KROWS) + 1:P + KROWS]
                                    ins = nc.vector.tensor_copy(part, src[:, :])
                                    if k == PARTS - 1:
                                        ins.then_inc(s_mcol, 1)
                                        break
                                    n += 1
                                    ins.then_inc(s_part, 1)
                                    dve.wait_ge(s_part, t * 4 + n)
                                    n += 1
                                    nc.vector.tensor_tensor(nrem[:, :], src[:, :], part, ALU.subtract).then_inc(s_part, 1)
                                    dve.wait_ge(s_part, t * 4 + n)
                                    src = nrem

                            def clear_diagonal(t, u, r16):
                                dve.wait_ge(s_blk[u], r16)
                                d = blk[u][:, bass.ts(t, P)]
                                nc.vector.tensor_tensor(d, d, offdiag[:, :], ALU.mult).then_inc(s_dz, 1)

                            def weigh(t, u, q):
                                c = q % NCH
                                if q == 0:
                                    dve.wait_ge(s_dz, t + 1)
                                dve.wait_ge(s_r, t * Q + q + 1)
                                wait_from(dve, s_num, t * Q + q + 1 - WGT)
                                nc.vector.tensor_tensor(wgt[q % WGT][:, :], expd[q % EXPD][:, :], blk[u][:, c * CH:(c + 1) * CH],
                                                        ALU.mult).then_inc(s_b, 1)

                            def inverse(t, u):
                                dve.wait_ge(s_den, (t + 1) * Q)
                                wait_from(dve, s_es, t - 1)
                                nc.vector.tensor_reduce(iden[u][:, :], den[u].rearrange("p (h c) -> p h c", c=NCH), AX_X,
                                                        ALU.add).then_inc(s_inv, 1)
                                dve.wait_ge(s_inv, t * 3 + 1)
                                nc.vector.tensor_scalar(iden[u][:, :], iden[u][:, :], 1e-30, float(HEADS),
                                                        ALU.max, ALU.mult).then_inc(s_inv, 1)
                                dve.wait_ge(s_inv, t * 3 + 2)
                                nc.vector.reciprocal(iden[u][:, :], iden[u][:, :]).then_inc(s_inv, 1)

                            def combine(t, u):
                                dve.wait_ge(s_inv, t * 3 + 3)
                                dve.wait_ge(s_num, (t + 1) * Q)
                                if not (isinstance(t, int) and t < 2):
                                    dve.wait_ge(s_eout[u], (t - u) * 8)
                                for h in range(HEADS):
                                    a = ps[:, 4 + u, h * D:(h + 1) * D]
                                    if h == 0:
                                        ins = nc.vector.tensor_scalar(es[u][:, :], a, iden[u][:, 0:1], None, ALU.mult)
                                    else:
                                        ins = nc.vector.scalar_tensor_tensor(out=es[u][:, :], in0=a,
                                                                             scalar=iden[u][:, h:h + 1], in1=es[u][:, :],
                                                                             op0=ALU.mult, op1=ALU.add)
                                    if h < HEADS - 1:
                                        ins.then_inc(s_e, 1)
                                        dve.wait_ge(s_e, t * 2 + 1 + h)
                                    else:
                                        ins.then_inc(s_es, 1)

                            nc.vector.tensor_scalar(nbig[:, :], identb[:, :], -BIG, None, ALU.mult).then_inc(s_id2, 1)
                            nc.vector.memset(mcol[:, :], 0.0).then_inc(s_id2, 1)
                            dve.wait_ge(s_id2, 2)
                            for h in range(HEADS):
                                for k in range(PARTS):
                                    at = h * P + h * KROWS + k
                                    last = nc.vector.memset(mcol[:, at:at + 1], 1.0)
                            last.then_inc(s_init, 1)
                            dve.wait_ge(s_init, 1)
                            for t in range(2):
                                row_diagonal(t)
                                for k in range(Q):
                                    if k < NCH:
                                        row_mask(t, k)
                                        dve.wait_ge(s_mask, t * NCH + k + 1)
                                    slot_free(t, k)
                                    row_piece(t, t, k)
                                max_parts(t, t)
                                if t == 0:
                                    clear_diagonal(0, 0, 16)

                            def body(t, u, left):
                                later = not (isinstance(t, int) and t == 0)
                                for q in range(Q):
                                    pieces = {0: [], Q - 4: [Q - 5, Q - 4]}.get(q, [q - 1 if q < Q - 4 else q])
                                    if left < 2:
                                        pieces = []
                                    if pieces and pieces[0] < NCH:
                                        dve.wait_ge(s_mask, (t + 2) * NCH + pieces[0] + 1)
                                    for k in pieces:
                                        slot_free(t + 2, k)
                                    weigh(t, u, q)
                                    if q == 0:
                                        if left and later:
                                            max_parts(t + 1, 1 - u)
                                        if left == 2:
                                            row_diagonal(t + 2)
                                    if q < NCH and left == 2:
                                        row_mask(t + 2, q)
                                    for k in pieces:
                                        row_piece(t + 2, u, k)
                                    if q == 4 and left:
                                        clear_diagonal(t + 1, 1 - u, (t + 1 - (1 - u)) * 8 + 16)
                                    if q == 5 and later:
                                        combine(t - 1, 1 - u)
                                    if q == 1 and not later:
                                        inverse(0, 0)
                                    if q == 7 and left:
                                        inverse(t + 1, 1 - u)
                                if not left:
                                    combine(t, u)
                            blocks(dve, body)

                    @block.tensor
                    def _(pe):
                        with only_if_signed(pe, False):
                            def exponents(t, u, q):
                                h, c = q // NCH, q % NCH
                                wait_from(pe, s_r, t * Q + q - 1)
                                if q == 0:
                                    pe.wait_ge(s_mrow, t + 1)
                                if h == 0:
                                    pe.wait_ge(s_lt, t * NCH + c + 1)
                                for b in range(CH // 512):
                                    bank = 2 * (q % 2) + b
                                    nc.tensor.matmul(ps[:, bank, :], nbig[:, :],
                                                     maskT[u][:, c * CH + b * 512:c * CH + (b + 1) * 512],
                                                     start=True, stop=False, skip_group_check=True)
                                    for k in range(4):
                                        j = c * TPC + b * 4 + k
                                        last = nc.tensor.matmul(ps[:, bank, k * P:(k + 1) * P], prow[:, j * P:(j + 1) * P],
                                                                mrow[u][:, h * P:(h + 1) * P], start=False, stop=True,
                                                                skip_group_check=True)
                                last.then_inc(s_x, 1)

                            def weighted_sum(t, u, q):
                                h, c = q // NCH, q % NCH
                                pe.wait_ge(s_b, t * Q + q + 1)
                                if q == 0:
                                    wait_from(pe, s_es, t - 1)
                                for k in range(TPC):
                                    j = c * TPC + k
                                    last = nc.tensor.matmul(ps[:, 4 + u, h * D:(h + 1) * D],
                                                            wgt[q % WGT][:, k * P:(k + 1) * P],
                                                            hW[:, (j * HEADS + h) * D:(j * HEADS + h + 1) * D],
                                                            start=(j == 0), stop=(j == NT - 1))
                                last.then_inc(s_num, 1)

                            def turn_max(t):
                                pe.wait_ge(s_mcol, t + 1)
                                wait_from(pe, s_mrow, t)
                                for h in range(HEADS):
                                    last = nc.tensor.transpose(ps[:, 6, :].bitcast(BF16)[:, h * P:(h + 1) * P],
                                                               mcol[:, h * P:(h + 1) * P], identb[:, :])
                                last.then_inc(s_mtr, 1)

                            pe.wait_ge(s_init, 1)
                            turn_max(0)
                            exponents(0, 0, 0)
                            exponents(0, 0, 1)

                            def body(t, u, left):
                                for q in range(Q):
                                    if q + 2 < Q:
                                        exponents(t, u, q + 2)
                                    elif left:
                                        exponents(t + 1, 1 - u, q + 2 - Q)
                                    weighted_sum(t, u, q)
                                    if q == 3 and left:
                                        turn_max(t + 1)
                            blocks(pe, body)

                    @block.scalar
                    def _(act):
                        with only_if_signed(act, False):
                            def row_sum(t, u, k):
                                slot = k % SLOTS
                                act.wait_ge(s_nm, t * HEADS + k // NCH + 1)
                                if k == 0:
                                    wait_from(act, s_inv, (t - 1) * 3)
                                piece = score[:, slot * CH:(slot + 1) * CH]
                                nc.scalar.activation(piece, piece, ACT.Exp, bias=nmax[u][:, k // NCH:k // NCH + 1],
                                                     accum_out=den[u][:, k:k + 1]).then_inc(s_den, 1)

                            def mask_chunk(t, u, c):
                                if c == 0:
                                    act.wait_ge(s_dz, t + 1)
                                    wait_from(act, s_x, (t - 1) * Q)
                                nc.scalar.activation(maskT[u][:, c * CH:(c + 1) * CH], blk[u][:, c * CH:(c + 1) * CH],
                                                     ACT.Relu, scale=-2.0**126, bias=1.0).then_inc(s_lt, 1)

                            def max_row(t, u):
                                act.wait_ge(s_mtr, t + 1)
                                nc.scalar.copy(mrow[u][:, :], ps[:, 6, :].bitcast(BF16)[:, 0:HEADS * P]).then_inc(s_mrow, 1)

                            def body(t, u, left):
                                for q in range(Q):
                                    act.wait_ge(s_x, t * Q + q + 1)
                                    wait_from(act, s_b, t * Q + q + 1 - EXPD)
                                    nc.scalar.activation(expd[q % EXPD][:, :], ps[:, 2 * (q % 2):2 * (q % 2) + 2, :]
                                                         .rearrange("p a c -> p (a c)"), ACT.Exp).then_inc(s_r, 1)
                                    if q < LAG:
                                        if left and not (isinstance(t, int) and t == 0):
                                            row_sum(t + 1, 1 - u, q + Q - LAG)
                                    elif left == 2:
                                        row_sum(t + 2, u, q - LAG)
                                    if q == 4 and left:
                                        max_row(t + 1, 1 - u)
                                    if 6 <= q < 6 + NCH and left:
                                        mask_chunk(t + 1, 1 - u, q - 6)
                            for t in range(2):
                                for k in range(Q):
                                    row_sum(t, t, k)
                                if t == 0:
                                    max_row(0, 0)
                                    for c in range(NCH):
                                        mask_chunk(0, 0, c)
                            blocks(act, body)


            with ExitStack() as cl:
                blk, row, score, wgt = [sb(f"signed_{k}", [P, N], c=cl) for k in ("blk", "row", "score", "wgt")]
                pb, qb = ebc[:, 0:N], ebc[:, N:2 * N]
                dcol = sb("signed_dcol", [P, HEADS * NT], c=cl)
                ones = sb("signed_ones", [P, P], c=cl)
                mdiag = sb("signed_mdiag", [P, P], c=cl)
                nmax, den, iden = [sb(f"signed_{k}", [P, 1], c=cl) for k in ("nmax", "den", "iden")]
                es = sb("signed_es", [P, D], c=cl)
                s_adj, s_sc, s_v0, s_v, s_nm, s_dg, s_mb, s_den, s_w, s_ex, s_wt, s_num, s_es, s_out = [
                    sem(f"signed_{k}") for k in (
                        "adj_in", "scores_in", "constants", "steps", "negmax", "max_diag", "max_row",
                        "den", "exponent", "expd", "weighted", "summed", "es", "es_out")]
                PER = 2 + 13 * HEADS - 1

                def each_tile(eng, body, after=None):
                    with only_if_signed(eng, True):
                        body(0)
                        with eng.Fori(1, NT) as t:
                            body(t)
                        if after is not None:
                            after()

                with nc.Block() as block:
                    @block.sync
                    def _(sp):
                        def load(t):
                            wait_from(sp, s_wt, t * HEADS)
                            sp.dma_start(row[:, :], adj[bass.ts(t, P), :]).then_inc(s_adj, 16)
                            sp.dma_start(blk[:, :], adjT[t]).then_inc(s_adj, 16)
                            for h in range(HEADS):
                                wait_from(sp, s_w, t * HEADS + h)
                                sp.dma_start(pb[:, :], e_dram[h:h + 1, :].broadcast_to([P, N])).then_inc(s_sc, 16)
                                sp.dma_start(qb[:, :], e_dram[HEADS + h:HEADS + h + 1, :]
                                             .broadcast_to([P, N])).then_inc(s_sc, 16)
                        each_tile(sp, load)

                    @block.tensor
                    def _(pe):
                        def body(t):
                            for h in range(HEADS):
                                pe.wait_ge(s_dg, t * HEADS + h + 1)
                                nc.tensor.matmul(ps[:, 0, 0:P], ones[:, :], mdiag[:, :], start=True,
                                                 stop=True).then_inc(s_mb, 1)
                                pe.wait_ge(s_wt, t * HEADS + h + 1)
                                for j in range(NT):
                                    last = nc.tensor.matmul(ps[:, 1, 0:D], wgt[:, j * P:(j + 1) * P],
                                                            hW[:, (j * HEADS + h) * D:(j * HEADS + h + 1) * D],
                                                            start=(j == 0), stop=(j == NT - 1))
                                last.then_inc(s_num, 1)
                        each_tile(pe, body)

                    @block.scalar
                    def _(act):
                        def body(t):
                            for h in range(HEADS):
                                act.wait_ge(s_nm, t * HEADS + h + 1)
                                nc.scalar.activation(wgt[:, :], score[:, :], ACT.Exp, bias=nmax[:, 0:1],
                                                     accum_out=den[:, :]).then_inc(s_den, 1)
                                act.wait_ge(s_w, t * HEADS + h + 1)
                                nc.scalar.activation(score[:, :], score[:, :], ACT.Exp).then_inc(s_ex, 1)
                            act.wait_ge(s_es, t + 1)
                            act.dma_start(sup_dram[:, bass.ts(t, P)], es[:, :]).then_inc(s_out, 16)
                        each_tile(act, body, lambda: act.wait_ge(s_out, NT * 16))

                    @block.vector
                    def _(dve):
                        def body(t):
                            step = [0]

                            def link(ins):
                                step[0] += 1
                                ins.then_inc(s_v, 1)
                                dve.wait_ge(s_v, t * PER + step[0])

                            dve.wait_ge(s_adj, t * 32 + 32)
                            for m in (row, blk):
                                d = m[:, bass.ts(t, P)]
                                link(nc.vector.tensor_tensor(d, d, offdiag[:, :], ALU.mult))
                            s3, b3 = [m[:, :].rearrange("p (j i) -> p j i", i=P) for m in (score, blk)]
                            for h in range(HEADS):
                                dve.wait_ge(s_sc, (t * HEADS + h) * 32 + 32)
                                link(nc.vector.tensor_tensor(pb[:, :], pb[:, :], qb[:, :], ALU.subtract))
                                link(nc.vector.scalar_tensor_tensor(out=score[:, :], in0=row[:, :], scalar=0.0,
                                                                    in1=pb[:, :], op0=ALU.is_gt, op1=ALU.mult))
                                link(nc.vector.tensor_tensor(score[:, :], score[:, :], qb[:, :], ALU.add))
                                link(nc.vector.tensor_scalar(qb[:, :], row[:, :], 0.0, -BIG, ALU.is_equal, ALU.mult))
                                link(nc.vector.tensor_tensor(score[:, :], score[:, :], qb[:, :], ALU.add))
                                link(nc.vector.tensor_reduce(nmax[:, :], score[:, :], AX_X, ALU.max))
                                nc.vector.tensor_scalar(nmax[:, :], nmax[:, :], -BIG / 2, -1.0, ALU.max,
                                                        ALU.mult).then_inc(s_nm, 1)
                                dve.wait_ge(s_nm, t * HEADS + h + 1)
                                nc.vector.tensor_scalar(mdiag[:, :], ident[:, :], nmax[:, 0:1], None,
                                                        ALU.mult).then_inc(s_dg, 1)
                                dve.wait_ge(s_den, t * HEADS + h + 1)
                                dj = dcol[:, h * NT:(h + 1) * NT].rearrange("p (j a) -> p j a", a=1)
                                qj = esc[:, (HEADS + h) * NT:(HEADS + h + 1) * NT].rearrange("p (j a) -> p j a", a=1)
                                link(nc.vector.scalar_tensor_tensor(out=s3, in0=b3, scalar=0.0,
                                                                    in1=dj.broadcast_to([P, NT, P]), op0=ALU.is_gt,
                                                                    op1=ALU.mult))
                                link(nc.vector.tensor_tensor(s3, s3, qj.broadcast_to([P, NT, P]), ALU.add))
                                dve.wait_ge(s_mb, t * HEADS + h + 1)
                                link(nc.vector.tensor_tensor(s3, s3, ps[:, 0, 0:P].rearrange("p (a i) -> p a i", a=1)
                                                             .broadcast_to([P, NT, P]), ALU.add))
                                link(nc.vector.tensor_scalar(qb[:, :], blk[:, :], 0.0, -BIG, ALU.is_equal, ALU.mult))
                                nc.vector.tensor_tensor(score[:, :], score[:, :], qb[:, :], ALU.add).then_inc(s_w, 1)
                                dve.wait_ge(s_ex, t * HEADS + h + 1)
                                nc.vector.tensor_tensor(wgt[:, :], score[:, :], blk[:, :], ALU.mult).then_inc(s_wt, 1)
                                link(nc.vector.tensor_scalar(iden[:, :], den[:, :], 1e-30, float(HEADS), ALU.max,
                                                             ALU.mult))
                                link(nc.vector.reciprocal(iden[:, :], iden[:, :]))
                                dve.wait_ge(s_num, t * HEADS + h + 1)
                                if h == 0:
                                    wait_from(dve, s_out, t * 16)
                                    link(nc.vector.tensor_scalar(es[:, :], ps[:, 1, 0:D], iden[:, 0:1], None, ALU.mult))
                                    continue
                                ins = nc.vector.scalar_tensor_tensor(out=es[:, :], in0=ps[:, 1, 0:D],
                                                                     scalar=iden[:, 0:1], in1=es[:, :],
                                                                     op0=ALU.mult, op1=ALU.add)
                                if h < HEADS - 1:
                                    link(ins)
                                else:
                                    ins.then_inc(s_es, 1)
                            assert step[0] == PER, step[0]

                        nc.vector.memset(ones[:, :], 1.0).then_inc(s_v0, 1)
                        nc.vector.tensor_tensor(dcol[:, :], esc[:, 0:HEADS * NT], esc[:, HEADS * NT:], ALU.subtract)\
                            .then_inc(s_v0, 1)
                        dve.wait_ge(s_v0, 2)
                        each_tile(dve, body)

        with ExitStack() as c2:
            x = sb("x2", [P, N], c=c2)
            with ExitStack() as cg:
                x1, es, edge = [sb(f"node_{k}", [P, N], c=cg) for k in ("x1", "support", "edge")]
                own = gru_buffers(cg, "node")
                wih, whh = sb("node_wih", [P, 384], c=cg), sb("node_whh", [P, 384], c=cg)
                braw, bias = sb("node_braw", [P, 768], c=cg), sb("node_bias", [P, 512], c=cg)
                s_in, s_b, s_n, s_ta, s_fa = [sem(f"node_{k}") for k in ("in", "bias_ready", "norm", "root_in", "root_out")]
                s_grp = [sem(f"node_group_in{q}") for q in range(NT // 4)]
                _, pe_f, act_f, dve_f = gru(es, x1, edge, x, wih, whh, bias, diag, own, "node", arrived=s_grp,
                                         after_dve=lambda dve: norm_dve(dve, Chain(dve, s_n), x, s_ta, s_fa))
                with nc.Block() as block:
                    @block.sync
                    def _(sp):
                        sp.dma_start(wih[:, :], t_in["node_WihT"]).then_inc(s_in, 16)
                        sp.dma_start(whh[:, :], t_in["node_WhhT"]).then_inc(s_in, 16)
                        sp.dma_start(braw[:, :], t_in["node_b"].broadcast_to([P, 768])).then_inc(s_in, 16)
                        for q in range(NT // 4):
                            for to, kept in ((es, sup_dram), (x1, x_dram), (edge, edge_dram)):
                                sp.dma_start(to[:, q * 512:(q + 1) * 512],
                                             kept[:, q * 512:(q + 1) * 512]).then_inc(s_grp[q], 16)

                    @block.tensor
                    def _(pe):
                        pe.wait_ge(s_in, 48)
                        pe_f(pe)

                    @block.scalar
                    def _(act):
                        act_f(act)
                        norm_act(act, x, s_ta, s_fa)

                    @block.vector
                    def _(dve):
                        dve.wait_ge(s_in, 48)
                        gru_bias(dve, Chain(dve, s_b), braw, bias)
                        dve_f(dve)

            next_layer()
            with ExitStack() as cl:
                xhT = sb("xhT", [P, N], c=cl)
                XW = D + 1
                x1s = sb("x_ones", [P, NT * XW], c=cl)
                agg = sb("agg2", [P, N], c=cl)
                bs = sb("bscale", [P, 1], c=cl)
                w2, b2b = sb("w2", [P, D], c=cl), sb("bias2", [P, D], c=cl)
                blk = [sb(f"blk2_{i}", [P, N], c=cl) for i in range(RING)]
                tnh = [sb(f"tnh{i}", [P, CH], c=cl) for i in range(2)]
                expd = [sb(f"expd2_{i}", [P, CH], c=cl) for i in range(2)]
                wgt = [sb(f"wgt2_{i}", [P, CH], c=cl) for i in range(2)]
                rec = sb("rec", [P, 1], c=cl)
                s_blk = [sem(f"cos_blk_in{i}") for i in range(RING)]
                s_w, s_c, s_ta, s_fa, s_xh, s_tr, s_ev = [sem(f"cos_{k}") for k in (
                    "w_in", "chain", "root_in", "root_out", "xhat", "tr", "ev")]
                with nc.Block() as block:
                    @block.sync
                    def _(sp):
                        sp.dma_start(w2[:, :], t_in["W2T"]).then_inc(s_w, 16)
                        sp.dma_start(b2b[:, :], t_in["bias2"].broadcast_to([P, D])).then_inc(s_w, 16)
                        for i in range(RING):
                            sp.dma_start(blk[i][:, :], adjT[i]).then_inc(s_blk[i], 16)
                        sp.wait_ge(s_w, 32)

                    @block.vector
                    def _(dve):
                        link = Chain(dve, s_c)
                        for t in range(NT):
                            last = nc.vector.tensor_tensor_reduce(agg[:, t * P:(t + 1) * P], x[:, t * P:(t + 1) * P],
                                                                  x[:, t * P:(t + 1) * P], 1.0, 0.0, ALU.mult, ALU.add,
                                                                  rstd[:, t:t + 1])
                        link(last)
                        inverse_sqrt(dve, link, rstd[:, :], vc(4), vc(5), s_ta, s_fa)
                        for t in range(NT):
                            last = nc.vector.tensor_scalar(agg[:, t * P:(t + 1) * P], x[:, t * P:(t + 1) * P],
                                                           rstd[:, t:t + 1], None, ALU.mult)
                        last.then_inc(s_xh, 1)
                        link(nc.vector.memset(x1s[:, :], 1.0))
                        link(nc.vector.tensor_copy(x1s[:, :].rearrange("p (t c) -> p t c", c=XW)[:, :, 0:D],
                                                   x[:, :].rearrange("p (t c) -> p t c", c=D)))
                        link(nc.vector.tensor_scalar(bs[:, :], bval[:, :], 0.125, None, ALU.mult))

                    @block.tensor
                    def _(pe):
                        pe.wait_ge(s_xh, 1)
                        pe_transposes(pe, agg, s_tr, s_ev)

                    @block.scalar
                    def _(act):
                        root_act(act, s_ta, s_fa)
                        act_evacuates(act, xhT, s_tr, s_ev)

                s_x, s_t, s_r, s_b, s_num, s_d, s_ag = [sem(f"cos_{k}") for k in (
                    "cosine", "tanh", "expd", "weighted", "summed", "recip", "agg")]
                Q = NCH

                def cos_tiles(eng, body):
                    for t in range(RING):
                        body(t, t, False)
                    with eng.Fori(1, NT // RING - 1) as r:
                        for u in range(RING):
                            body(r * RING + u, u, False)
                    for u in range(RING):
                        body(NT - RING + u, u, u == RING - 1)

                with nc.Block() as block:
                    @block.sync
                    def _(sp):
                        def load(t, u, last):
                            if isinstance(t, int) and t < RING:
                                return
                            sp.wait_ge(s_b, (t - RING + 1) * Q)
                            sp.dma_start(blk[u][:, :], adjT[t]).then_inc(s_blk[u], 16)
                        cos_tiles(sp, load)

                    @block.tensor
                    def _(pe):
                        def cosines(t, u, q):
                            wait_from(pe, s_t, t * Q + q - 1)
                            for k in range(TPC):
                                j = q * TPC + k
                                last = nc.tensor.matmul(ps[:, 2 * (q % 2) + k // 4, (k % 4) * P:(k % 4 + 1) * P],
                                                        xhT[:, j * P:(j + 1) * P], xhT[:, bass.ts(t, P)],
                                                        start=True, stop=True)
                            last.then_inc(s_x, 1)

                        def weighted_sum(t, u, q):
                            pe.wait_ge(s_b, t * Q + q + 1)
                            if q == 0:
                                wait_from(pe, s_ag, t - 1)
                            for k in range(TPC):
                                j = q * TPC + k
                                last = nc.tensor.matmul(ps[:, 4 + u % 2, 0:XW], wgt[q % 2][:, k * P:(k + 1) * P],
                                                        x1s[:, j * XW:(j + 1) * XW], start=(j == 0), stop=(j == NT - 1))
                            last.then_inc(s_num, 1)
                        cosines(0, 0, 0)
                        cosines(0, 0, 1)

                        def body(t, u, last):
                            for q in range(Q):
                                if q + 2 < Q:
                                    cosines(t, u, q + 2)
                                elif not last:
                                    cosines(t + 1, (u + 1) % RING, q + 2 - Q)
                                weighted_sum(t, u, q)
                        cos_tiles(pe, body)

                    @block.scalar
                    def _(act):
                        def tanh(t, q):
                            act.wait_ge(s_x, t * Q + q + 1)
                            wait_from(act, s_r, t * Q + q - 1)
                            nc.scalar.activation(tnh[q % 2][:, :], ps[:, 2 * (q % 2):2 * (q % 2) + 2, :]
                                                 .rearrange("p a c -> p (a c)"), ACT.Tanh,
                                                 scale=bs[:, 0:1]).then_inc(s_t, 1)
                        tanh(0, 0)

                        def body(t, u, last):
                            for q in range(Q):
                                if q + 1 < Q:
                                    tanh(t, q + 1)
                                elif not last:
                                    tanh(t + 1, 0)
                                act.wait_ge(s_t, t * Q + q + 1)
                                wait_from(act, s_b, t * Q + q - 1)
                                nc.scalar.activation(expd[q % 2][:, :], tnh[q % 2][:, :], ACT.Exp,
                                                     scale=8.0).then_inc(s_r, 1)
                        cos_tiles(act, body)

                    @block.vector
                    def _(dve):
                        def finish(t, u):
                            dve.wait_ge(s_num, (t + 1) * Q)
                            nc.vector.reciprocal(rec[:, :], ps[:, 4 + u % 2, D:D + 1]).then_inc(s_d, 1)
                            dve.wait_ge(s_d, t + 1)
                            nc.vector.tensor_scalar(agg[:, bass.ts(t, P)], ps[:, 4 + u % 2, 0:D], rec[:, 0:1], None,
                                                    ALU.mult).then_inc(s_ag, 1)

                        def body(t, u, last):
                            for q in range(Q):
                                if q == 0:
                                    dve.wait_ge(s_blk[u], (t - u) * (16 // RING) + 16)
                                dve.wait_ge(s_r, t * Q + q + 1)
                                wait_from(dve, s_num, t * Q + q - 1)
                                nc.vector.tensor_tensor(wgt[q % 2][:, :], expd[q % 2][:, :],
                                                        blk[u][:, q * CH:(q + 1) * CH], ALU.mult).then_inc(s_b, 1)
                                if q == 0 and not (isinstance(t, int) and t == 0):
                                    finish(t - 1, (u - 1) % RING)
                            if last:
                                finish(t, u)
                        cos_tiles(dve, body)

                s_tr, s_ev, s_l, s_y, s_c, s_n, s_ta, s_fa = [sem(f"lin_{k}") for k in (
                    "tr", "ev", "psum", "y", "stats", "norm", "root_in", "root_out")]
                heat_in = [[sem(f"heat{half}_blk_in{i}") for i in range(RING)] for half in range(2)]
                with nc.Block() as block:
                    @block.sync
                    def _(sp):
                        for i in range(RING):
                            sp.dma_start(blk[i][:, :], adjC[i]).then_inc(heat_in[0][i], 16)

                    @block.tensor
                    def _(pe):
                        pe_transposes(pe, agg, s_tr, s_ev)
                        for q in range(NT // 4):
                            pe.wait_ge(s_ev, q + 1)
                            if q >= 2:
                                pe.wait_ge(s_y, 2 * (q - 1))
                            for k in range(4):
                                t = 4 * q + k
                                last = nc.tensor.matmul(ps[:, 2 + q % 2, k * P:(k + 1) * P], xhT[:, t * P:(t + 1) * P],
                                                        w2[:, :], start=True, stop=True)
                            last.then_inc(s_l, 1)

                    @block.scalar
                    def _(act):
                        act_evacuates(act, xhT, s_tr, s_ev)
                        norm_act(act, x, s_ta, s_fa)

                    @block.vector
                    def _(dve):
                        for q in range(NT // 4):
                            dve.wait_ge(s_l, q + 1)
                            y4 = x[:, q * 512:(q + 1) * 512]
                            nc.vector.tensor_tensor(y4, y4, ps[:, 2 + q % 2, :], ALU.add).then_inc(s_y, 1)
                            dve.wait_ge(s_y, 2 * q + 1)
                            nc.vector.tensor_tensor(y4.rearrange("p (k c) -> p k c", c=D),
                                                    y4.rearrange("p (k c) -> p k c", c=D),
                                                    b2b[:, :].rearrange("p (a c) -> p a c", a=1).broadcast_to([P, 4, D]),
                                                    ALU.add).then_inc(s_y, 1)
                            dve.wait_ge(s_y, 2 * q + 2)
                            for k in range(4):
                                t = 4 * q + k
                                last = nc.vector.bn_stats(stats[:, 6 * t:6 * t + 6], x[:, t * P:(t + 1) * P])
                        last.then_inc(s_c, 1)
                        dve.wait_ge(s_c, 1)
                        norm_dve(dve, Chain(dve, s_n), x, s_ta, s_fa)

                spec, ring = xhT, blk
                coef = sb("coef", [P, NT], c=cl)
                teff = sb("teff", [P, 1], c=cl)
                s_c, s_co, s_coef = sem("heat_chain"), sem("heat_exponent"), sem("heat_coef")
                s_sum, s_ev = [[sem(f"heat{half}_{k}") for half in range(2)] for k in ("summed", "read")]
                s_st, s_n, s_ta, s_fa, s_out = [sem(f"heat_{k}") for k in ("stats", "norm", "root_in", "root_out", "stored")]
                s_even, s_odd = sem("heat_even_scaled"), sem("heat_odd_scaled")
                with nc.Block() as block:
                    @block.sync
                    def _(sp):
                        def columns(t, u, r):
                            if isinstance(t, int):
                                return
                            sp.wait_ge(s_sum[0], t - RING + 1)
                            sp.dma_start(ring[u][:, :], adjC[t]).then_inc(heat_in[0][u], 16)
                        tiles(sp, columns, RING)

                        def rows(t, u, r):
                            if isinstance(t, int):
                                sp.wait_ge(s_sum[0], NT - RING + t + 1)
                            else:
                                sp.wait_ge(s_sum[1], t - RING + 1)
                            sp.dma_start(ring[u][:, :], adjT[t]).then_inc(heat_in[1][u], 16)
                        tiles(sp, rows, RING)
                        QT = NT // 4
                        for q in range(4):
                            sp.wait_ge(s_even, q + 1)
                            sp.wait_ge(s_odd, q + 1)
                            sp.dma_start(out_node[:, q * QT:(q + 1) * QT, :],
                                         x[:, q * QT * P:(q + 1) * QT * P].rearrange("p (t c) -> p t c", c=P))\
                                .then_inc(s_out, 16)
                        sp.wait_ge(s_out, 64)

                    @block.tensor
                    def _(pe):
                        for half, operand in enumerate((x, spec)):
                            if half == 1:
                                pe.wait_ge(s_ev[0], NT)

                            def product(t, u, r):
                                pe.wait_ge(heat_in[half][u], r * 16 + 16)
                                wait_from(pe, s_ev[half], t - 1)
                                for j in range(NT):
                                    last = nc.tensor.matmul(ps[:, u % 2, 0:D], ring[u][:, j * P:(j + 1) * P],
                                                            operand[:, j * P:(j + 1) * P], start=(j == 0),
                                                            stop=(j == NT - 1))
                                last.then_inc(s_sum[half], 1)
                            tiles(pe, product, RING)

                    @block.scalar
                    def _(act):
                        act.wait_ge(s_co, 1)
                        nc.scalar.activation(coef[:, :], coef[:, :], ACT.Exp, scale=-1.0).then_inc(s_coef, 1)
                        norm_act(act, x, s_ta, s_fa, s_odd)

                    @block.vector
                    def _(dve):
                        link = Chain(dve, s_c)
                        link(nc.vector.tensor_scalar(teff[:, :], tval[:, :], 1e-8, None, ALU.max))
                        nc.vector.tensor_scalar(coef[:, :], evals[:, :], teff[:, 0:1], None, ALU.mult).then_inc(s_co, 1)
                        dve.wait_ge(s_coef, 1)

                        def scale(t, u, r):
                            dve.wait_ge(s_sum[0], t + 1)
                            nc.vector.tensor_scalar(spec[:, bass.ts(t, P)], ps[:, u % 2, 0:D], coef[:, bass.ds(t, 1)],
                                                    None, ALU.mult).then_inc(s_ev[0], 1)
                        tiles(dve, scale, RING)

                        def residual(t, u, r):
                            dve.wait_ge(s_sum[1], t + 1)
                            xt = x[:, bass.ts(t, P)]
                            nc.vector.tensor_tensor(xt, xt, ps[:, u % 2, 0:D], ALU.add).then_inc(s_ev[1], 1)
                            dve.wait_ge(s_ev[1], t + 1)
                            nc.vector.bn_stats(stats[:, bass.ts(t, 6)], xt).then_inc(s_st, 1)
                        tiles(dve, residual, RING)
                        dve.wait_ge(s_st, NT)
                        norm_dve(dve, Chain(dve, s_n), x, s_ta, s_fa, s_even)


def layouts(inp):
    import numpy as np
    adj = np.ascontiguousarray(inp["adj"])
    blk = adj.reshape(NT, P, NT, P)
    f = np.ascontiguousarray
    return {
        "x": f(inp["x"]),
        "adj": adj,
        "adjT_blk": f(blk.transpose(0, 3, 2, 1)).reshape(NT, P, N),
        "adj_cols": f(blk.transpose(2, 1, 0, 3)).reshape(NT, P, N),
        "diag": f(np.diagonal(adj).reshape(NT, P).T),
        "evals": f(inp["L3_gnn_evals"].reshape(NT, P).T),
        "t": f(inp["L3_gnn_t"].reshape(1, 1)),
        "b2": f(inp["L2_gnn_b"].reshape(1, 1)),
        "W0T": f(inp["L0_gnn_W"].T),
        "b0": f(inp["L0_gnn_b"].reshape(1, D)),
        "gat_W": f(inp["L1_gnn_gat_W"].transpose(1, 0, 2)).reshape(D, HEADS * D),
        "gat_WT": f(inp["L1_gnn_gat_W"].transpose(2, 0, 1)).reshape(D, HEADS * D),
        "gat_a": f(inp["L1_gnn_gat_a"].reshape(HEADS, 2, D).transpose(2, 0, 1)).reshape(D, 2 * HEADS),
        "edge_WihT": f(inp["L1_gnn_edge_Wih"].T),
        "edge_WhhT": f(inp["L1_gnn_edge_Whh"].T),
        "edge_b": f(np.concatenate([inp["L1_gnn_edge_bih"], inp["L1_gnn_edge_bhh"]]).reshape(1, 6 * D)),
        "node_WihT": f(inp["L1_gnn_node_Wih"].T),
        "node_WhhT": f(inp["L1_gnn_node_Whh"].T),
        "node_b": f(np.concatenate([inp["L1_gnn_node_bih"], inp["L1_gnn_node_bhh"]]).reshape(1, 6 * D)),
        "W2T": f(inp["L2_gnn_W"].T),
        "bias2": f(inp["L2_gnn_bias"].reshape(1, D)),
    }


def kernel(**inputs):
    import numpy as _np
    import concourse.bacc as _bacc
    from concourse import mybir as _mybir
    from concourse.bass_utils import run_bass_kernel_spmd as _run

    nc = _bacc.Bacc("TRN2", target_bir_lowering=False, num_devices=1,
                     dynamic_dma_scratch_size=1024)
    arrays, args = {}, {}
    for name, a in layouts({k: _np.asarray(v) for k, v in inputs.items()}).items():
        arrays[f"in_{name}_dram"] = a
        args[name] = nc.dram_tensor(f"in_{name}_dram", a.shape, _mybir.dt.from_np(a.dtype), kind="ExternalInput").ap()
    out = nc.dram_tensor("out_0_dram", (N, D), F32, kind="ExternalOutput").ap()
    build(nc, args, out)
    r = _run(nc, [arrays], core_ids=[0])
    return r.results[0]["out_0_dram"]
```

```python
from contextlib import ExitStack, contextmanager

import concourse.bass as bass
from concourse import mybir

ALU = mybir.AluOpType
ACT = mybir.ActivationFunctionType
F32 = mybir.dt.float32
BF16 = mybir.dt.bfloat16
I32 = mybir.dt.int32
AX_X = mybir.AxisListType.X

P = 128
N = 4096
D = 128
NT = N // P
HEADS = 3
RING = 4
LN_EPS = 1e-5
ALPHA = 0.2
BIG = float(2.0**100)
CH = 1024
TPC = CH // P
NCH = N // CH
PARTS = 3
KROWS = 2 * PARTS


def tiles(eng, body, unroll):
    for u in range(unroll):
        body(u, u, 0)
    with eng.Fori(1, NT // unroll) as r:
        for u in range(unroll):
            body(r * unroll + u, u, r)


def wait_from(eng, sem, value):
    if not isinstance(value, int) or value > 0:
        eng.wait_ge(sem, value)


class Chain:

    def __init__(self, eng, sem):
        self.eng, self.sem, self.n = eng, sem, 0

    def __call__(self, instruction):
        instruction.then_inc(self.sem, 1)
        self.n += 1
        self.eng.wait_ge(self.sem, self.n)


def build(nc, t_in, out):
    with ExitStack() as ctx:
        def sb(name, shape, dt=F32, c=ctx):
            return c.enter_context(nc.sbuf_tensor(name, shape, dt))

        live = []

        def sem(name):
            live.append(nc.alloc_semaphore(name=name))
            return live[-1]

        def next_layer():
            nc.clear_and_free_semaphores(live)
            live.clear()
            nc.all_engine_barrier()

        ps = ctx.enter_context(nc.psum_tensor("banks", [P, 8, 512], F32))

        ident = sb("ident", [P, P])
        identb = sb("identb", [P, P], BF16)
        offdiag = sb("offdiag", [P, P])
        stats = sb("stats", [P, NT * 6])
        moments = sb("moments", [P, NT * 2])
        col = sb("col", [P, 8 * NT])
        rstd = sb("rstd", [P, NT])
        diag = sb("diag", [P, NT])
        evals = sb("evals", [P, NT])
        tval = sb("tval", [P, 1])
        bval = sb("bval", [P, 1])

        x_dram = nc.dram_tensor("x_spill", [P, N], F32).ap()
        edge_dram = nc.dram_tensor("edge_spill", [P, N], F32).ap()
        sup_dram = nc.dram_tensor("support_spill", [P, N], F32).ap()
        e_dram = nc.dram_tensor("e_spill", [3 * HEADS, N], F32).ap()
        x_node = t_in["x"].rearrange("(t p) c -> p t c", p=P)
        out_node = out.rearrange("(t p) c -> p t c", p=P)
        adj, adjT, adjC = t_in["adj"], t_in["adjT_blk"], t_in["adj_cols"]

        def vc(k):
            return col[:, k * NT:(k + 1) * NT]

        def inverse_sqrt(dve, link, v, sq_in, sq_out, to_act, from_act):
            nc.vector.reciprocal(sq_in, v).then_inc(to_act, 1)
            dve.wait_ge(from_act, 1)
            tmp = vc(6)
            link(nc.vector.tensor_tensor(tmp, sq_out, sq_out, ALU.mult))
            link(nc.vector.tensor_tensor(tmp, tmp, v, ALU.mult))
            link(nc.vector.tensor_scalar(tmp, tmp, -0.5, 1.5, ALU.mult, ALU.add))
            link(nc.vector.tensor_tensor(v, tmp, sq_out, ALU.mult))

        def norm_dve(dve, link, y, to_act, from_act, scaled=None):
            for t in range(NT):
                last = nc.vector.bn_aggr(moments[:, 2 * t:2 * t + 2], stats[:, 6 * t:6 * t + 6])
            link(last)
            mean = moments[:, :].rearrange("p (t k) -> p k t", k=2)
            link(nc.vector.tensor_scalar(rstd[:, :], mean[:, 1, :], LN_EPS, None, ALU.add))
            inverse_sqrt(dve, link, rstd[:, :], vc(4), vc(5), to_act, from_act)
            link(nc.vector.tensor_tensor(vc(6), mean[:, 0, :], rstd[:, :], ALU.mult))
            nc.vector.tensor_scalar(vc(7), vc(6), -1.0, None, ALU.mult).then_inc(to_act, 1)
            for t in range(0, NT, 2):
                last = nc.vector.tensor_scalar(y[:, t * P:(t + 1) * P], y[:, t * P:(t + 1) * P],
                                               moments[:, 2 * t:2 * t + 1], rstd[:, t:t + 1],
                                               ALU.subtract, ALU.mult)
                if scaled is not None and t % (NT // 4) == NT // 4 - 2:
                    last.then_inc(scaled, 1)
            if scaled is None:
                link(last)

        def root_act(act, to_act, from_act):
            act.wait_ge(to_act, 1)
            nc.scalar.activation(vc(5), vc(4), ACT.Sqrt).then_inc(from_act, 1)

        def norm_act(act, y, to_act, from_act, scaled=None):
            root_act(act, to_act, from_act)
            act.wait_ge(to_act, 2)
            for t in range(1, NT, 2):
                last = nc.scalar.activation(y[:, t * P:(t + 1) * P], y[:, t * P:(t + 1) * P], ACT.Identity,
                                            scale=rstd[:, t:t + 1], bias=vc(7)[:, t:t + 1])
                if scaled is not None and t % (NT // 4) == NT // 4 - 1:
                    last.then_inc(scaled, 1)

        def pe_transposes(pe, src, s_tr, s_ev, ready=()):
            for q in range(NT // 4):
                for s in ready:
                    pe.wait_ge(s, q + 1)
                if q >= 2:
                    pe.wait_ge(s_ev, q - 1)
                for k in range(4):
                    t = 4 * q + k
                    last = nc.tensor.transpose(ps[:, q % 2, k * P:(k + 1) * P], src[:, t * P:(t + 1) * P],
                                               ident[:, :])
                last.then_inc(s_tr, 1)

        def act_evacuates(act, dst, s_tr, s_ev):
            for q in range(NT // 4):
                act.wait_ge(s_tr, q + 1)
                nc.scalar.copy(dst[:, q * 512:(q + 1) * 512], ps[:, q % 2, :]).then_inc(s_ev, 1)

        UC = 2 * HEADS * PARTS
        c1, ca = ExitStack(), ExitStack()
        hW = sb("hW", [P, NT * HEADS * D], c=c1)
        ebc = sb("ebc", [P, HEADS * N], c=c1)
        row = sb("row", [P, N], c=c1)
        prow = sb("prow", [P, N], BF16, c=c1)
        esc = sb("esc", [P, 2 * HEADS * NT], c=c1)
        flag = sb("flag", [P, 1], I32, c=c1)
        x = sb("x1", [P, N], c=ca)
        ns = sb("ns", [P, N], c=ca)
        with ExitStack() as c01:
            g = ns
            ring = [hW[:, i * N:(i + 1) * N] for i in range(HEADS)] + [ebc[:, 0:N]]
            xT = ebc[:, N:2 * N]
            rowsum = sb("rowsum", [P, NT], c=c01)
            rinv = sb("rinv", [P, NT], c=c01)
            negsum = sb("negsum", [P, NT], c=c01)
            anyneg, ones = sb("anyneg", [P, 1], c=c01), sb("ones", [P, 1], c=c01)
            s_blk = [sem(f"blk0_in{i}") for i in range(RING)]
            with ExitStack() as c0:
                w = sb("w0", [P, D], c=c0)
                b = sb("b0", [P, D], c=c0)
                s_id0, s_id, s_w, s_x = sem("id_memset"), sem("id_ready"), sem("w0_in"), sem("x_in")
                s_row = [sem(f"row_in{i}") for i in range(RING)]
                s_negsum, s_any, s_count = sem("negative_summed"), sem("any_negative"), sem("negative_partitions")
                s_rowused, s_tr, s_xT = sem("row_summed"), sem("xT_psum"), sem("xT_sbuf")
                s_h, s_hev = sem("h_psum"), sem("h_sbuf")
                s_c, s_ta, s_fa = sem("chain0"), sem("root0_in"), sem("root0_out")
                with nc.Block() as block:
                    @block.sync
                    def _(sp):
                        sp.dma_start(w[:, :], t_in["W0T"]).then_inc(s_w, 16)
                        sp.dma_start(b[:, :], t_in["b0"].broadcast_to([P, D])).then_inc(s_w, 16)
                        sp.dma_start(diag[:, :], t_in["diag"]).then_inc(s_w, 16)
                        sp.dma_start(evals[:, :], t_in["evals"]).then_inc(s_w, 16)
                        sp.dma_start(tval[:, :], t_in["t"].broadcast_to([P, 1])).then_inc(s_w, 16)
                        sp.dma_start(bval[:, :], t_in["b2"].broadcast_to([P, 1])).then_inc(s_w, 16)
                        sp.dma_start(x[:, :].rearrange("p (t c) -> p t c", c=P), x_node).then_inc(s_x, 16)

                        def load(t, u, r):
                            wait_from(sp, s_rowused, t - RING + 1)
                            wait_from(sp, s_negsum, t - RING + 1)
                            sp.dma_start(ring[u][:, :], adj[bass.ts(t, P), :]).then_inc(s_row[u], 16)
                        tiles(sp, load, RING)
                        for u in range(RING):
                            sp.wait_ge(s_rowused, NT - RING + u + 1)
                            sp.wait_ge(s_negsum, NT - RING + u + 1)
                            sp.dma_start(ring[u][:, :], adjT[u]).then_inc(s_blk[u], 16)

                    @block.gpsimd
                    def _(pool):
                        nc.gpsimd.memset(ident[:, :], 0.0).then_inc(s_id0, 1)
                        nc.gpsimd.memset(identb[:, :], 0.0).then_inc(s_id0, 1)
                        nc.gpsimd.memset(offdiag[:, :], 1.0).then_inc(s_id0, 1)
                        pool.wait_ge(s_id0, 3)
                        for m, fill in ((ident, 1.0), (identb, 1.0), (offdiag, 0.0)):
                            nc.gpsimd.affine_select(out=m[:, :], in_=m[:, :], compare_op=ALU.not_equal, fill=fill,
                                                    base=0, pattern=[[-1, P]], channel_multiplier=1).then_inc(s_id, 1)

                    @block.tensor
                    def _(pe):
                        pe.wait_ge(s_id, 3)
                        pe.wait_ge(s_x, 16)
                        pe.wait_ge(s_w, 96)
                        for q in range(NT // 4):
                            if q >= 2:
                                pe.wait_ge(s_xT, q - 1)
                            for k in range(4):
                                t = 4 * q + k
                                last = nc.tensor.transpose(ps[:, q % 2, k * P:(k + 1) * P], x[:, t * P:(t + 1) * P],
                                                           ident[:, :])
                            last.then_inc(s_tr, 1)
                        for q in range(NT // 4):
                            pe.wait_ge(s_xT, q + 1)
                            if q >= 2:
                                pe.wait_ge(s_hev, q - 1)
                            for k in range(4):
                                t = 4 * q + k
                                last = nc.tensor.matmul(ps[:, 2 + q % 2, k * P:(k + 1) * P],
                                                        xT[:, t * P:(t + 1) * P], w[:, :], start=True, stop=True)
                            last.then_inc(s_h, 1)
                        pe.wait_ge(s_any, 2)
                        nc.tensor.matmul(ps[0:1, 7, 0:1], anyneg[:, :], ones[:, :], start=True,
                                         stop=True).then_inc(s_count, 1)

                    @block.scalar
                    def _(act):
                        for q in range(NT // 4):
                            act.wait_ge(s_tr, q + 1)
                            nc.scalar.copy(xT[:, q * 512:(q + 1) * 512], ps[:, q % 2, :]).then_inc(s_xT, 1)

                        def negative_sum(t, u, r):
                            act.wait_ge(s_row[u], r * 16 + 16)
                            wait_from(act, s_negsum, t)
                            nc.scalar.activation(prow[:, :], ring[u][:, :], ACT.Relu, scale=-1.0,
                                                 accum_out=negsum[:, bass.ds(t, 1)]).then_inc(s_negsum, 1)
                        tiles(act, negative_sum, RING)
                        root_act(act, s_ta, s_fa)
                        act.wait_ge(s_ta, 2)
                        for t in range(1, NT, 2):
                            nc.scalar.activation(g[:, t * P:(t + 1) * P], g[:, t * P:(t + 1) * P], ACT.Copy,
                                                 scale=rinv[:, t:t + 1])

                    @block.vector
                    def _(dve):
                        dve.wait_ge(s_w, 96)
                        for q in range(NT // 4):
                            dve.wait_ge(s_h, q + 1)
                            nc.vector.tensor_tensor(
                                g[:, q * 512:(q + 1) * 512].rearrange("p (k c) -> p k c", c=D),
                                ps[:, 2 + q % 2, :].rearrange("p (k c) -> p k c", c=D),
                                b[:, :].rearrange("p (a c) -> p a c", a=1).broadcast_to([P, 4, D]),
                                ALU.add).then_inc(s_hev, 1)

                        def row_sum(t, u, r):
                            dve.wait_ge(s_row[u], r * 16 + 16)
                            nc.vector.tensor_reduce(rowsum[:, bass.ds(t, 1)], ring[u][:, :], AX_X,
                                                    ALU.add).then_inc(s_rowused, 1)
                        tiles(dve, row_sum, RING)
                        dve.wait_ge(s_rowused, NT)
                        dve.wait_ge(s_hev, NT // 4)
                        link = Chain(dve, s_c)
                        dve.wait_ge(s_negsum, NT)
                        link(nc.vector.tensor_reduce(anyneg[:, :], negsum[:, :], AX_X, ALU.max))
                        nc.vector.tensor_scalar(anyneg[:, :], anyneg[:, :], 0.0, None, ALU.is_gt).then_inc(s_any, 1)
                        nc.vector.memset(ones[:, :], 1.0).then_inc(s_any, 1)
                        dve.wait_ge(s_count, 1)
                        link(nc.vector.tensor_scalar(flag[0:1, :], ps[0:1, 7, 0:1], 1.0, None, ALU.min))
                        link(nc.vector.tensor_scalar(rinv[:, :], rowsum[:, :], 1.0, None, ALU.add))
                        link(nc.vector.tensor_scalar(vc(0), rinv[:, :], 0.0, None, ALU.is_equal))
                        link(nc.vector.tensor_tensor(rinv[:, :], rinv[:, :], vc(0), ALU.add))
                        inverse_sqrt(dve, link, rinv[:, :], vc(4), vc(5), s_ta, s_fa)
                        link(nc.vector.tensor_scalar(vc(0), vc(0), -1.0, 1.0, ALU.mult, ALU.add))
                        link(nc.vector.tensor_tensor(rinv[:, :], rinv[:, :], vc(0), ALU.mult))
                        nc.vector.tensor_copy(vc(3), rinv[:, :]).then_inc(s_ta, 1)
                        for t in range(0, NT, 2):
                            last = nc.vector.tensor_scalar(g[:, t * P:(t + 1) * P], g[:, t * P:(t + 1) * P],
                                                           rinv[:, t:t + 1], None, ALU.mult)
                        link(last)

            s_agg, s_ev, s_c = sem("agg0_psum"), sem("agg0_read"), sem("chain0b")
            s_c2, s_ta, s_fa = sem("chain0c"), sem("root0b_in"), sem("root0b_out")
            with nc.Block() as block:
                @block.sync
                def _(sp):
                    def load(t, u, r):
                        if isinstance(t, int):
                            return
                        sp.wait_ge(s_agg, t - RING + 1)
                        sp.dma_start(ring[u][:, :], adjT[t]).then_inc(s_blk[u], 16)
                    tiles(sp, load, RING)

                @block.tensor
                def _(pe):
                    def aggregate(t, u, r):
                        pe.wait_ge(s_blk[u], r * 16 + 16)
                        wait_from(pe, s_ev, t - 1)
                        for j in range(NT):
                            last = nc.tensor.matmul(ps[:, u % 2, 0:D], ring[u][:, j * P:(j + 1) * P],
                                                    g[:, j * P:(j + 1) * P], start=(j == 0), stop=(j == NT - 1))
                        last.then_inc(s_agg, 1)
                    tiles(pe, aggregate, RING)

                @block.scalar
                def _(act):
                    norm_act(act, x, s_ta, s_fa)

                @block.vector
                def _(dve):
                    tmp = col[:, 0:P]

                    def residual(t, u, r):
                        dve.wait_ge(s_agg, t + 1)
                        nc.vector.tensor_tensor(tmp, ps[:, u % 2, 0:D], g[:, bass.ts(t, P)],
                                                ALU.add).then_inc(s_ev, 1)
                        dve.wait_ge(s_ev, t + 1)
                        nc.vector.scalar_tensor_tensor(out=x[:, bass.ts(t, P)], in0=tmp, scalar=rinv[:, bass.ds(t, 1)],
                                                       in1=x[:, bass.ts(t, P)], op0=ALU.mult,
                                                       op1=ALU.add).then_inc(s_c, 1)
                        dve.wait_ge(s_c, t + 1)
                        nc.vector.bn_stats(stats[:, bass.ts(t, 6)], x[:, bass.ts(t, P)]).then_inc(s_c2, 1)
                    tiles(dve, residual, RING)
                    dve.wait_ge(s_c2, NT)
                    link = Chain(dve, sem("chain0d"))
                    norm_dve(dve, link, x, s_ta, s_fa)

        next_layer()
        def gru(src, x, base, dst, wih, whh, bias, scale, own, which, after_dve=None, arrived=None):
            srcT, xT, pre, rz, cand, diff = own
            s_tr, s_tev, s_gate, s_pre, s_rz, s_nin, s_n, s_c = [sem(f"gru_{which}_{k}") for k in (
                "transposed", "transposed_sbuf", "gates", "pre", "rz", "cand_in", "cand", "chain")]
            GROUPS, STEPS = NT // 4, 6

            def groups(eng, body):
                body(0, 0, True)
                body(1, 1, True)
                with eng.Fori(1, GROUPS // 2 - 1) as r:
                    body(r * 2, 0, True)
                    body(r * 2 + 1, 1, True)
                body(GROUPS - 2, 0, True)
                body(GROUPS - 1, 1, False)

            def on_pe(pe):
                def transposes(q):
                    if arrived is not None:
                        pe.wait_ge(arrived[q], 48)
                    wait_from(pe, s_tev, q)
                    for k in range(4):
                        c = slice((4 * q + k) * P, (4 * q + k + 1) * P)
                        nc.tensor.transpose(ps[:, 0, k * P:(k + 1) * P], src[:, c], ident[:, :])
                        last = nc.tensor.transpose(ps[:, 1, k * P:(k + 1) * P], x[:, c], ident[:, :])
                    last.then_inc(s_tr, 1)

                def gates(q):
                    pe.wait_ge(s_tev, q + 1)
                    for k in range(4):
                        if k % 2 == 0:
                            wait_from(pe, s_pre, 2 * q - 1 + k // 2)
                        c = slice(k * P, (k + 1) * P)
                        nc.tensor.matmul(ps[:, 2 + k, 0:256], srcT[q % 2][:, c], wih[:, 0:256], start=True, stop=False)
                        nc.tensor.matmul(ps[:, 2 + k, 0:256], xT[q % 2][:, c], whh[:, 0:256], start=False, stop=True)
                        nc.tensor.matmul(ps[:, 2 + k, 256:384], srcT[q % 2][:, c], wih[:, 256:384], start=False,
                                         stop=True, skip_group_check=True)
                        last = nc.tensor.matmul(ps[:, 2 + k, 384:512], xT[q % 2][:, c], whh[:, 256:384], start=False,
                                                stop=True, skip_group_check=True)
                        if k % 2:
                            last.then_inc(s_gate, 1)

                transposes(0)
                for q in range(GROUPS):
                    if q + 1 < GROUPS:
                        transposes(q + 1)
                    gates(q)

            def on_act(act):
                def evacuate(q, u):
                    act.wait_ge(s_tr, q + 1)
                    wait_from(act, s_gate, 2 * q - 2)
                    nc.scalar.copy(srcT[u][:, :], ps[:, 0, :])
                    nc.scalar.copy(xT[u][:, :], ps[:, 1, :]).then_inc(s_tev, 1)

                def body(q, u, more):
                    if more:
                        evacuate(q + 1, 1 - u)
                    act.wait_ge(s_pre, 2 * q + 2)
                    nc.scalar.activation(by_tile(rz[u], 256), by_tile(pre[u], 512)[:, :, 0:256], ACT.Tanh,
                                         scale=0.5).then_inc(s_rz, 1)
                    act.wait_ge(s_nin, q + 1)
                    nc.scalar.activation(cand[:, :], cand[:, :], ACT.Tanh).then_inc(s_n, 1)
                evacuate(0, 0)
                groups(act, body)

            def by_tile(a, width):
                return a[:, :].rearrange("p (k c) -> p k c", c=width)

            def on_dve(dve):
                def add_bias(q, u):
                    for half in range(2):
                        dve.wait_ge(s_gate, 2 * q + half + 1)
                        nc.vector.tensor_tensor(by_tile(pre[u], 512)[:, 2 * half:2 * half + 2, :],
                                                ps[:, 2 + 2 * half:4 + 2 * half, :],
                                                bias[:, :].rearrange("p (a c) -> p a c", a=1).broadcast_to([P, 2, 512]),
                                                ALU.add).then_inc(s_pre, 1)

                def body(q, u, more):
                    pre3, rz3, cand3, diff3 = by_tile(pre[u], 512), by_tile(rz[u], 256), by_tile(cand, P), by_tile(diff, P)
                    dve.wait_ge(s_pre, 2 * q + 2)
                    dve.wait_ge(s_rz, q + 1)
                    step = [0]

                    def link(ins):
                        step[0] += 1
                        ins.then_inc(s_c, 1)
                        dve.wait_ge(s_c, q * STEPS + step[0])
                    link(nc.vector.scalar_tensor_tensor(out=cand3, in0=rz3[:, :, 0:P], scalar=1.0,
                                                        in1=pre3[:, :, 384:512], op0=ALU.add, op1=ALU.mult))
                    nc.vector.scalar_tensor_tensor(out=cand3, in0=cand3, scalar=0.5, in1=pre3[:, :, 256:384],
                                                   op0=ALU.mult, op1=ALU.add).then_inc(s_nin, 1)
                    if more:
                        add_bias(q + 1, 1 - u)
                    dve.wait_ge(s_n, q + 1)
                    x4 = x[:, bass.ts(q, 512)].rearrange("p (k c) -> p k c", c=P)
                    link(nc.vector.tensor_tensor(diff3, x4, cand3, ALU.subtract))
                    link(nc.vector.scalar_tensor_tensor(out=diff3, in0=rz3[:, :, P:256], scalar=1.0, in1=diff3,
                                                        op0=ALU.add, op1=ALU.mult))
                    link(nc.vector.scalar_tensor_tensor(out=diff3, in0=diff3, scalar=0.5, in1=cand3,
                                                        op0=ALU.mult, op1=ALU.add))
                    for k in range(4):
                        t = q * 4 + k
                        last = nc.vector.scalar_tensor_tensor(
                            out=dst[:, bass.ts(t, P)], in0=diff[:, k * P:(k + 1) * P], scalar=scale[:, bass.ds(t, 1)],
                            in1=base[:, bass.ts(t, P)], op0=ALU.mult, op1=ALU.add)
                    link(last)
                    if after_dve is not None:
                        for k in range(4):
                            last = nc.vector.bn_stats(stats[:, bass.ts(q * 4 + k, 6)], dst[:, bass.ts(q * 4 + k, P)])
                        last.then_inc(s_c, 1)
                    else:
                        nc.vector.tensor_copy(col[:, 0:1], diff[:, 0:1]).then_inc(s_c, 1)
                add_bias(0, 0)
                groups(dve, body)
                dve.wait_ge(s_c, STEPS * GROUPS)
                if after_dve is not None:
                    after_dve(dve)

            return s_c, on_pe, on_act, on_dve

        def gru_buffers(c, which):
            pairs = [[sb(f"{which}_{k}{i}", [P, n], c=c) for i in range(2)] for k, n in (
                ("srcT", 512), ("xT", 512), ("pre", 2048), ("rz", 1024))]
            return pairs + [sb(f"{which}_{k}", [P, 512], c=c) for k in ("cand", "diff")]

        def gru_bias(dve, link, braw, bias):
            link(nc.vector.tensor_tensor(bias[:, 0:256], braw[:, 0:256], braw[:, 384:640], ALU.add))
            link(nc.vector.tensor_copy(bias[:, 256:384], braw[:, 256:384]))
            link(nc.vector.tensor_copy(bias[:, 384:512], braw[:, 640:768]))

        with c1:
            with ca:
                usplit = sb("usplit", [P, NT * UC], BF16, c=ca)
                usp3 = usplit[:, :].rearrange("p (t k) -> p t k", k=UC)
                cl = ExitStack()
                ring = [ebc[:, i * N:(i + 1) * N] for i in range(HEADS)] + [sb("ring1_last", [P, N], c=cl)]
                raw = sb("raw", [P, NT * 2 * UC], c=cl)
                pcol = sb("pcol", [P, N], BF16, c=cl)
                p3 = pcol[:, :].rearrange("p (t k) -> p t k", k=P)
                s_blk = [sem(f"blk1_in{i}") for i in range(RING)]

                @contextmanager
                def only_if_signed(eng, signed):
                    found = eng.alloc_register(f"negative_weights_{len(found_in)}")
                    found_in.append(found)
                    eng.load(found, flag[0:1, 0:1])
                    with eng.If_eq(found, int(signed)):
                        yield
                found_in = []

                with ExitStack() as cp:
                    xT = sb("x1T", [P, N], c=cp)
                    gW = sb("gW", [P, HEADS * D], c=cp)
                    gWT = sb("gWT", [P, HEADS * D], c=cp)
                    ga = sb("ga", [P, 2 * HEADS], c=cp)
                    va = sb("va", [P, 2 * HEADS], c=cp)
                    u = sb("u", [P, NT * 2 * HEADS], c=cp)
                    s_in, s_tr, s_ev, s_va, s_vac, s_u, s_hw, s_hwe, s_c = [sem(f"proj_{k}") for k in (
                        "in", "tr", "ev", "va", "vac", "u", "hw", "hwe", "chain")]
                    with nc.Block() as block:
                        @block.sync
                        def _(sp):
                            sp.dma_start(gW[:, :], t_in["gat_W"]).then_inc(s_in, 16)
                            sp.dma_start(gWT[:, :], t_in["gat_WT"]).then_inc(s_in, 16)
                            sp.dma_start(ga[:, :], t_in["gat_a"]).then_inc(s_in, 16)
                            for i in range(RING):
                                sp.dma_start(ring[i][:, :], adjT[i]).then_inc(s_blk[i], 16)
                            x_kept = sem("x1_kept")
                            sp.dma_start(x_dram, x[:, :]).then_inc(x_kept, 16)
                            sp.wait_ge(x_kept, 16)

                        @block.tensor
                        def _(pe):
                            pe.wait_ge(s_in, 48)
                            for h in range(HEADS):
                                last = nc.tensor.matmul(ps[:, 7, 2 * h:2 * h + 2], gWT[:, h * D:(h + 1) * D],
                                                        ga[:, 2 * h:2 * h + 2], start=True, stop=True)
                            last.then_inc(s_va, 1)
                            pe_transposes(pe, x, s_tr, s_ev)
                            pe.wait_ge(s_ev, NT // 4)
                            pe.wait_ge(s_vac, 1)
                            for t in range(NT):
                                last = nc.tensor.matmul(ps[:, 6, t * 6:t * 6 + 6], xT[:, t * P:(t + 1) * P], va[:, :],
                                                        start=True, stop=True)
                            last.then_inc(s_u, 1)
                            for t in range(NT):
                                if t >= 4:
                                    pe.wait_ge(s_hwe, t - 3)
                                nc.tensor.matmul(ps[:, 2 + t % 4, 0:HEADS * D], xT[:, t * P:(t + 1) * P], gW[:, :],
                                                 start=True, stop=True).then_inc(s_hw, 1)

                        @block.scalar
                        def _(act):
                            act_evacuates(act, xT, s_tr, s_ev)
                            for t in range(NT):
                                act.wait_ge(s_hw, t + 1)
                                nc.scalar.copy(hW[:, t * 384:(t + 1) * 384], ps[:, 2 + t % 4, 0:384]).then_inc(s_hwe, 1)

                        @block.vector
                        def _(dve):
                            link = Chain(dve, s_c)
                            dve.wait_ge(s_va, 1)
                            nc.vector.tensor_copy(va[:, :], ps[:, 7, 0:6]).then_inc(s_vac, 1)
                            link(nc.vector.memset(pcol[:, :], 0.0))
                            for h in range(HEADS):
                                last = nc.vector.memset(p3[:, :, KROWS * h + PARTS:KROWS * (h + 1)], 1.0)
                            link(last)
                            link(nc.vector.memset(raw[:, :], 0.0))
                            dve.wait_ge(s_u, 1)
                            link(nc.vector.tensor_copy(u[:, :], ps[:, 6, 0:NT * 6]))
                            u3 = u[:, :].rearrange("p (t k) -> p t k", k=6)
                            for k in range(PARTS):
                                part = usp3[:, :, 6 * k:6 * k + 6]
                                link(nc.vector.tensor_copy(part, u3))
                                if k < PARTS - 1:
                                    link(nc.vector.tensor_tensor(u3, u3, part, ALU.subtract))

                with cl:
                    pos = [sb(f"pos{i}", [P, N], BF16, c=cl) for i in range(2)]
                    neg = [row[:, i * N // 2:(i + 1) * N // 2].bitcast(BF16) for i in range(2)]
                    s_dz, s_pos, s_neg, s_ns, s_pn, s_rd = [sem(f"sums_{k}") for k in (
                        "diag_cleared", "positive", "negative", "ns_psum", "pn_psum", "read")]

                    def either_way(eng, body):
                        for signed in (False, True):
                            with only_if_signed(eng, signed):
                                tiles(eng, lambda t, u, r: body(t, u, r, signed), RING)

                    with nc.Block() as block:
                        @block.sync
                        def _(sp):
                            def load(t, u, r, signed):
                                if isinstance(t, int):
                                    return
                                sp.wait_ge(s_ns, t - RING + 1)
                                sp.wait_ge(s_neg if signed else s_pos, t - RING + 1)
                                sp.dma_start(ring[u][:, :], adjT[t]).then_inc(s_blk[u], 16)
                            either_way(sp, load)

                        @block.vector
                        def _(dve):
                            def masks(t, u, r, signed):
                                dve.wait_ge(s_blk[u], r * 16 + 16)
                                d = ring[u][:, bass.ts(t, P)]
                                nc.vector.tensor_tensor(d, d, offdiag[:, :], ALU.mult).then_inc(s_dz, 1)
                                dve.wait_ge(s_dz, t + 1)
                                wait_from(dve, s_pn, t - 1)
                                nc.vector.tensor_scalar(pos[u % 2][:, :], ring[u][:, :], 0.0, None,
                                                        ALU.is_gt).then_inc(s_pos, 1)
                                if signed:
                                    nc.vector.tensor_scalar(neg[u % 2][:, :], ring[u][:, :], 0.0, None,
                                                            ALU.is_lt).then_inc(s_neg, 1)
                            either_way(dve, masks)

                        @block.tensor
                        def _(pe):
                            def sums(t, u, r, signed):
                                pe.wait_ge(s_blk[u], r * 16 + 16)
                                pe.wait_ge(s_dz, t + 1)
                                wait_from(pe, s_rd, t - 1)
                                for j in range(NT):
                                    last = nc.tensor.matmul(ps[:, u % 2, 0:D], ring[u][:, j * P:(j + 1) * P],
                                                            x[:, j * P:(j + 1) * P], start=(j == 0), stop=(j == NT - 1))
                                last.then_inc(s_ns, 1)
                                sides = ((pos[u % 2], s_pos), (neg[u % 2], s_neg))[:2 if signed else 1]
                                for m, (mask, ready) in enumerate(sides):
                                    pe.wait_ge(ready, t + 1)
                                    for j in range(NT):
                                        last = nc.tensor.matmul(ps[:, 2 + u % 2, m * UC:(m + 1) * UC],
                                                                mask[:, j * P:(j + 1) * P],
                                                                usplit[:, j * UC:(j + 1) * UC],
                                                                start=(j == 0), stop=(j == NT - 1))
                                last.then_inc(s_pn, 1)
                            either_way(pe, sums)

                        @block.scalar
                        def _(act):
                            def keep(t, u, r, signed):
                                act.wait_ge(s_ns, t + 1)
                                nc.scalar.copy(ns[:, bass.ts(t, P)], ps[:, u % 2, 0:D])
                                act.wait_ge(s_pn, t + 1)
                                width = (2 if signed else 1) * UC
                                nc.scalar.copy(raw[:, bass.ds(t * 2 * UC, width)],
                                               ps[:, 2 + u % 2, 0:width]).then_inc(s_rd, 1)
                            either_way(act, keep)

                    s_c, s_e, s_ec, s_row, s_wr, s_pt, s_prow = [sem(f"score_{k}") for k in (
                        "chain", "e", "e_rows", "rowT", "written", "pcol_T", "prow")]
                    sm = sb("score_parts", [P, NT * 12], c=cl)
                    e_rows = sb("e_rows", [P, 3 * P], c=cl)
                    rem = sb("rem", [P, HEADS * NT], c=cl)
                    with nc.Block() as block:
                        @block.vector
                        def _(dve):
                            link = Chain(dve, s_c)
                            r4 = raw[:, :].rearrange("p (t m k) -> p t m k", m=2, k=UC)
                            s4 = sm[:, :].rearrange("p (t m k) -> p t m k", m=2, k=6)
                            for m in range(2):
                                link(nc.vector.tensor_tensor(s4[:, :, m, :], r4[:, :, m, 12:18], r4[:, :, m, 6:12], ALU.add))
                                link(nc.vector.tensor_tensor(s4[:, :, m, :], s4[:, :, m, :], r4[:, :, m, 0:6], ALU.add))
                            e4 = esc[:, :].rearrange("p (s h t) -> p s h t", s=2, h=HEADS)
                            for h in range(HEADS):
                                for s in range(2):
                                    link(nc.vector.tensor_tensor(e4[:, s, h, :], s4[:, :, s, 2 * h],
                                                                 s4[:, :, 1 - s, 2 * h + 1], ALU.add))
                            link(nc.vector.tensor_scalar(sm[:, 0:192], esc[:, :], ALPHA, None, ALU.mult))
                            link(nc.vector.tensor_tensor(esc[:, :], esc[:, :], sm[:, 0:192], ALU.max))
                            link(nc.vector.tensor_copy(rem[:, :], esc[:, 0:HEADS * NT]))
                            for k in range(PARTS):
                                for h in range(HEADS):
                                    link(nc.vector.tensor_copy(p3[:, :, KROWS * h + k], rem[:, h * NT:(h + 1) * NT]))
                                    if k < PARTS - 1:
                                        link(nc.vector.tensor_tensor(rem[:, h * NT:(h + 1) * NT],
                                                                     rem[:, h * NT:(h + 1) * NT],
                                                                     p3[:, :, KROWS * h + k], ALU.subtract))
                            nc.vector.tensor_copy(rem[:, 0:1], rem[:, 0:1]).then_inc(s_e, 1)

                        @block.tensor
                        def _(pe):
                            pe.wait_ge(s_e, 1)
                            nc.tensor.transpose(ps[0:HEADS * NT, 6, 0:P], esc[:, 0:HEADS * NT], ident[:, :])
                            nc.tensor.transpose(ps[0:HEADS * NT, 6, P:2 * P], esc[:, HEADS * NT:], ident[:, :])\
                                .then_inc(s_row, 1)
                            for q in range(NT // 4):
                                if q >= 2:
                                    pe.wait_ge(s_prow, q - 1)
                                for k in range(4):
                                    t = 4 * q + k
                                    last = nc.tensor.transpose(
                                        ps[:, q % 2, :].bitcast(BF16)[:, k * P:(k + 1) * P], pcol[:, t * P:(t + 1) * P],
                                        identb[:, :])
                                last.then_inc(s_pt, 1)

                        @block.scalar
                        def _(act):
                            act.wait_ge(s_row, 1)
                            nc.scalar.copy(e_rows[0:HEADS * NT, 0:2 * P], ps[0:HEADS * NT, 6, 0:2 * P]).then_inc(s_ec, 1)
                            nc.scalar.activation(e_rows[0:HEADS * NT, 2 * P:3 * P], ps[0:HEADS * NT, 6, 0:P], ACT.Copy,
                                                 scale=-1.0).then_inc(s_ec, 1)
                            act.wait_ge(s_ec, 2)
                            for s in range(3):
                                act.dma_start(e_dram[s * HEADS:(s + 1) * HEADS, :].rearrange("h (t p) -> (h t) p", p=P),
                                              e_rows[0:HEADS * NT, s * P:(s + 1) * P]).then_inc(s_wr, 16)
                            for q in range(NT // 4):
                                act.wait_ge(s_pt, q + 1)
                                nc.scalar.copy(prow[:, q * 512:(q + 1) * 512],
                                               ps[:, q % 2, :].bitcast(BF16)[:, 0:512]).then_inc(s_prow, 1)
                            act.wait_ge(s_wr, 48)

                with ExitStack() as cg:
                    own = gru_buffers(cg, "edge")
                    wih, whh = sb("edge_wih", [P, 384], c=cg), sb("edge_whh", [P, 384], c=cg)
                    braw, bias = sb("edge_braw", [P, 768], c=cg), sb("edge_bias", [P, 512], c=cg)
                    s_row = [sem(f"gat_row_in{c}") for c in range(NCH)]
                    s_in, s_b, s_dn = sem("edge_in"), sem("edge_bias_ready"), sem("edge_out")
                    s_fin, pe_f, act_f, dve_f = gru(ns, x, x, ns, wih, whh, bias, diag, own, "edge")
                    with nc.Block() as block:
                        @block.sync
                        def _(sp):
                            sp.dma_start(wih[:, :], t_in["edge_WihT"]).then_inc(s_in, 16)
                            sp.dma_start(whh[:, :], t_in["edge_WhhT"]).then_inc(s_in, 16)
                            sp.dma_start(braw[:, :], t_in["edge_b"].broadcast_to([P, 768])).then_inc(s_in, 16)
                            s_ebc = sem("e_rows_in")
                            for h in range(HEADS):
                                sp.dma_start(ebc[:, h * N:(h + 1) * N],
                                             e_dram[2 * HEADS + h:2 * HEADS + h + 1, :]
                                             .broadcast_to([P, N])).then_inc(s_ebc, 16)
                            for c in range(NCH):
                                sp.dma_start(row[:, c * CH:(c + 1) * CH],
                                             adj[0:P, c * CH:(c + 1) * CH]).then_inc(s_row[c], 16)
                            for q in range(NT // 4):
                                sp.wait_ge(s_fin, 6 * (q + 1))
                                sp.dma_start(edge_dram[:, q * 512:(q + 1) * 512],
                                             ns[:, q * 512:(q + 1) * 512]).then_inc(s_dn, 16)
                            sp.wait_ge(s_ebc, 16 * HEADS)
                            sp.wait_ge(s_dn, 16 * NT // 4)

                        @block.tensor
                        def _(pe):
                            pe.wait_ge(s_in, 48)
                            pe_f(pe)

                        @block.scalar
                        def _(act):
                            act_f(act)

                        @block.vector
                        def _(dve):
                            dve.wait_ge(s_in, 48)
                            gru_bias(dve, Chain(dve, s_b), braw, bias)
                            dve_f(dve)

            SLOTS, EXPD, WGT, LAG = 6, 3, 3, 5
            with ExitStack() as cl:
                blk = [sb(f"at{i}", [P, N], c=cl) for i in range(2)]
                score = sb("score", [P, SLOTS * CH], c=cl)
                maskT = [sb(f"maskT{i}", [P, N], BF16, c=cl) for i in range(2)]
                expd = [sb(f"expd{i}", [P, CH], c=cl) for i in range(EXPD)]
                wgt = [sb(f"wgt{i}", [P, CH], c=cl) for i in range(WGT)]
                mcol = sb("mcol", [P, HEADS * P], BF16, c=cl)
                mrow = [sb(f"mrow{i}", [P, HEADS * P], BF16, c=cl) for i in range(2)]
                Q = HEADS * NCH
                es = [col[:, i * D:(i + 1) * D] for i in range(2)]
                den = [stats[:, i * Q:(i + 1) * Q] for i in range(2)]
                mx = stats[:, 2 * Q:3 * Q]
                nmax = [stats[:, 3 * Q + i * HEADS:3 * Q + (i + 1) * HEADS] for i in range(2)]
                iden = [stats[:, 3 * Q + (2 + i) * HEADS:3 * Q + (3 + i) * HEADS] for i in range(2)]
                nbig = moments[:, :].bitcast(BF16)
                nrem = stats[:, 3 * Q + 4 * HEADS:3 * Q + 5 * HEADS]
                s_mask, s_top, s_nm, s_den = [sem(f"gat_{k}") for k in (
                    "mask_steps", "max", "negmax", "den")]
                s_blk = [sem(f"gat_blk_in{i}") for i in range(2)]
                s_part, s_mcol, s_mtr, s_mrow, s_lt, s_x, s_r, s_b, s_num = [sem(f"gat_{k}") for k in (
                    "part_steps", "mcol", "mcol_T", "mrow", "mask", "exponent", "expd", "weighted", "summed")]
                s_e, s_es = sem("gat_es_steps"), sem("gat_es")
                s_eout = [sem(f"gat_es_out{i}") for i in range(2)]
                s_dz, s_rz, s_inv = sem("gat_diag_cleared"), sem("gat_row_diag_cleared"), sem("gat_inverse_steps")
                s_id2, s_init = sem("gat_init"), sem("gat_mcol_init")

                def blocks(eng, body, start=0):
                    for t in range(start, 2):
                        body(t, t, 2)
                    with eng.Fori(1, NT // 2 - 1) as r:
                        body(r * 2, 0, 2)
                        body(r * 2 + 1, 1, 2)
                    body(NT - 2, 0, 1)
                    body(NT - 1, 1, 0)

                with nc.Block() as block:
                    @block.sync
                    def _(sp):
                        with only_if_signed(sp, False):
                            def rows(t):
                                for c in range(NCH):
                                    wait_from(sp, s_top, t * Q - NCH + c + 1)
                                    sp.dma_start(row[:, c * CH:(c + 1) * CH],
                                                 adj[bass.ts(t, P), c * CH:(c + 1) * CH]).then_inc(s_row[c], 16)

                            def store(t, u):
                                sp.wait_ge(s_es, t + 1)
                                sp.dma_start(sup_dram[:, bass.ts(t, P)], es[u][:, :]).then_inc(s_eout[u], 16)

                            sp.dma_start(blk[0][:, :], adjT[0]).then_inc(s_blk[0], 16)
                            rows(1)
                            sp.dma_start(blk[1][:, :], adjT[1]).then_inc(s_blk[1], 16)
                            rows(2)

                            def load(t, u, left):
                                if left:
                                    rows(t + 1)
                                sp.wait_ge(s_b, (t - 1) * Q)
                                sp.dma_start(blk[u][:, :], adjT[t]).then_inc(s_blk[u], 16)
                                store(t - 2, u)
                            blocks(sp, load, start=2)
                            for u in range(2):
                                store(NT - 2 + u, u)
                            for u in range(2):
                                sp.wait_ge(s_eout[u], 16 * NT // 2)

                    @block.vector
                    def _(dve):
                        with only_if_signed(dve, False):
                            def row_diagonal(t, c):
                                dve.wait_ge(s_row[c], (t + 1) * 16)
                                d = row[:, bass.ts(t, P)]
                                nc.vector.tensor_tensor(d, d, offdiag[:, :], ALU.mult).then_inc(s_rz, 1)

                            def row_mask(t, c, crossed):
                                if c == crossed:
                                    dve.wait_ge(s_rz, t + 1)
                                else:
                                    dve.wait_ge(s_row[c], (t + 1) * 16)
                                piece = row[:, c * CH:(c + 1) * CH]
                                nc.vector.tensor_scalar(piece, piece, 0.0, BIG, ALU.is_equal,
                                                        ALU.mult).then_inc(s_mask, 1)

                            def row_piece(t, u, k):
                                h, c = k // NCH, k % NCH
                                slot = k % SLOTS
                                nc.vector.tensor_tensor_reduce(score[:, slot * CH:(slot + 1) * CH],
                                                               row[:, c * CH:(c + 1) * CH],
                                                               ebc[:, h * N + c * CH:h * N + (c + 1) * CH], 1.0, BIG / 2,
                                                               ALU.add, ALU.min, mx[:, k:k + 1]).then_inc(s_top, 1)
                                if c < NCH - 1:
                                    return
                                dve.wait_ge(s_top, t * Q + k + 1)
                                nc.vector.tensor_reduce(nmax[u][:, h:h + 1], mx[:, h * NCH:(h + 1) * NCH], AX_X,
                                                        ALU.min).then_inc(s_nm, 1)

                            def slot_free(t, k):
                                wait_from(dve, s_den, t * Q + k + 1 - SLOTS)

                            def max_step(t, u, n):
                                if n == 0:
                                    dve.wait_ge(s_nm, (t + 1) * HEADS)
                                    wait_from(dve, s_mtr, t)
                                else:
                                    dve.wait_ge(s_part, t * 4 + n)
                                src, k = nmax[u] if n < 2 else nrem, n // 2
                                part = mcol[:, PARTS + k:PARTS + k + 2 * (P + KROWS) + 1:P + KROWS]
                                if n % 2 == 0:
                                    nc.vector.tensor_copy(part, src[:, :]).then_inc(s_part if n < 4 else s_mcol, 1)
                                else:
                                    nc.vector.tensor_tensor(nrem[:, :], src[:, :], part, ALU.subtract).then_inc(s_part, 1)

                            def clear_diagonal(t, u, r16):
                                dve.wait_ge(s_blk[u], r16)
                                d = blk[u][:, bass.ts(t, P)]
                                nc.vector.tensor_tensor(d, d, offdiag[:, :], ALU.mult).then_inc(s_dz, 1)

                            def weigh(t, u, q):
                                c = q % NCH
                                if q == 0:
                                    dve.wait_ge(s_dz, t + 1)
                                dve.wait_ge(s_r, t * Q + q + 1)
                                wait_from(dve, s_num, t * Q + q + 1 - WGT)
                                nc.vector.tensor_tensor(wgt[q % WGT][:, :], expd[q % EXPD][:, :], blk[u][:, c * CH:(c + 1) * CH],
                                                        ALU.mult).then_inc(s_b, 1)

                            def inverse_step(t, u, n):
                                if n == 0:
                                    dve.wait_ge(s_den, (t + 1) * Q)
                                    wait_from(dve, s_es, t - 1)
                                    nc.vector.tensor_reduce(iden[u][:, :], den[u].rearrange("p (h c) -> p h c", c=NCH), AX_X,
                                                            ALU.add).then_inc(s_inv, 1)
                                    return
                                dve.wait_ge(s_inv, t * 3 + n)
                                if n == 1:
                                    nc.vector.tensor_scalar(iden[u][:, :], iden[u][:, :], 1e-30, float(HEADS),
                                                            ALU.max, ALU.mult).then_inc(s_inv, 1)
                                else:
                                    nc.vector.reciprocal(iden[u][:, :], iden[u][:, :]).then_inc(s_inv, 1)

                            def combine_step(t, u, h):
                                a = ps[:, 4 + u, h * D:(h + 1) * D]
                                if h == 0:
                                    dve.wait_ge(s_inv, t * 3 + 3)
                                    dve.wait_ge(s_num, (t + 1) * Q)
                                    if not (isinstance(t, int) and t < 2):
                                        dve.wait_ge(s_eout[u], (t - u) * 8)
                                    ins = nc.vector.tensor_scalar(es[u][:, :], a, iden[u][:, 0:1], None, ALU.mult)
                                else:
                                    dve.wait_ge(s_e, t * 2 + h)
                                    ins = nc.vector.scalar_tensor_tensor(out=es[u][:, :], in0=a, scalar=iden[u][:, h:h + 1],
                                                                         in1=es[u][:, :], op0=ALU.mult, op1=ALU.add)
                                ins.then_inc(s_e if h < HEADS - 1 else s_es, 1)

                            nc.vector.tensor_scalar(nbig[:, :], identb[:, :], -BIG, None, ALU.mult).then_inc(s_id2, 1)
                            nc.vector.memset(mcol[:, :], 0.0).then_inc(s_id2, 1)
                            dve.wait_ge(s_id2, 2)
                            for h in range(HEADS):
                                for k in range(PARTS):
                                    at = h * P + h * KROWS + k
                                    last = nc.vector.memset(mcol[:, at:at + 1], 1.0)
                            last.then_inc(s_init, 1)
                            dve.wait_ge(s_init, 1)
                            for t in range(2):
                                row_diagonal(t, 0)
                                for k in range(Q):
                                    if k < NCH:
                                        row_mask(t, k, 0)
                                        dve.wait_ge(s_mask, t * NCH + k + 1)
                                    slot_free(t, k)
                                    row_piece(t, t, k)
                                for n in range(5):
                                    max_step(t, t, n)
                                if t == 0:
                                    clear_diagonal(0, 0, 16)

                            def body(t, u, left, crossed=None):
                                later = not (isinstance(t, int) and t == 0)
                                for q in range(Q):
                                    pieces = {0: [], Q - 4: [Q - 5, Q - 4]}.get(q, [q - 1 if q < Q - 4 else q])
                                    if left < 2:
                                        pieces = []
                                    if pieces and pieces[0] < NCH:
                                        dve.wait_ge(s_mask, (t + 2) * NCH + pieces[0] + 1)
                                    for k in pieces:
                                        slot_free(t + 2, k)
                                    weigh(t, u, q)
                                    split = left and later
                                    if q == 0 and split:
                                        max_step(t + 1, 1 - u, 0)
                                    if q == crossed:
                                        row_diagonal(t + 2, q)
                                    if q < 2 and split:
                                        max_step(t + 1, 1 - u, 2 * q + 1)
                                    if q < NCH and left == 2:
                                        row_mask(t + 2, q, crossed)
                                    if q < 2 and split:
                                        max_step(t + 1, 1 - u, 2 * q + 2)
                                    for k in pieces:
                                        row_piece(t + 2, u, k)
                                    if q == 4 and left:
                                        clear_diagonal(t + 1, 1 - u, (t + 1 - (1 - u)) * 8 + 16)
                                    if 4 <= q < 4 + HEADS and later:
                                        combine_step(t - 1, 1 - u, q - 4)
                                    if 1 <= q < 4 and not later:
                                        inverse_step(0, 0, q - 1)
                                    if 7 <= q < 10 and left:
                                        inverse_step(t + 1, 1 - u, q - 7)
                                if not left:
                                    for h in range(HEADS):
                                        combine_step(t, u, h)
                            for t in range(4):
                                body(t, t % 2, 2, 0)
                            for c in range(NCH):
                                with dve.Fori(max(2, c * TPC // 2 - 1), (c + 1) * TPC // 2 - 1) as r:
                                    body(r * 2, 0, 2, c)
                                    body(r * 2 + 1, 1, 2, c)
                            body(NT - 2, 0, 1)
                            body(NT - 1, 1, 0)

                    @block.tensor
                    def _(pe):
                        with only_if_signed(pe, False):
                            def exponents(t, u, q):
                                h, c = q // NCH, q % NCH
                                wait_from(pe, s_r, t * Q + q - 1)
                                if q == 0:
                                    pe.wait_ge(s_mrow, t + 1)
                                if h == 0:
                                    pe.wait_ge(s_lt, t * NCH + c + 1)
                                for b in range(CH // 512):
                                    bank = 2 * (q % 2) + b
                                    nc.tensor.matmul(ps[:, bank, :], nbig[:, :],
                                                     maskT[u][:, c * CH + b * 512:c * CH + (b + 1) * 512],
                                                     start=True, stop=False, skip_group_check=True)
                                    for k in range(4):
                                        j = c * TPC + b * 4 + k
                                        last = nc.tensor.matmul(ps[:, bank, k * P:(k + 1) * P], prow[:, j * P:(j + 1) * P],
                                                                mrow[u][:, h * P:(h + 1) * P], start=False, stop=True,
                                                                skip_group_check=True)
                                last.then_inc(s_x, 1)

                            def weighted_sum(t, u, q):
                                h, c = q // NCH, q % NCH
                                pe.wait_ge(s_b, t * Q + q + 1)
                                if q == 0:
                                    wait_from(pe, s_es, t - 1)
                                for k in range(TPC):
                                    j = c * TPC + k
                                    last = nc.tensor.matmul(ps[:, 4 + u, h * D:(h + 1) * D],
                                                            wgt[q % WGT][:, k * P:(k + 1) * P],
                                                            hW[:, (j * HEADS + h) * D:(j * HEADS + h + 1) * D],
                                                            start=(j == 0), stop=(j == NT - 1))
                                last.then_inc(s_num, 1)

                            def turn_max(t):
                                pe.wait_ge(s_mcol, t + 1)
                                wait_from(pe, s_mrow, t)
                                for h in range(HEADS):
                                    last = nc.tensor.transpose(ps[:, 6, :].bitcast(BF16)[:, h * P:(h + 1) * P],
                                                               mcol[:, h * P:(h + 1) * P], identb[:, :])
                                last.then_inc(s_mtr, 1)

                            pe.wait_ge(s_init, 1)
                            turn_max(0)
                            exponents(0, 0, 0)
                            exponents(0, 0, 1)

                            def body(t, u, left):
                                for q in range(Q):
                                    if q + 2 < Q:
                                        exponents(t, u, q + 2)
                                    elif left:
                                        exponents(t + 1, 1 - u, q + 2 - Q)
                                    weighted_sum(t, u, q)
                                    if q == 3 and left:
                                        turn_max(t + 1)
                            blocks(pe, body)

                    @block.scalar
                    def _(act):
                        with only_if_signed(act, False):
                            def row_sum(t, u, k):
                                slot = k % SLOTS
                                act.wait_ge(s_nm, t * HEADS + k // NCH + 1)
                                if k == 0:
                                    wait_from(act, s_inv, (t - 1) * 3)
                                piece = score[:, slot * CH:(slot + 1) * CH]
                                nc.scalar.activation(piece, piece, ACT.Exp, scale=-1.0, bias=nmax[u][:, k // NCH:k // NCH + 1],
                                                     accum_out=den[u][:, k:k + 1]).then_inc(s_den, 1)

                            def mask_chunk(t, u, c):
                                if c == 0:
                                    act.wait_ge(s_dz, t + 1)
                                    wait_from(act, s_x, (t - 1) * Q)
                                nc.scalar.activation(maskT[u][:, c * CH:(c + 1) * CH], blk[u][:, c * CH:(c + 1) * CH],
                                                     ACT.Relu, scale=-2.0**126, bias=1.0).then_inc(s_lt, 1)

                            def max_row(t, u):
                                act.wait_ge(s_mtr, t + 1)
                                nc.scalar.copy(mrow[u][:, :], ps[:, 6, :].bitcast(BF16)[:, 0:HEADS * P]).then_inc(s_mrow, 1)

                            def body(t, u, left):
                                for q in range(Q):
                                    act.wait_ge(s_x, t * Q + q + 1)
                                    wait_from(act, s_b, t * Q + q + 1 - EXPD)
                                    nc.scalar.activation(expd[q % EXPD][:, :], ps[:, 2 * (q % 2):2 * (q % 2) + 2, :]
                                                         .rearrange("p a c -> p (a c)"), ACT.Exp).then_inc(s_r, 1)
                                    if q < LAG:
                                        if left and not (isinstance(t, int) and t == 0):
                                            row_sum(t + 1, 1 - u, q + Q - LAG)
                                    elif left == 2:
                                        row_sum(t + 2, u, q - LAG)
                                    if q == 4 and left:
                                        max_row(t + 1, 1 - u)
                                    if 6 <= q < 6 + NCH and left:
                                        mask_chunk(t + 1, 1 - u, q - 6)
                            for t in range(2):
                                for k in range(Q):
                                    row_sum(t, t, k)
                                if t == 0:
                                    max_row(0, 0)
                                    for c in range(NCH):
                                        mask_chunk(0, 0, c)
                            blocks(act, body)


            with ExitStack() as cl:
                blk, score, wgt = [sb(f"signed_{k}", [P, N], c=cl) for k in ("blk", "score", "wgt")]
                pb, qb = ebc[:, 0:N], ebc[:, N:2 * N]
                dcol = sb("signed_dcol", [P, HEADS * NT], c=cl)
                ones = sb("signed_ones", [P, P], c=cl)
                mdiag = sb("signed_mdiag", [P, P], c=cl)
                nmax, den, iden = [sb(f"signed_{k}", [P, 1], c=cl) for k in ("nmax", "den", "iden")]
                es = sb("signed_es", [P, D], c=cl)
                s_adj, s_sc, s_v0, s_v, s_nm, s_dg, s_mb, s_den, s_w, s_ex, s_wt, s_num, s_es, s_out = [
                    sem(f"signed_{k}") for k in (
                        "adj_in", "scores_in", "constants", "steps", "negmax", "max_diag", "max_row",
                        "den", "exponent", "expd", "weighted", "summed", "es", "es_out")]
                PER = 2 + 13 * HEADS - 1

                def each_tile(eng, body, after=None):
                    with only_if_signed(eng, True):
                        body(0)
                        with eng.Fori(1, NT) as t:
                            body(t)
                        if after is not None:
                            after()

                with nc.Block() as block:
                    @block.sync
                    def _(sp):
                        def load(t):
                            wait_from(sp, s_wt, t * HEADS)
                            sp.dma_start(row[:, :], adj[bass.ts(t, P), :]).then_inc(s_adj, 16)
                            sp.dma_start(blk[:, :], adjT[t]).then_inc(s_adj, 16)
                            for h in range(HEADS):
                                wait_from(sp, s_w, t * HEADS + h)
                                sp.dma_start(pb[:, :], e_dram[h:h + 1, :].broadcast_to([P, N])).then_inc(s_sc, 16)
                                sp.dma_start(qb[:, :], e_dram[HEADS + h:HEADS + h + 1, :]
                                             .broadcast_to([P, N])).then_inc(s_sc, 16)
                        each_tile(sp, load)

                    @block.tensor
                    def _(pe):
                        def body(t):
                            for h in range(HEADS):
                                pe.wait_ge(s_dg, t * HEADS + h + 1)
                                nc.tensor.matmul(ps[:, 0, 0:P], ones[:, :], mdiag[:, :], start=True,
                                                 stop=True).then_inc(s_mb, 1)
                                pe.wait_ge(s_wt, t * HEADS + h + 1)
                                for j in range(NT):
                                    last = nc.tensor.matmul(ps[:, 1, 0:D], wgt[:, j * P:(j + 1) * P],
                                                            hW[:, (j * HEADS + h) * D:(j * HEADS + h + 1) * D],
                                                            start=(j == 0), stop=(j == NT - 1))
                                last.then_inc(s_num, 1)
                        each_tile(pe, body)

                    @block.scalar
                    def _(act):
                        def body(t):
                            for h in range(HEADS):
                                act.wait_ge(s_nm, t * HEADS + h + 1)
                                nc.scalar.activation(wgt[:, :], score[:, :], ACT.Exp, bias=nmax[:, 0:1],
                                                     accum_out=den[:, :]).then_inc(s_den, 1)
                                act.wait_ge(s_w, t * HEADS + h + 1)
                                nc.scalar.activation(score[:, :], score[:, :], ACT.Exp).then_inc(s_ex, 1)
                            act.wait_ge(s_es, t + 1)
                            act.dma_start(sup_dram[:, bass.ts(t, P)], es[:, :]).then_inc(s_out, 16)
                        each_tile(act, body, lambda: act.wait_ge(s_out, NT * 16))

                    @block.vector
                    def _(dve):
                        def body(t):
                            step = [0]

                            def link(ins):
                                step[0] += 1
                                ins.then_inc(s_v, 1)
                                dve.wait_ge(s_v, t * PER + step[0])

                            dve.wait_ge(s_adj, t * 32 + 32)
                            for m in (row, blk):
                                d = m[:, bass.ts(t, P)]
                                link(nc.vector.tensor_tensor(d, d, offdiag[:, :], ALU.mult))
                            s3, b3 = [m[:, :].rearrange("p (j i) -> p j i", i=P) for m in (score, blk)]
                            for h in range(HEADS):
                                dve.wait_ge(s_sc, (t * HEADS + h) * 32 + 32)
                                link(nc.vector.tensor_tensor(pb[:, :], pb[:, :], qb[:, :], ALU.subtract))
                                link(nc.vector.scalar_tensor_tensor(out=score[:, :], in0=row[:, :], scalar=0.0,
                                                                    in1=pb[:, :], op0=ALU.is_gt, op1=ALU.mult))
                                link(nc.vector.tensor_tensor(score[:, :], score[:, :], qb[:, :], ALU.add))
                                link(nc.vector.tensor_scalar(qb[:, :], row[:, :], 0.0, -BIG, ALU.is_equal, ALU.mult))
                                link(nc.vector.tensor_tensor(score[:, :], score[:, :], qb[:, :], ALU.add))
                                link(nc.vector.tensor_reduce(nmax[:, :], score[:, :], AX_X, ALU.max))
                                nc.vector.tensor_scalar(nmax[:, :], nmax[:, :], -BIG / 2, -1.0, ALU.max,
                                                        ALU.mult).then_inc(s_nm, 1)
                                dve.wait_ge(s_nm, t * HEADS + h + 1)
                                nc.vector.tensor_scalar(mdiag[:, :], ident[:, :], nmax[:, 0:1], None,
                                                        ALU.mult).then_inc(s_dg, 1)
                                dve.wait_ge(s_den, t * HEADS + h + 1)
                                dj = dcol[:, h * NT:(h + 1) * NT].rearrange("p (j a) -> p j a", a=1)
                                qj = esc[:, (HEADS + h) * NT:(HEADS + h + 1) * NT].rearrange("p (j a) -> p j a", a=1)
                                link(nc.vector.scalar_tensor_tensor(out=s3, in0=b3, scalar=0.0,
                                                                    in1=dj.broadcast_to([P, NT, P]), op0=ALU.is_gt,
                                                                    op1=ALU.mult))
                                link(nc.vector.tensor_tensor(s3, s3, qj.broadcast_to([P, NT, P]), ALU.add))
                                dve.wait_ge(s_mb, t * HEADS + h + 1)
                                link(nc.vector.tensor_tensor(s3, s3, ps[:, 0, 0:P].rearrange("p (a i) -> p a i", a=1)
                                                             .broadcast_to([P, NT, P]), ALU.add))
                                link(nc.vector.tensor_scalar(qb[:, :], blk[:, :], 0.0, -BIG, ALU.is_equal, ALU.mult))
                                nc.vector.tensor_tensor(score[:, :], score[:, :], qb[:, :], ALU.add).then_inc(s_w, 1)
                                dve.wait_ge(s_ex, t * HEADS + h + 1)
                                nc.vector.tensor_tensor(wgt[:, :], score[:, :], blk[:, :], ALU.mult).then_inc(s_wt, 1)
                                link(nc.vector.tensor_scalar(iden[:, :], den[:, :], 1e-30, float(HEADS), ALU.max,
                                                             ALU.mult))
                                link(nc.vector.reciprocal(iden[:, :], iden[:, :]))
                                dve.wait_ge(s_num, t * HEADS + h + 1)
                                if h == 0:
                                    wait_from(dve, s_out, t * 16)
                                    link(nc.vector.tensor_scalar(es[:, :], ps[:, 1, 0:D], iden[:, 0:1], None, ALU.mult))
                                    continue
                                ins = nc.vector.scalar_tensor_tensor(out=es[:, :], in0=ps[:, 1, 0:D],
                                                                     scalar=iden[:, 0:1], in1=es[:, :],
                                                                     op0=ALU.mult, op1=ALU.add)
                                if h < HEADS - 1:
                                    link(ins)
                                else:
                                    ins.then_inc(s_es, 1)
                            assert step[0] == PER, step[0]

                        nc.vector.memset(ones[:, :], 1.0).then_inc(s_v0, 1)
                        nc.vector.tensor_tensor(dcol[:, :], esc[:, 0:HEADS * NT], esc[:, HEADS * NT:], ALU.subtract)\
                            .then_inc(s_v0, 1)
                        dve.wait_ge(s_v0, 2)
                        each_tile(dve, body)

        with ExitStack() as c2:
            x = sb("x2", [P, N], c=c2)
            with ExitStack() as cg:
                x1, es, edge = [sb(f"node_{k}", [P, N], c=cg) for k in ("x1", "support", "edge")]
                own = gru_buffers(cg, "node")
                wih, whh = sb("node_wih", [P, 384], c=cg), sb("node_whh", [P, 384], c=cg)
                braw, bias = sb("node_braw", [P, 768], c=cg), sb("node_bias", [P, 512], c=cg)
                s_in, s_b, s_n, s_ta, s_fa = [sem(f"node_{k}") for k in ("in", "bias_ready", "norm", "root_in", "root_out")]
                s_grp = [sem(f"node_group_in{q}") for q in range(NT // 4)]
                _, pe_f, act_f, dve_f = gru(es, x1, edge, x, wih, whh, bias, diag, own, "node", arrived=s_grp,
                                         after_dve=lambda dve: norm_dve(dve, Chain(dve, s_n), x, s_ta, s_fa))
                with nc.Block() as block:
                    @block.sync
                    def _(sp):
                        sp.dma_start(wih[:, :], t_in["node_WihT"]).then_inc(s_in, 16)
                        sp.dma_start(whh[:, :], t_in["node_WhhT"]).then_inc(s_in, 16)
                        sp.dma_start(braw[:, :], t_in["node_b"].broadcast_to([P, 768])).then_inc(s_in, 16)
                        for q in range(NT // 4):
                            for to, kept in ((es, sup_dram), (x1, x_dram), (edge, edge_dram)):
                                sp.dma_start(to[:, q * 512:(q + 1) * 512],
                                             kept[:, q * 512:(q + 1) * 512]).then_inc(s_grp[q], 16)

                    @block.tensor
                    def _(pe):
                        pe.wait_ge(s_in, 48)
                        pe_f(pe)

                    @block.scalar
                    def _(act):
                        act_f(act)
                        norm_act(act, x, s_ta, s_fa)

                    @block.vector
                    def _(dve):
                        dve.wait_ge(s_in, 48)
                        gru_bias(dve, Chain(dve, s_b), braw, bias)
                        dve_f(dve)

            next_layer()
            with ExitStack() as cl:
                xhT = sb("xhT", [P, N], c=cl)
                XW = D + 1
                x1s = sb("x_ones", [P, NT * XW], c=cl)
                agg = sb("agg2", [P, N], c=cl)
                bs = sb("bscale", [P, 1], c=cl)
                w2, b2b = sb("w2", [P, D], c=cl), sb("bias2", [P, D], c=cl)
                blk = [sb(f"blk2_{i}", [P, N], c=cl) for i in range(RING)]
                tnh = [sb(f"tnh{i}", [P, CH], c=cl) for i in range(2)]
                expd = [sb(f"expd2_{i}", [P, CH], c=cl) for i in range(2)]
                wgt = [sb(f"wgt2_{i}", [P, CH], c=cl) for i in range(2)]
                rec = sb("rec", [P, 1], c=cl)
                s_blk = [sem(f"cos_blk_in{i}") for i in range(RING)]
                s_w, s_c, s_ta, s_fa, s_xh, s_xo, s_tr, s_ev = [sem(f"cos_{k}") for k in (
                    "w_in", "chain", "root_in", "root_out", "xhat_even", "xhat_odd", "tr", "ev")]
                with nc.Block() as block:
                    @block.sync
                    def _(sp):
                        sp.dma_start(w2[:, :], t_in["W2T"]).then_inc(s_w, 16)
                        sp.dma_start(b2b[:, :], t_in["bias2"].broadcast_to([P, D])).then_inc(s_w, 16)
                        for i in range(RING):
                            sp.dma_start(blk[i][:, :], adjT[i]).then_inc(s_blk[i], 16)
                        sp.wait_ge(s_w, 32)

                    @block.vector
                    def _(dve):
                        link = Chain(dve, s_c)
                        var = moments[:, :].rearrange("p (t k) -> p k t", k=2)[:, 1, :]
                        link(nc.vector.tensor_tensor(vc(3), rstd[:, :], rstd[:, :], ALU.mult))
                        link(nc.vector.scalar_tensor_tensor(out=rstd[:, :], in0=vc(3), scalar=float(D), in1=var,
                                                            op0=ALU.mult, op1=ALU.mult))
                        inverse_sqrt(dve, link, rstd[:, :], vc(4), vc(5), s_ta, s_fa)
                        nc.vector.tensor_copy(vc(3), rstd[:, :]).then_inc(s_ta, 1)
                        for t in range(0, NT, 2):
                            last = nc.vector.tensor_scalar(agg[:, t * P:(t + 1) * P], x[:, t * P:(t + 1) * P],
                                                           rstd[:, t:t + 1], None, ALU.mult)
                            if t % 4 == 2:
                                last.then_inc(s_xh, 1)
                        link(nc.vector.memset(x1s[:, :], 1.0))
                        link(nc.vector.tensor_copy(x1s[:, :].rearrange("p (t c) -> p t c", c=XW)[:, :, 0:D],
                                                   x[:, :].rearrange("p (t c) -> p t c", c=D)))
                        link(nc.vector.tensor_scalar(bs[:, :], bval[:, :], 0.125, None, ALU.mult))

                    @block.tensor
                    def _(pe):
                        pe_transposes(pe, agg, s_tr, s_ev, (s_xh, s_xo))

                    @block.scalar
                    def _(act):
                        root_act(act, s_ta, s_fa)
                        act.wait_ge(s_ta, 2)
                        for t in range(1, NT, 2):
                            last = nc.scalar.activation(agg[:, t * P:(t + 1) * P], x[:, t * P:(t + 1) * P],
                                                        ACT.Copy, scale=rstd[:, t:t + 1])
                            if t % 4 == 3:
                                last.then_inc(s_xo, 1)
                        act_evacuates(act, xhT, s_tr, s_ev)

                s_x, s_t, s_r, s_b, s_num, s_d, s_ag = [sem(f"cos_{k}") for k in (
                    "cosine", "tanh", "expd", "weighted", "summed", "recip", "agg")]
                Q = NCH

                def cos_tiles(eng, body):
                    for t in range(RING):
                        body(t, t, False)
                    with eng.Fori(1, NT // RING - 1) as r:
                        for u in range(RING):
                            body(r * RING + u, u, False)
                    for u in range(RING):
                        body(NT - RING + u, u, u == RING - 1)

                with nc.Block() as block:
                    @block.sync
                    def _(sp):
                        def load(t, u, last):
                            if isinstance(t, int) and t < RING:
                                return
                            sp.wait_ge(s_b, (t - RING + 1) * Q)
                            sp.dma_start(blk[u][:, :], adjT[t]).then_inc(s_blk[u], 16)
                        cos_tiles(sp, load)

                    @block.tensor
                    def _(pe):
                        def cosines(t, u, q):
                            wait_from(pe, s_t, t * Q + q - 1)
                            for k in range(TPC):
                                j = q * TPC + k
                                last = nc.tensor.matmul(ps[:, 2 * (q % 2) + k // 4, (k % 4) * P:(k % 4 + 1) * P],
                                                        xhT[:, j * P:(j + 1) * P], xhT[:, bass.ts(t, P)],
                                                        start=True, stop=True)
                            last.then_inc(s_x, 1)

                        def weighted_sum(t, u, q):
                            pe.wait_ge(s_b, t * Q + q + 1)
                            if q == 0:
                                wait_from(pe, s_ag, t - 1)
                            for k in range(TPC):
                                j = q * TPC + k
                                last = nc.tensor.matmul(ps[:, 4 + u % 2, 0:XW], wgt[q % 2][:, k * P:(k + 1) * P],
                                                        x1s[:, j * XW:(j + 1) * XW], start=(j == 0), stop=(j == NT - 1))
                            last.then_inc(s_num, 1)
                        cosines(0, 0, 0)
                        cosines(0, 0, 1)

                        def body(t, u, last):
                            for q in range(Q):
                                if q + 2 < Q:
                                    cosines(t, u, q + 2)
                                elif not last:
                                    cosines(t + 1, (u + 1) % RING, q + 2 - Q)
                                weighted_sum(t, u, q)
                        cos_tiles(pe, body)

                    @block.scalar
                    def _(act):
                        def tanh(t, q):
                            act.wait_ge(s_x, t * Q + q + 1)
                            wait_from(act, s_r, t * Q + q - 1)
                            nc.scalar.activation(tnh[q % 2][:, :], ps[:, 2 * (q % 2):2 * (q % 2) + 2, :]
                                                 .rearrange("p a c -> p (a c)"), ACT.Tanh,
                                                 scale=bs[:, 0:1]).then_inc(s_t, 1)
                        tanh(0, 0)

                        def body(t, u, last):
                            for q in range(Q):
                                if q + 1 < Q:
                                    tanh(t, q + 1)
                                elif not last:
                                    tanh(t + 1, 0)
                                act.wait_ge(s_t, t * Q + q + 1)
                                wait_from(act, s_b, t * Q + q - 1)
                                nc.scalar.activation(expd[q % 2][:, :], tnh[q % 2][:, :], ACT.Exp,
                                                     scale=8.0).then_inc(s_r, 1)
                        cos_tiles(act, body)

                    @block.vector
                    def _(dve):
                        def finish(t, u):
                            dve.wait_ge(s_num, (t + 1) * Q)
                            nc.vector.reciprocal(rec[:, :], ps[:, 4 + u % 2, D:D + 1]).then_inc(s_d, 1)
                            dve.wait_ge(s_d, t + 1)
                            nc.vector.tensor_scalar(agg[:, bass.ts(t, P)], ps[:, 4 + u % 2, 0:D], rec[:, 0:1], None,
                                                    ALU.mult).then_inc(s_ag, 1)

                        def body(t, u, last):
                            for q in range(Q):
                                if q == 0:
                                    dve.wait_ge(s_blk[u], (t - u) * (16 // RING) + 16)
                                dve.wait_ge(s_r, t * Q + q + 1)
                                wait_from(dve, s_num, t * Q + q - 1)
                                nc.vector.tensor_tensor(wgt[q % 2][:, :], expd[q % 2][:, :],
                                                        blk[u][:, q * CH:(q + 1) * CH], ALU.mult).then_inc(s_b, 1)
                                if q == 0 and not (isinstance(t, int) and t == 0):
                                    finish(t - 1, (u - 1) % RING)
                            if last:
                                finish(t, u)
                        cos_tiles(dve, body)

                s_tr, s_ev, s_l, s_y, s_c, s_n, s_ta, s_fa = [sem(f"lin_{k}") for k in (
                    "tr", "ev", "psum", "y", "stats", "norm", "root_in", "root_out")]
                heat_in = [[sem(f"heat{half}_blk_in{i}") for i in range(RING)] for half in range(2)]
                with nc.Block() as block:
                    @block.sync
                    def _(sp):
                        for i in range(RING):
                            sp.dma_start(blk[i][:, :], adjC[i]).then_inc(heat_in[0][i], 16)

                    @block.tensor
                    def _(pe):
                        pe_transposes(pe, agg, s_tr, s_ev)
                        for q in range(NT // 4):
                            pe.wait_ge(s_ev, q + 1)
                            if q >= 2:
                                pe.wait_ge(s_y, 2 * (q - 1))
                            for k in range(4):
                                t = 4 * q + k
                                last = nc.tensor.matmul(ps[:, 2 + q % 2, k * P:(k + 1) * P], xhT[:, t * P:(t + 1) * P],
                                                        w2[:, :], start=True, stop=True)
                            last.then_inc(s_l, 1)

                    @block.scalar
                    def _(act):
                        act_evacuates(act, xhT, s_tr, s_ev)
                        norm_act(act, x, s_ta, s_fa)

                    @block.vector
                    def _(dve):
                        for q in range(NT // 4):
                            dve.wait_ge(s_l, q + 1)
                            y4 = x[:, q * 512:(q + 1) * 512]
                            nc.vector.tensor_tensor(y4, y4, ps[:, 2 + q % 2, :], ALU.add).then_inc(s_y, 1)
                            dve.wait_ge(s_y, 2 * q + 1)
                            nc.vector.tensor_tensor(y4.rearrange("p (k c) -> p k c", c=D),
                                                    y4.rearrange("p (k c) -> p k c", c=D),
                                                    b2b[:, :].rearrange("p (a c) -> p a c", a=1).broadcast_to([P, 4, D]),
                                                    ALU.add).then_inc(s_y, 1)
                            dve.wait_ge(s_y, 2 * q + 2)
                            for k in range(4):
                                t = 4 * q + k
                                last = nc.vector.bn_stats(stats[:, 6 * t:6 * t + 6], x[:, t * P:(t + 1) * P])
                        last.then_inc(s_c, 1)
                        dve.wait_ge(s_c, 1)
                        norm_dve(dve, Chain(dve, s_n), x, s_ta, s_fa)

                spec, ring = xhT, blk
                coef = sb("coef", [P, NT], c=cl)
                teff = sb("teff", [P, 1], c=cl)
                s_c, s_co, s_coef = sem("heat_chain"), sem("heat_exponent"), sem("heat_coef")
                s_sum, s_ev = [[sem(f"heat{half}_{k}") for half in range(2)] for k in ("summed", "read")]
                s_st, s_n, s_ta, s_fa, s_out = [sem(f"heat_{k}") for k in ("stats", "norm", "root_in", "root_out", "stored")]
                s_even, s_odd = sem("heat_even_scaled"), sem("heat_odd_scaled")
                with nc.Block() as block:
                    @block.sync
                    def _(sp):
                        def columns(t, u, r):
                            if isinstance(t, int):
                                return
                            sp.wait_ge(s_sum[0], t - RING + 1)
                            sp.dma_start(ring[u][:, :], adjC[t]).then_inc(heat_in[0][u], 16)
                        tiles(sp, columns, RING)

                        def rows(t, u, r):
                            if isinstance(t, int):
                                sp.wait_ge(s_sum[0], NT - RING + t + 1)
                            else:
                                sp.wait_ge(s_sum[1], t - RING + 1)
                            sp.dma_start(ring[u][:, :], adjT[t]).then_inc(heat_in[1][u], 16)
                        tiles(sp, rows, RING)
                        QT = NT // 4
                        for q in range(4):
                            sp.wait_ge(s_even, q + 1)
                            sp.wait_ge(s_odd, q + 1)
                            sp.dma_start(out_node[:, q * QT:(q + 1) * QT, :],
                                         x[:, q * QT * P:(q + 1) * QT * P].rearrange("p (t c) -> p t c", c=P))\
                                .then_inc(s_out, 16)
                        sp.wait_ge(s_out, 64)

                    @block.tensor
                    def _(pe):
                        for half, operand in enumerate((x, spec)):
                            if half == 1:
                                pe.wait_ge(s_ev[0], NT)

                            def product(t, u, r):
                                pe.wait_ge(heat_in[half][u], r * 16 + 16)
                                wait_from(pe, s_ev[half], t - 1)
                                for j in range(NT):
                                    last = nc.tensor.matmul(ps[:, u % 2, 0:D], ring[u][:, j * P:(j + 1) * P],
                                                            operand[:, j * P:(j + 1) * P], start=(j == 0),
                                                            stop=(j == NT - 1))
                                last.then_inc(s_sum[half], 1)
                            tiles(pe, product, RING)

                    @block.scalar
                    def _(act):
                        act.wait_ge(s_co, 1)
                        nc.scalar.activation(coef[:, :], coef[:, :], ACT.Exp, scale=-1.0).then_inc(s_coef, 1)
                        norm_act(act, x, s_ta, s_fa, s_odd)

                    @block.vector
                    def _(dve):
                        link = Chain(dve, s_c)
                        link(nc.vector.tensor_scalar(teff[:, :], tval[:, :], 1e-8, None, ALU.max))
                        nc.vector.tensor_scalar(coef[:, :], evals[:, :], teff[:, 0:1], None, ALU.mult).then_inc(s_co, 1)
                        dve.wait_ge(s_coef, 1)

                        def scale(t, u, r):
                            dve.wait_ge(s_sum[0], t + 1)
                            nc.vector.tensor_scalar(spec[:, bass.ts(t, P)], ps[:, u % 2, 0:D], coef[:, bass.ds(t, 1)],
                                                    None, ALU.mult).then_inc(s_ev[0], 1)
                        tiles(dve, scale, RING)

                        def residual(t, u, r):
                            dve.wait_ge(s_sum[1], t + 1)
                            xt = x[:, bass.ts(t, P)]
                            nc.vector.tensor_tensor(xt, xt, ps[:, u % 2, 0:D], ALU.add).then_inc(s_ev[1], 1)
                            dve.wait_ge(s_ev[1], t + 1)
                            nc.vector.bn_stats(stats[:, bass.ts(t, 6)], xt).then_inc(s_st, 1)
                        tiles(dve, residual, RING)
                        dve.wait_ge(s_st, NT)
                        norm_dve(dve, Chain(dve, s_n), x, s_ta, s_fa, s_even)


def layouts(inp):
    import numpy as np
    adj = np.ascontiguousarray(inp["adj"])
    blk = adj.reshape(NT, P, NT, P)
    f = np.ascontiguousarray
    return {
        "x": f(inp["x"]),
        "adj": adj,
        "adjT_blk": f(blk.transpose(0, 3, 2, 1)).reshape(NT, P, N),
        "adj_cols": f(blk.transpose(2, 1, 0, 3)).reshape(NT, P, N),
        "diag": f(np.diagonal(adj).reshape(NT, P).T),
        "evals": f(inp["L3_gnn_evals"].reshape(NT, P).T),
        "t": f(inp["L3_gnn_t"].reshape(1, 1)),
        "b2": f(inp["L2_gnn_b"].reshape(1, 1)),
        "W0T": f(inp["L0_gnn_W"].T),
        "b0": f(inp["L0_gnn_b"].reshape(1, D)),
        "gat_W": f(inp["L1_gnn_gat_W"].transpose(1, 0, 2)).reshape(D, HEADS * D),
        "gat_WT": f(inp["L1_gnn_gat_W"].transpose(2, 0, 1)).reshape(D, HEADS * D),
        "gat_a": f(inp["L1_gnn_gat_a"].reshape(HEADS, 2, D).transpose(2, 0, 1)).reshape(D, 2 * HEADS),
        "edge_WihT": f(inp["L1_gnn_edge_Wih"].T),
        "edge_WhhT": f(inp["L1_gnn_edge_Whh"].T),
        "edge_b": f(np.concatenate([inp["L1_gnn_edge_bih"], inp["L1_gnn_edge_bhh"]]).reshape(1, 6 * D)),
        "node_WihT": f(inp["L1_gnn_node_Wih"].T),
        "node_WhhT": f(inp["L1_gnn_node_Whh"].T),
        "node_b": f(np.concatenate([inp["L1_gnn_node_bih"], inp["L1_gnn_node_bhh"]]).reshape(1, 6 * D)),
        "W2T": f(inp["L2_gnn_W"].T),
        "bias2": f(inp["L2_gnn_bias"].reshape(1, D)),
    }


def kernel(**inputs):
    import numpy as _np
    import concourse.bacc as _bacc
    from concourse import mybir as _mybir
    from concourse.bass_utils import run_bass_kernel_spmd as _run

    nc = _bacc.Bacc("TRN2", target_bir_lowering=False, num_devices=1, dynamic_dma_scratch_size=1024)
    arrays, args = {}, {}
    for name, a in layouts({k: _np.asarray(v) for k, v in inputs.items()}).items():
        arrays[f"in_{name}_dram"] = a
        args[name] = nc.dram_tensor(f"in_{name}_dram", a.shape, _mybir.dt.from_np(a.dtype), kind="ExternalInput").ap()
    out = nc.dram_tensor("out_0_dram", (N, D), F32, kind="ExternalOutput").ap()
    build(nc, args, out)
    r = _run(nc, [arrays], core_ids=[0])
    return r.results[0]["out_0_dram"]
```
